# Optimizing a Trainium2 kernel written in Bass

```python
import numpy as np
import jax
import jax.numpy as jnp

def _softmax(x, axis=-1):
    return jax.nn.softmax(x, axis=axis)

def _gelu(x):
    return jax.nn.gelu(x, approximate=True)

def _silu(x):
    return jax.nn.silu(x)

def _sigmoid(x):
    return jax.nn.sigmoid(x)

def _layernorm(x, axis=-1, eps=1e-05):
    m = jnp.mean(x, axis=axis, keepdims=True)
    v = jnp.var(x, axis=axis, keepdims=True)
    return (x - m) / jnp.sqrt(v + eps)

def _scatter_add(tgt, idx, src, axis=0):
    return tgt.at[idx].add(src)

def _segment_sum(src, seg, n):
    return jax.ops.segment_sum(src, seg, n)
kernel_name = 'mk_seq_postln_d1_jaxref_r4_0c7530'

def setup_inputs(seed: int=0):
    np.random.seed(seed)
    _w = jnp.asarray

    def _L0_attn_setup():
        import jax, jax.numpy as jnp
        import numpy as np
        B, T, D = (1, 1024, 256)
        H, KD, VD = (16, 64, 64)
        MIN_THETA, MAX_THETA = (1.0, 10000.0)

        def _sin_cos(t, d, dtype):
            half = d // 2
            p = jnp.arange(half, dtype=dtype) / (half - 1)
            thetas = MIN_THETA * (MAX_THETA / MIN_THETA) ** p
            pos = jnp.arange(t, dtype=dtype)[:, None] / thetas[None, :]
            return (jnp.sin(pos), jnp.cos(pos))

        def _rope(x, sin, cos):
            d = x.shape[-1] // 2
            x_hi, x_lo = (x[..., :d], x[..., d:])
            y_lo = x_lo * cos + x_hi * sin
            y_hi = x_hi * cos - x_lo * sin
            return jnp.concatenate([y_lo, y_hi], axis=-1)
        key = jax.random.key(seed)
        k0, k1, k2 = jax.random.split(key, 3)
        x = jax.random.normal(k0, (B, T, D), dtype=jnp.float32)
        W_in = jax.random.normal(k1, ((2 * KD + VD) * H, D), dtype=jnp.float32) * 0.02
        b_in = jnp.zeros(((2 * KD + VD) * H,), dtype=jnp.float32)
        W_out = jax.random.normal(k2, (D, H * VD), dtype=jnp.float32) * 0.02
        b_out = jnp.zeros((D,), dtype=jnp.float32)
        return {'x': x, 'W_in': W_in, 'b_in': b_in, 'W_out': W_out, 'b_out': b_out}
    _L0_attn_in = _L0_attn_setup()

    def _L0_ffn_setup():
        import jax, jax.numpy as jnp
        import numpy as np
        N_EXPERTS = 16
        TOP_K = int(N_EXPERTS * 0.2)
        EPS = 1e-12
        key = jax.random.key(seed)
        ks = jax.random.split(key, 6)
        B, T, D, H, E = (4, 256, 256, 512, N_EXPERTS)
        x = jax.random.normal(ks[0], (B, T, D), dtype=jnp.float32)
        gate = jax.random.normal(ks[1], (D, E), dtype=jnp.float32)
        W1 = jax.random.normal(ks[2], (E, D, H), dtype=jnp.float32) * (1.0 / np.sqrt(D))
        b1 = jax.random.normal(ks[3], (E, H), dtype=jnp.float32) * 0.02
        W2 = jax.random.normal(ks[4], (E, H, D), dtype=jnp.float32) * (1.0 / np.sqrt(H))
        b2 = jax.random.normal(ks[5], (E, D), dtype=jnp.float32) * 0.02
        return {'x': x, 'gate': gate, 'W1': W1, 'b1': b1, 'W2': W2, 'b2': b2}
    _L0_ffn_in = _L0_ffn_setup()
    _d = {'L0_attn_x': _L0_attn_in['x'], 'L0_attn_W_in': _L0_attn_in['W_in'], 'L0_attn_b_in': _L0_attn_in['b_in'], 'L0_attn_W_out': _L0_attn_in['W_out'], 'L0_attn_b_out': _L0_attn_in['b_out'], 'L0_ffn_gate': _L0_ffn_in['gate'], 'L0_ffn_W1': _L0_ffn_in['W1'], 'L0_ffn_b1': _L0_ffn_in['b1'], 'L0_ffn_W2': _L0_ffn_in['W2'], 'L0_ffn_b2': _L0_ffn_in['b2']}
    _x0 = _d['L0_attn_x']
    _d['L0_attn_x'] = jax.random.normal(jax.random.fold_in(jax.random.key(seed), 1), (4, 1024, 256), dtype=_x0.dtype)
    del _x0
    return _d

def reference(L0_attn_x, L0_attn_W_in, L0_attn_b_in, L0_attn_W_out, L0_attn_b_out, L0_ffn_gate, L0_ffn_W1, L0_ffn_b1, L0_ffn_W2, L0_ffn_b2):

    def _L0_attn_ref(x, W_in, b_in, W_out, b_out):
        import jax, jax.numpy as jnp
        import numpy as np
        B, T, D = (1, 1024, 256)
        H, KD, VD = (16, 64, 64)
        MIN_THETA, MAX_THETA = (1.0, 10000.0)

        def _sin_cos(t, d, dtype):
            half = d // 2
            p = jnp.arange(half, dtype=dtype) / (half - 1)
            thetas = MIN_THETA * (MAX_THETA / MIN_THETA) ** p
            pos = jnp.arange(t, dtype=dtype)[:, None] / thetas[None, :]
            return (jnp.sin(pos), jnp.cos(pos))

        def _rope(x, sin, cos):
            d = x.shape[-1] // 2
            x_hi, x_lo = (x[..., :d], x[..., d:])
            y_lo = x_lo * cos + x_hi * sin
            y_hi = x_hi * cos - x_lo * sin
            return jnp.concatenate([y_lo, y_hi], axis=-1)
        b, t, _ = x.shape
        proj = x @ W_in.T + b_in
        i1, i2 = (KD * H, 2 * KD * H)
        q = proj[..., :i1].reshape(b, t, H, KD).transpose(0, 2, 1, 3)
        k = proj[..., i1:i2].reshape(b, t, H, KD).transpose(0, 2, 1, 3)
        v = proj[..., i2:].reshape(b, t, H, VD).transpose(0, 2, 1, 3)
        sin, cos = _sin_cos(t, KD, x.dtype)
        q = _rope(q, sin, cos)
        k = _rope(k, sin, cos)
        scale = 1.0 / np.sqrt(KD)
        att = jnp.einsum('bhqd,bhkd->bhqk', q, k) * jnp.asarray(scale, x.dtype)
        mask = jnp.tril(jnp.ones((t, t), dtype=bool))
        att = jnp.where(mask[None, None], att, jnp.asarray(-jnp.inf, x.dtype))
        att = jax.nn.softmax(att, axis=-1)
        y = jnp.einsum('bhqk,bhkd->bhqd', att, v)
        y = y.transpose(0, 2, 1, 3).reshape(b, t, H * VD)
        return y @ W_out.T + b_out

    def _L0_ffn_ref(x, gate, W1, b1, W2, b2):
        import jax, jax.numpy as jnp
        import numpy as np
        N_EXPERTS = 16
        TOP_K = int(N_EXPERTS * 0.2)
        EPS = 1e-12
        raw_gate = jax.nn.softmax(jnp.einsum('btd,de->bte', x, gate), axis=-1)
        _, topk_idx = jax.lax.top_k(raw_gate, TOP_K)
        mask = jax.nn.one_hot(topk_idx, raw_gate.shape[-1], dtype=raw_gate.dtype).sum(axis=2)
        gate_topk = mask * raw_gate
        gate_topk = gate_topk / jnp.maximum(jnp.sum(jnp.abs(gate_topk), axis=-1, keepdims=True), EPS)
        hidden = jax.nn.relu(jnp.einsum('btd,edh->bteh', x, W1) + b1)
        expert_out = jnp.einsum('bteh,ehd->bted', hidden, W2) + b2
        return jnp.einsum('bte,bted->btd', gate_topk, expert_out)
    x = L0_attn_x
    x = _layernorm(x + _L0_attn_ref(x, L0_attn_W_in, L0_attn_b_in, L0_attn_W_out, L0_attn_b_out), axis=-1)
    x = _layernorm(x + _L0_ffn_ref(x, L0_ffn_gate, L0_ffn_W1, L0_ffn_b1, L0_ffn_W2, L0_ffn_b2), axis=-1)
    return x

_drawn_inputs = setup_inputs


def setup_inputs(seed=0):
    import zlib

    import numpy as np

    out = dict(_drawn_inputs(seed))
    spreads = {'L0_attn_b_in': (0.0, 0.1), 'L0_attn_b_out': (0.0, 0.1)}
    factors = {'L0_ffn_b1': 5.124, 'L0_ffn_b2': 3.541}
    for name, (base, spread) in spreads.items():
        noise = np.random.default_rng([zlib.crc32(name.encode()), seed]).standard_normal(out[name].shape)
        drawn = base * np.exp(spread * noise) if base else spread * noise
        out[name] = jnp.asarray(drawn.astype(out[name].dtype))
    for name, factor in factors.items():
        out[name] = (out[name] * factor).astype(out[name].dtype)
    return out
```

```python
from contextlib import ExitStack

import numpy as np

import concourse.bass as bass
from concourse import mybir

ALU = mybir.AluOpType
ACT = mybir.ActivationFunctionType
AX_X = mybir.AxisListType.X
F32 = mybir.dt.float32
F32R = mybir.dt.float32r
BF16 = mybir.dt.bfloat16
I32 = mybir.dt.int32
U32 = mybir.dt.uint32

P = 128
B, T, D = 4, 1024, 256
H, HD = 16, 64
HALF = HD // 2
NTOK = B * T
TILES = NTOK // P
TB = T // P
DK = D // P
PAIRS = H // 2
STEPS = B * PAIRS
CHUNKS = 4
ITERS = STEPS // 2
MASKED = -1.0e30
EPS = 1e-5

S_PER, PF_PER, T_PER, PV_PER, Y_PER = 16, 4, 32, 20, 4
QK_DMAS = 20

ORDER = """S4 S5 U00 S6 U01 V00 S7 R0
S8 U10 V01 N0 S9 U11 V10 U12 V11 Y0 S10 U13 V12 R1 Z0 S11
S12 U20 V13 N1 O0 S13 U21 V20 U22 V21 Y1 S14 U23 V22 R2 Z1 U24 V23 S15 U25 V24 O1
U30 V25 N2 F0 U31 V30 U32 V31 Y2 F1 U33 V32 R3 Z2 U34 V33 H0 U35 V34 O2 U36 V35 U37 V36 H1 V37 N3
F2 F3 X0 X1 Y3 X2 Z3 X3 O3""".split()

T_UNITS = [e for e in ORDER if e[0] in "UYZO"]
U_UNITS = [e for e in ORDER if e[0] == "U"]
TAKES = {}
for _e in T_UNITS:
    TAKES[_e] = "D" if _e[0] in "YO" or (_e[0] == "U" and U_UNITS.index(_e) % 2 == 0) else "A"
D_UNITS = [e for e in T_UNITS if TAKES[e] == "D"]
A_UNITS = [e for e in T_UNITS if TAKES[e] == "A"]


def at(per, n, k):
    return per * (n + 1) + k + 1


def keys_of(q, j):
    return (128, 1) if j == 2 * q + 1 else (256, 0)


def attention_phase(nc, A, dram, shared):
    x, W_in, b_in, W_out, cosT, sinT = A["x"], A["W_in"], A["b_in"], A["W_out"], A["cos"], A["sin"]
    xsplit, wsplit, = dram["xsplit"], dram["wsplit"]
    x1, vo = shared["x1"], shared["vo"]
    with ExitStack() as ctx:
        def sb(name, shape, dt):
            return ctx.enter_context(nc.sbuf_tensor(name, shape, dt))

        def sem(name):
            return ctx.enter_context(nc.semaphore(name))

        w_sb = [sb(f"w_sb{s}", [P, 2, DK, 384], F32R) for s in range(2)]
        xT = sb("xT", [P, 2, DK, T], F32R)
        woT = sb("woT", [P, PAIRS, D], F32)
        rot = sb("rot", [P, 4, 512], F32)
        roped = sb("roped", [P, 2, 512], F32)
        hi = sb("hi", [P, 2, T], F32R)
        lo = sb("lo", [P, 2, T], F32R)
        q1 = [[sb(f"q1_{s}{h}", [P, T], F32R) for h in range(2)] for s in range(2)]
        k1 = [[sb(f"k1_{s}{h}", [P, T], F32R) for h in range(2)] for s in range(2)]
        q2 = [sb(f"q2_{s}", [P, T], F32R) for s in range(2)]
        v_sb = [sb(f"v_sb{s}", [P, TB, P], F32) for s in range(2)]
        prob = [sb("prob0", [P, 2, 2, 768], F32), sb("prob1", [P, 2, 2, 1024], F32)]
        pT = sb("pT", [P, 4, 512], F32)
        cos = sb("cos_sb", [P, T], F32)
        sin = sb("sin_sb", [P, T], F32)
        ych = sb("ych", [P, 2, 256], F32)
        yrow = sb("yrow", [P, 2, 256], F32)
        yT = sb("yT", [P, 2, 256], F32)
        ident = sb("ident", [P, P], F32)
        identb = sb("identb", [P, P], BF16)
        maskb = sb("maskb", [P, P], BF16)
        bias = sb("bias", [P, 3, PAIRS], F32)
        zrow = sb("zrow", [P, D], F32)
        negm = sb("negm", [P, 2, 16], F32)
        den = sb("den", [P, 2, 16], F32)
        rden = sb("rden", [P, 2, 16], F32)

        s_ps = ctx.enter_context(nc.psum_tensor("s_ps", [P, 2, 1024], F32))
        t_ps = ctx.enter_context(nc.psum_tensor("t_ps", [P, 2, 512], F32))
        y_ps = ctx.enter_context(nc.psum_tensor("y_ps", [P, 2, 512], F32))

        names = ("vo_done zeroed consts x_in w_in tab_in bias_in wo_in setup_tr setup_hi setup_lo xsp wo_tr wo_ev "
                 "x_ld s_fill p_fill t_fill pv_done y_taken max_done exp_done rope_read v_taken "
                 "taken_d taken_a added hi_done lo_done rden_done").split()
        m = {k: sem(k) for k in names}
        wsp = [sem(f"wsp{s}") for s in range(2)]
        w_ld = [sem(f"w_ld{s}") for s in range(2)]
        qk_ld = [sem(f"qk_ld{s}") for s in range(2)]

        w_raw_qk = prob[1][:].rearrange("p a b c -> p (a b c)").rearrange("p (n h d) -> p n h d", n=PAIRS, h=2)
        w_raw_v = prob[0][:].rearrange("p a b c -> p (a b c)")[:, 0:PAIRS * D].rearrange("p (n d) -> p n d", n=PAIRS)
        wo_raw = pT[:].rearrange("p a b -> p (a b)").rearrange("p (r c) -> p r c", r=2)

        W_UNITS = [(p, k) for p in range(PAIRS) for k in range(DK)]
        X_UNITS = [(b, k, c) for b in range(B) for k in range(DK) for c in range(2)]
        WO_UNITS = [(r, c) for r in range(2) for c in range(2)]
        NW, NX = len(W_UNITS), len(X_UNITS)

        block = ctx.enter_context(nc.Block())

        @block.sync
        def _(sp):
            for qk in range(2):
                for hh in range(2):
                    o = 32 * (2 * qk + hh)
                    for f in range(2):
                        src = W_in[qk * 1024:(qk + 1) * 1024, :].rearrange("(n h f d) c -> h f d n c",
                                                                           h=2, f=2, d=HALF)[hh, f]
                        sp.dma_start(w_raw_qk[o:o + 32, :, f, :], src).then_inc(m["w_in"], 16)
            sp.dma_start(w_raw_v, W_in[2048:3072, :].rearrange("(n r) c -> r n c", r=P)).then_inc(m["w_in"], 16)
            xv = x.rearrange("b (t p) d -> p (b t) d", p=P)
            for b in range(B):
                sp.dma_start(x1[:, b * TB:(b + 1) * TB, :], xv[:, b * TB:(b + 1) * TB, :]).then_inc(m["x_in"], 16)
            sp.dma_start(wo_raw, W_out.rearrange("(r p) c -> p r c", p=P)).then_inc(m["wo_in"], 16)
            sp.dma_start(cos[:], cosT).then_inc(m["tab_in"], 16)
            sp.dma_start(sin[:], sinT).then_inc(m["tab_in"], 16)
            for half in range(2):
                for qk in range(2):
                    for hh in range(2):
                        src = b_in[qk * 1024:(qk + 1) * 1024].rearrange("(n h f d) -> f h d n", h=2, f=2, d=HALF)[half, hh]
                        o = 32 * (2 * qk + hh)
                        sp.dma_start(bias[o:o + 32, half, :], src,
                                     allow_slow_non_contiguous=True).then_inc(m["bias_in"], 16)
            sp.dma_start(bias[:, 2, :], b_in[2048:3072].rearrange("(n r) -> r n", r=P),
                         allow_slow_non_contiguous=True).then_inc(m["bias_in"], 16)
            for p in range(PAIRS):
                sp.wait_ge(m["setup_hi"], DK * (p + 1))
                sp.wait_ge(m["setup_lo"], DK * (p + 1))
                sp.dma_start(wsplit[p], w_sb[p % 2][:].rearrange("p a k c -> p (a k c)").bitcast(F32)).then_inc(wsp[p % 2], 16)
            for b in range(B):
                sp.wait_ge(m["setup_hi"], NW + 4 * (b + 1))
                sp.wait_ge(m["setup_lo"], NW + 4 * (b + 1))
                sp.dma_start(xsplit[b], xT[:].rearrange("p a k c -> p (a k c)").bitcast(F32)).then_inc(m["xsp"], 16)
            for s in range(2):
                sp.wait_ge(wsp[s], 16 * PAIRS // 2)
            sp.wait_ge(m["xsp"], 16 * B)

            def load_w(s, pair):
                sp.dma_start(w_sb[s][:].rearrange("p a k c -> p (a k c)").bitcast(F32), pair).then_inc(w_ld[s], 16)

            def load_x(batch):
                sp.dma_start(xT[:].rearrange("p a k c -> p (a k c)").bitcast(F32), batch).then_inc(m["x_ld"], 16)

            def stack_qk(n, s):
                sp.wait_ge(m["hi_done"], 2 * n + 2)
                sp.wait_ge(m["lo_done"], 2 * n + 2)
                for h in range(2):
                    for f in range(2):
                        q_in, k_in = 32 * h, 64 + 32 * h
                        pos = 32 * f
                        flip = 64 * h
                        for dst, src, i in ((q1[s][h][pos:pos + 32], hi, q_in),
                                            (q1[s][h][64 + pos:96 + pos], hi, q_in),
                                            (q2[s][64 * h + pos:64 * h + pos + 32], lo, q_in),
                                            (k1[s][h][flip + pos:flip + pos + 32], hi, k_in),
                                            (k1[s][h][64 - flip + pos:96 - flip + pos], lo, k_in)):
                            sp.dma_start(dst.bitcast(F32), src[i:i + 32, f, :].bitcast(F32)).then_inc(qk_ld[s], 16)

            load_x(xsplit[0])
            for s in range(2):
                load_w(s, wsplit[s])
            rows = dram["xs"].shape[0] // P
            sp.wait_ge(m["consts"], 7)
            sp.dma_start(dram["xs"].rearrange("(p r) d -> p r d", p=P),
                         zrow[:].rearrange("p (a d) -> p a d", a=1).broadcast_to([P, rows, D])).then_inc(m["zeroed"], 16)
            for s in range(2):
                sp.wait_ge(m["p_fill"], 4 * s + 4)
                load_w(s, wsplit[2 + s])
                if s == 1:
                    load_x(xsplit[0])
                stack_qk(s, s)
            with nc.sync.Fori(0, ITERS - 1) as it:
                for s in range(2):
                    n = it * 2 + s
                    sp.wait_ge(m["p_fill"], 4 * n + 12)
                    load_w(s, wsplit[bass.ds((n + 4) % PAIRS, 1)].rearrange("a p c -> (a p) c"))
                    if s == 1:
                        load_x(xsplit[bass.ds(((it + 2) % ITERS) // (ITERS // B), 1)].rearrange("a p c -> (a p) c"))
                    sp.wait_ge(m["s_fill"], at(S_PER, n, 15))
                    stack_qk(n + 2, s)
            for s in range(2):
                sp.wait_ge(w_ld[s], 16 * (ITERS + 1))
            sp.wait_ge(m["x_ld"], 16 * (ITERS + 1))
            sp.wait_ge(m["zeroed"], 16)

        @block.gpsimd
        def _(pool):
            pool.memset(ident[:], 0.0).then_inc(m["consts"], 1)
            pool.memset(identb[:], 0.0).then_inc(m["consts"], 1)
            pool.memset(maskb[:], 0.0).then_inc(m["consts"], 1)
            pool.memset(zrow[:], 0.0).then_inc(m["consts"], 1)
            pool.wait_ge(m["consts"], 4)
            for t in (ident, identb):
                pool.affine_select(out=t[:], in_=t[:], compare_op=ALU.not_equal, fill=1.0, base=0,
                                   pattern=[[-1, P]], channel_multiplier=1).then_inc(m["consts"], 1)
            pool.affine_select(out=maskb[:], in_=maskb[:], compare_op=ALU.is_ge, fill=MASKED, base=0,
                               pattern=[[-1, P]], channel_multiplier=1).then_inc(m["consts"], 1)

            def rope_chunk(n, c):
                pool.wait_ge(m["rope_read"], 2 * n + c + 1)
                if not (isinstance(n, int) and n == 0 and c == 0):
                    pool.wait_ge(m["hi_done"], 2 * n + c)
                    pool.wait_ge(m["lo_done"], 2 * n + c)
                nc.gpsimd.tensor_tensor(roped[:, 0, :], rot[:, 0, :], rot[:, 1, :], ALU.add).then_inc(m["added"], 1)
                nc.gpsimd.tensor_tensor(roped[:, 1, :], rot[:, 2, :], rot[:, 3, :], ALU.subtract).then_inc(m["added"], 1)
                pool.wait_ge(m["hi_done"], 2 * n + c + 1)
                pool.wait_ge(m["added"], 4 * n + 2 * c + 2)
                nc.gpsimd.tensor_tensor(lo[:, :, 512 * c:512 * c + 512], roped[:],
                                        hi[:, :, 512 * c:512 * c + 512].bitcast(F32),
                                        ALU.subtract).then_inc(m["lo_done"], 1)

            for n in range(2):
                for c in range(2):
                    rope_chunk(n, c)
            with nc.gpsimd.Fori(0, ITERS - 1) as it:
                for s in range(2):
                    for c in range(2):
                        rope_chunk(it * 2 + s + 2, c)

        @block.tensor
        def _(pe):
            pe.wait_ge(m["consts"], 7)
            unit = 0

            def setup_bank():
                if unit >= 2:
                    pe.wait_ge(m["setup_hi"], unit - 1)
                    pe.wait_ge(m["setup_lo"], unit - 1)
                return t_ps[:, unit % 2, :]

            pe.wait_ge(m["w_in"], 16 * 9)
            for p, k in W_UNITS:
                bank = setup_bank()
                for i in range(3):
                    src = w_raw_qk[:, p, i, k * P:(k + 1) * P] if i < 2 else w_raw_v[:, p, k * P:(k + 1) * P]
                    ins = nc.tensor.transpose(bank[:, i * P:(i + 1) * P], src, ident[:])
                ins.then_inc(m["setup_tr"], 1)
                unit += 1
            for b, k, c in X_UNITS:
                pe.wait_ge(m["x_in"], 64)
                bank = setup_bank()
                for i in range(4):
                    src = x1[:, b * TB + 4 * c + i, k * P:(k + 1) * P]
                    ins = nc.tensor.transpose(bank[:, i * P:(i + 1) * P], src, ident[:])
                ins.then_inc(m["setup_tr"], 1)
                unit += 1
            pe.wait_ge(m["wo_in"], 16)
            for i, (r, c) in enumerate(WO_UNITS):
                if i < 2:
                    pe.wait_ge(m["setup_hi"], unit)
                    pe.wait_ge(m["setup_lo"], unit)
                else:
                    pe.wait_ge(m["wo_ev"], i - 1)
                for j in range(4):
                    src = wo_raw[:, r, (4 * c + j) * P:(4 * c + j + 1) * P]
                    ins = nc.tensor.transpose(t_ps[:, i % 2, j * P:(j + 1) * P], src, ident[:])
                ins.then_inc(m["wo_tr"], 1)
            pe.wait_ge(m["wo_ev"], 4)

            def score_fill(n, s, i):
                h, blk = i % 2, i // 2
                width = (blk + 1) * P
                rows = slice(64 * h, 64 * h + 64)
                for c0 in range(0, width, 512):
                    w = min(512, width - c0)
                    out = s_ps[:, i % 2, c0:c0 + w]
                    last = c0 + w == width
                    qs = slice(blk * P, blk * P + P)
                    nc.tensor.matmul(out, q1[s][h][:, qs], k1[s][h][:, c0:c0 + w], start=True, stop=False,
                                     skip_group_check=True)
                    ins = nc.tensor.matmul(out, q2[s][rows, qs], k1[s][h][rows, c0:c0 + w], start=False,
                                           stop=not last, skip_group_check=True)
                ins = nc.tensor.matmul(s_ps[:, i % 2, width - P:width], identb[:], maskb[:], start=False, stop=True,
                                       skip_group_check=True)
                ins.then_inc(m["s_fill"], 1)

            PRODUCTS = ((0, 0), (0, 1), (1, 0))

            def proj_fill(s, f):
                for half in range(2) if f < 2 else ():
                    out = s_ps[:, f % 2, 512 * half:512 * half + 512]
                    todo = [(a, b, k) for a, b in PRODUCTS for k in range(DK)]
                    for a, b, k in todo:
                        ins = nc.tensor.matmul(out, w_sb[s][:, a, k, half * P:(half + 1) * P],
                                               xT[:, b, k, 512 * f:512 * f + 512],
                                               start=(a, b, k) == todo[0], stop=(a, b, k) == todo[-1])
                if f >= 2:
                    for i in range(4):
                        t = 4 * (f - 2) + i
                        out = s_ps[:, f % 2, i * P:(i + 1) * P]
                        todo = [(a, b, k) for a, b in PRODUCTS for k in range(DK)]
                        for a, b, k in todo:
                            ins = nc.tensor.matmul(out, xT[:, b, k, t * P:(t + 1) * P], w_sb[s][:, a, k, 256:384],
                                                   start=(a, b, k) == todo[0], stop=(a, b, k) == todo[-1])
                ins.then_inc(m["p_fill"], 1)

            def wait_taken(n, unit):
                if TAKES[unit] == "D":
                    pe.wait_ge(m["taken_d"], at(len(D_UNITS), n, D_UNITS.index(unit)))
                else:
                    pe.wait_ge(m["taken_a"], at(len(A_UNITS), n, A_UNITS.index(unit)))

            def step(n, s, projects, follows):
                p = n % PAIRS
                for e in ORDER:
                    kind, q = e[0], int(e[1])
                    if kind == "S":
                        i = int(e[1:])
                        pe.wait_ge(m["exp_done"], at(S_PER, n, i - 2))
                        score_fill(n, s, i)
                    elif kind == "X" and follows:
                        if q == 0:
                            pe.wait_ge(qk_ld[1 - s], 16 * QK_DMAS * ((n + 1) // 2 + 1))
                        if q < 2 and projects:
                            pe.wait_ge(m["v_taken"], at(2, n + 2, q))
                        elif q < 2:
                            pe.wait_ge(m["exp_done"], at(S_PER, n, 14 + q))
                        else:
                            pe.wait_ge(m["exp_done"], at(S_PER, n + 1, q - 2))
                        score_fill(n + 1, 1 - s, q)
                    elif kind == "F" and projects:
                        if q == 0:
                            pe.wait_ge(w_ld[s], 16 * ((n + 2) // 2 + 1))
                            pe.wait_ge(m["x_ld"], 16 * ((n + 2) // 2 + 1))
                        if q < 2:
                            pe.wait_ge(m["exp_done"], at(S_PER, n, 14 + q))
                        else:
                            pe.wait_ge(m["rope_read"], 2 * (n + 2) + q - 1)
                        proj_fill(s, q)
                    if kind in "UYZO":
                        u = T_UNITS.index(e)
                        wait_taken(n if u >= 2 else n - 1, T_UNITS[u - 2])
                        bank = t_ps[:, u % 2, :]
                    if kind == "U":
                        j = int(e[2])
                        w, first = keys_of(q, j)
                        pe.wait_ge(m["exp_done"], at(S_PER, n, 4 * q + 3))
                        for h in range(2):
                            for ii in range(first, 2):
                                o = h * w + (ii - first) * P
                                ins = nc.tensor.transpose(bank[:, o:o + P], prob[q % 2][:, h, ii, j * P:(j + 1) * P],
                                                          ident[:])
                        ins.then_inc(m["t_fill"], 1)
                    if kind == "V":
                        j = int(e[2])
                        w, first = keys_of(q, j)
                        uu = U_UNITS.index(f"U{q}{j}")
                        if j == 0:
                            pe.wait_ge(m["y_taken"], at(Y_PER, n, q - 2))
                            pe.wait_ge(m["v_taken"], at(2, n, 1))
                        wait_taken(n, f"U{q}{j}")
                        for h in range(2):
                            ins = nc.tensor.matmul(y_ps[64 * h:64 * h + 64, q % 2, 256 - w:256],
                                                   v_sb[s][:, j, 64 * h:64 * h + 64],
                                                   pT[:, uu % 4, h * w:(h + 1) * w],
                                                   start=(j == 0), stop=(j == 2 * q + 1), skip_group_check=True)
                        ins.then_inc(m["pv_done"], 1)
                    if kind == "Y":
                        pe.wait_ge(m["y_taken"], at(Y_PER, n, q))
                        for ii in range(2):
                            ins = nc.tensor.transpose(bank[:, ii * P:(ii + 1) * P], ych[:, q % 2, ii * P:(ii + 1) * P],
                                                      ident[:])
                        ins.then_inc(m["t_fill"], 1)
                    if kind == "Z":
                        wait_taken(n, f"Y{q}")
                        for ii in range(2):
                            ins = nc.tensor.transpose(bank[:, ii * P:(ii + 1) * P], yrow[:, q % 2, ii * P:(ii + 1) * P],
                                                      ident[:])
                        ins.then_inc(m["t_fill"], 1)
                    if kind == "O":
                        wait_taken(n, f"Z{q}")
                        for ii in range(2):
                            ins = nc.tensor.matmul(bank[:, ii * D:(ii + 1) * D], yT[:, q % 2, ii * P:(ii + 1) * P],
                                                   woT[:, bass.ds(p, 1), :].rearrange("p a c -> p (a c)"),
                                                   start=True, stop=True, skip_group_check=True)
                        ins.then_inc(m["t_fill"], 1)

            pe.sem_inc(m["s_fill"], S_PER)
            pe.sem_inc(m["t_fill"], T_PER)
            pe.sem_inc(m["pv_done"], PV_PER)
            pe.wait_ge(m["x_ld"], 16)
            for n in range(2):
                pe.wait_ge(w_ld[n], 16)
                for f in range(4):
                    if f >= 2:
                        pe.wait_ge(m["rope_read"], 2 * n + f - 1)
                    elif n == 1:
                        pe.wait_ge(m["v_taken"], at(2, 0, f))
                    proj_fill(n, f)
            pe.wait_ge(qk_ld[0], 16 * QK_DMAS)
            for i in range(4):
                if i < 2:
                    pe.wait_ge(m["v_taken"], at(2, 1, i))
                else:
                    pe.wait_ge(m["exp_done"], at(S_PER, 0, i - 2))
                score_fill(0, 0, i)
            with nc.tensor.Fori(0, ITERS - 1) as it:
                for s in range(2):
                    step(it * 2 + s, s, True, True)
            for s in range(2):
                step(STEPS - 2 + s, s, False, s == 0)

        @block.scalar
        def _(act):
            for u in range(NW + NX):
                act.wait_ge(m["setup_tr"], u + 1)
                bank = t_ps[:, u % 2, :]
                if u < NW:
                    p, k = W_UNITS[u]
                    if p >= 2:
                        act.wait_ge(wsp[p % 2], 16 * (p // 2))
                    nc.scalar.activation(w_sb[p % 2][:, 0, k, :], bank[:, 0:384], ACT.Copy).then_inc(m["setup_hi"], 1)
                else:
                    b, k, c = X_UNITS[u - NW]
                    if b >= 1:
                        act.wait_ge(m["xsp"], 16 * b)
                    nc.scalar.activation(xT[:, 0, k, 512 * c:512 * c + 512], bank, ACT.Copy).then_inc(m["setup_hi"], 1)
            for i, (r, c) in enumerate(WO_UNITS):
                act.wait_ge(m["wo_tr"], i + 1)
                nc.scalar.activation(woT[:, 4 * c:4 * c + 4, r * P:(r + 1) * P],
                                     t_ps[:, i % 2, :].rearrange("p (j c) -> p j c", j=4),
                                     ACT.Copy).then_inc(m["wo_ev"], 1)

            def round_hi(n, c):
                act.wait_ge(m["added"], 4 * n + 2 * c + 2)
                if not (isinstance(n, int) and n == 0):
                    if isinstance(n, int):
                        act.wait_ge(qk_ld[(n - 1) % 2], 16 * QK_DMAS * ((n - 1) // 2 + 1))
                    else:
                        act.wait_ge(qk_ld[s_now[0] ^ 1], 16 * QK_DMAS * ((n - 1) // 2 + 1))
                nc.scalar.activation(hi[:, :, 512 * c:512 * c + 512], roped[:], ACT.Copy).then_inc(m["hi_done"], 1)

            def take_v(n, s, f):
                act.wait_ge(m["p_fill"], 4 * n + f + 1)
                nc.scalar.activation(v_sb[s][:, 4 * (f - 2):4 * (f - 2) + 4, :],
                                     s_ps[:, f % 2, 0:512].rearrange("p (t c) -> p t c", t=4),
                                     ACT.Copy).then_inc(m["v_taken"], 1)

            s_now = [0]

            def exps(n, s, i):
                h, blk = i % 2, i // 2
                q = blk // 2
                w = (blk + 1) * P
                act.wait_ge(m["max_done"], at(S_PER, n, i))
                if i % 4 == 0:
                    before, m_ = (n, q - 2) if q >= 2 else (n - 1, q + 2)
                    act.wait_ge(m["t_fill"], at(T_PER, before, T_UNITS.index(f"U{m_}{2 * m_ + 1}")))
                nc.scalar.activation(prob[q % 2][:, h, blk % 2, 0:w], s_ps[:, i % 2, 0:w], ACT.Exp,
                                     bias=negm[:, s, i:i + 1], scale=1.0,
                                     accum_out=den[:, s, i:i + 1]).then_inc(m["exp_done"], 1)

            def step(n, s, projects, follows):
                s_now[0] = s
                for e in ORDER:
                    kind, q = e[0], int(e[1])
                    if kind == "S":
                        exps(n, s, int(e[1:]))
                    elif kind == "X" and follows:
                        exps(n + 1, 1 - s, q)
                    elif kind == "H" and projects:
                        round_hi(n + 2, q)
                    elif kind == "F" and projects and q >= 2:
                        if q == 2:
                            act.wait_ge(m["pv_done"], at(PV_PER, n, PV_PER - 1))
                        take_v(n + 2, s, q)
                    elif kind == "N":
                        act.wait_ge(m["pv_done"], at(PV_PER, n, U_UNITS.index(f"U{q}{2 * q + 1}")))
                        act.wait_ge(m["t_fill"], at(T_PER, *((n, T_UNITS.index(f"Y{q - 2}")) if q >= 2 else
                                                            (n - 1, T_UNITS.index(f"Y{q + 2}")))))
                        nc.scalar.activation(ych[:, q % 2, :], y_ps[:, q % 2, 0:256], ACT.Copy)\
                            .then_inc(m["y_taken"], 1)
                    elif e in A_UNITS:
                        u = T_UNITS.index(e)
                        act.wait_ge(m["t_fill"], at(T_PER, n, u))
                        bank = t_ps[:, u % 2, :]
                        if kind == "U":
                            uu = U_UNITS.index(e)
                            w = keys_of(q, int(e[2]))[0]
                            act.wait_ge(m["pv_done"], at(PV_PER, n, uu - 4))
                            ins = nc.scalar.activation(pT[:, uu % 4, 0:2 * w], bank[:, 0:2 * w], ACT.Copy)
                        else:
                            act.wait_ge(m["t_fill"], at(T_PER, *((n, T_UNITS.index(f"O{q - 2}")) if q >= 2 else
                                                                (n - 1, T_UNITS.index(f"O{q + 2}")))))
                            ins = nc.scalar.activation(yT[:, q % 2, :], bank[:, 0:256], ACT.Copy)
                        ins.then_inc(m["taken_a"], 1)

            act.sem_inc(m["exp_done"], S_PER)
            act.sem_inc(m["y_taken"], Y_PER)
            act.sem_inc(m["v_taken"], 2)
            act.sem_inc(m["taken_a"], len(A_UNITS))
            for n in range(2):
                for c in range(2):
                    round_hi(n, c)
                for f in (2, 3):
                    take_v(n, n, f)
            for i in range(4):
                exps(0, 0, i)
            with nc.scalar.Fori(0, ITERS - 1) as it:
                for s in range(2):
                    step(it * 2 + s, s, True, True)
            for s in range(2):
                step(STEPS - 2 + s, s, False, s == 0)

        @block.vector
        def _(dve):
            for u in range(NW + NX):
                dve.wait_ge(m["setup_hi"], u + 1)
                bank = t_ps[:, u % 2, :]
                if u < NW:
                    p, k = W_UNITS[u]
                    hi_part, lo_part, src = w_sb[p % 2][:, 0, k, :], w_sb[p % 2][:, 1, k, :], bank[:, 0:384]
                else:
                    b, k, c = X_UNITS[u - NW]
                    cs = slice(512 * c, 512 * c + 512)
                    hi_part, lo_part, src = xT[:, 0, k, cs], xT[:, 1, k, cs], bank
                nc.vector.tensor_tensor(lo_part, src, hi_part.bitcast(F32), ALU.subtract).then_inc(m["setup_lo"], 1)

            def rotate(n, c):
                p = n % PAIRS
                dve.wait_ge(m["p_fill"], 4 * n + c + 1)
                if not (isinstance(n, int) and n == 0 and c == 0):
                    dve.wait_ge(m["added"], 4 * n + 2 * c)
                cs = slice(512 * c, 512 * c + 512)
                first, second = s_ps[:, c, 0:512], s_ps[:, c, 512:1024]
                for k, (src, half, tab) in enumerate(((second, 1, cos), (first, 0, sin), (first, 0, cos),
                                                      (second, 1, sin))):
                    ins = nc.vector.scalar_tensor_tensor(out=rot[:, k, :], in0=src,
                                                         scalar=bias[:, half, bass.ds(p, 1)],
                                                         in1=tab[:, cs], op0=ALU.add, op1=ALU.mult)
                ins.then_inc(m["rope_read"], 1)

            def maximum(n, s, i):
                w = (i // 2 + 1) * P
                dve.wait_ge(m["s_fill"], at(S_PER, n, i))
                nc.vector.tensor_reduce(negm[:, s, i:i + 1], s_ps[:, i % 2, 0:w], AX_X, ALU.max,
                                        negate=True).then_inc(m["max_done"], 1)

            def step(n, s, projects, follows):
                for e in ORDER:
                    kind, q = e[0], int(e[1])
                    if kind == "S":
                        maximum(n, s, int(e[1:]))
                    elif kind == "X" and follows:
                        maximum(n + 1, 1 - s, q)
                    elif kind == "F" and projects and q < 2:
                        rotate(n + 2, q)
                    elif kind == "R":
                        dve.wait_ge(m["exp_done"], at(S_PER, n, 4 * q + 3))
                        nc.vector.reciprocal(rden[:, s, 4 * q:4 * q + 4], den[:, s, 4 * q:4 * q + 4])\
                            .then_inc(m["rden_done"], 1)
                    elif e in D_UNITS:
                        u = T_UNITS.index(e)
                        dve.wait_ge(m["t_fill"], at(T_PER, n, u))
                        bank = t_ps[:, u % 2, :]
                        if kind == "U":
                            uu = U_UNITS.index(e)
                            w = keys_of(q, int(e[2]))[0]
                            dve.wait_ge(m["pv_done"], at(PV_PER, n, uu - 4))
                            ins = nc.vector.tensor_copy(pT[:, uu % 4, 0:2 * w], bank[:, 0:2 * w])
                        elif kind == "Y":
                            dve.wait_ge(m["rden_done"], 4 * n + q + 1)
                            dve.wait_ge(m["t_fill"], at(T_PER, *((n, T_UNITS.index(f"Z{q - 2}")) if q >= 2 else
                                                                (n - 1, T_UNITS.index(f"Z{q + 2}")))))
                            ins = nc.vector.tensor_tensor(
                                yrow[:, q % 2, :].rearrange("p (g d) -> p g d", g=4),
                                bank[:, 0:256].rearrange("p (g d) -> p g d", g=4),
                                rden[:, s, 4 * q:4 * q + 4].rearrange("p (g a) -> p g a", a=1).broadcast_to([P, 4, HD]),
                                ALU.mult)
                        else:
                            tile = (n // PAIRS) * TB + 2 * q
                            acc = x1[:, bass.ds(tile, 2), :].rearrange("p t d -> p (t d)")
                            dve.wait_ge(m["taken_d"], at(len(D_UNITS), n - 1, D_UNITS.index(e)))
                            ins = nc.vector.tensor_tensor(acc, bank, acc, ALU.add)
                        ins.then_inc(m["taken_d"], 1)

            dve.wait_ge(m["wo_ev"], 4)
            dve.wait_ge(m["bias_in"], 16 * 9)
            nc.vector.tensor_scalar(vo[:], woT[:, 0, :], bias[:, 2, 0:1], None, ALU.mult).then_inc(m["vo_done"], 1)
            for p in range(1, PAIRS):
                dve.wait_ge(m["vo_done"], p)
                nc.vector.scalar_tensor_tensor(out=vo[:], in0=woT[:, p, :], scalar=bias[:, 2, p:p + 1], in1=vo[:],
                                               op0=ALU.mult, op1=ALU.add).then_inc(m["vo_done"], 1)

            dve.sem_inc(m["max_done"], S_PER)
            dve.sem_inc(m["taken_d"], len(D_UNITS))
            dve.wait_ge(m["tab_in"], 32)
            for n in range(2):
                for c in range(2):
                    rotate(n, c)
            for i in range(4):
                maximum(0, 0, i)
            with nc.vector.Fori(0, ITERS - 1) as it:
                for s in range(2):
                    step(it * 2 + s, s, True, True)
            for s in range(2):
                step(STEPS - 2 + s, s, False, s == 0)

E_, TOPK, HID = 16, 3, 512
HK = HID // P
SLOT_TILES = (NTOK * TOPK + E_ * (P - 1)) // P
SLOT_TILES += SLOT_TILES % 2
SLOTS = SLOT_TILES * P
GRP = 4


def routing_phase(nc, A, dram, S):
    x1, w1, w2, b1T = S["x1"], S["w1"], S["w2"], S["b1T"]
    slot_i, wts, gT, etile, b2r, ident = S["slot_i"], S["wts"], S["gT"], S["etile"], S["b2r"], S["ident"]
    with ExitStack() as ctx:
        def sb(name, shape, dt):
            return ctx.enter_context(nc.sbuf_tensor(name, shape, dt))

        bout = sb("bout", [P, D], F32)
        gate = sb("gate_sb", [P, DK, E_], F32)
        b1row = sb("b1row", [E_, HID], F32)
        tri = sb("tri", [P, P], BF16)
        ones = sb("ones", [P, P], BF16)
        onesf = sb("onesf", [P, P], F32)
        stats = sb("stats", [P, TILES, 6], F32)
        mv = sb("mv", [P, TILES, 2], F32)
        r = [sb(f"ln_{i}", [P, TILES], F32) for i in range(4)]
        xtt = sb("xtt", [P, 2, 512], F32)
        prob = sb("gprob", [P, TILES, E_], F32)
        tmp = sb("gtmp", [P, TILES, E_], F32)
        red = sb("red", [P, 2, TILES], F32)
        top = sb("top", [P, TILES, 8], F32)
        topi = sb("topi", [P, TILES, 8], U32)
        topf = sb("topf", [P, TOPK, TILES], F32)
        io16 = sb("io16", [P, E_], F32)
        iot = sb("iot", [P, SLOT_TILES], F32)
        oh = sb("oh", [P, TOPK, TILES, E_], F32)
        mask = sb("gmask", [P, TILES, E_], F32)
        maskb = sb("gmaskb", [P, TILES, E_], BF16)
        tot = sb("tot", [P, E_, TILES], F32)
        inc = sb("inc", [P, E_, TILES], F32)
        zero = sb("gzero", [P, E_ * TILES], F32)
        cnt = sb("cnt", [P, 6, E_], F32)
        cnti = sb("cnti", [P, 2, E_], I32)
        slots = sb("slots", [P, TILES, E_], F32)
        slotf = sb("slotf", [P, TOPK, TILES], F32)
        g32 = sb("g32", [P, TILES, 32], F32)
        ef = sb("ef", [1, SLOT_TILES], F32)
        eps = sb("eps", [P, 1], F32)

        tr_ps = ctx.enter_context(nc.psum_tensor("tr_ps", [P, 2, 512], F32))
        lg_ps = ctx.enter_context(nc.psum_tensor("lg_ps", [P, 512], F32))
        b1_ps = ctx.enter_context(nc.psum_tensor("b1_ps", [P, 512], F32))
        pre_ps = ctx.enter_context(nc.psum_tensor("pre_ps", [P, 512], F32))
        all_ps = ctx.enter_context(nc.psum_tensor("all_ps", [P, 512], F32))
        names = ("r_w r_small r_const r_chain r_ln r_var r_std r_x1 r_xtr r_xtt r_lg r_b1 r_sub r_exp r_mask "
                 "r_pre r_slots r_scat r_g32 r_gtr r_gt r_b2z r_b2").split()
        m = {k: ctx.enter_context(nc.semaphore(k)) for k in names}
        block = ctx.enter_context(nc.Block())

        @block.sync
        def _(sp):
            sp.dma_start(bout[:], A["b_out"].rearrange("(a d) -> a d", a=1).broadcast_to([P, D])).then_inc(m["r_small"], 16)
            sp.dma_start(gate[:], A["gate"].rearrange("(k p) e -> p k e", p=P)).then_inc(m["r_small"], 16)
            sp.dma_start(b1row[:], A["b1"]).then_inc(m["r_small"], 16)
            sp.wait_ge(m["r_b2z"], 1)
            for i in range(4):
                sp.dma_start(b2r[32 * i:32 * i + E_, :], A["b2"]).then_inc(m["r_b2"], 16)
            for e in range(E_):
                sp.dma_start(w1[:, e], A["W1"][e].rearrange("(k p) h -> p k h", p=P)).then_inc(m["r_w"], 16)
                sp.dma_start(w2[:, e], A["W2"][e].rearrange("(k p) d -> p k d", p=P)).then_inc(m["r_w"], 16)
            sp.wait_ge(m["r_b2"], 64)
            sp.wait_ge(m["r_w"], 32 * E_)

        @block.gpsimd
        def _(pool):
            pool.memset(b2r[:], 0.0).then_inc(m["r_b2z"], 1)
            pool.memset(tri[:], 1.0).then_inc(m["r_const"], 1)
            pool.memset(ones[:], 1.0).then_inc(m["r_const"], 1)
            pool.memset(zero[:], 0.0).then_inc(m["r_const"], 1)
            pool.memset(g32[:], 0.0).then_inc(m["r_const"], 1)
            pool.iota(io16[:], pattern=[[1, E_]], base=0, channel_multiplier=0,
                      allow_small_or_imprecise_dtypes=True).then_inc(m["r_const"], 1)
            pool.iota(iot[:], pattern=[[1, SLOT_TILES]], base=0, channel_multiplier=0,
                      allow_small_or_imprecise_dtypes=True).then_inc(m["r_const"], 1)
            pool.memset(onesf[:], 1.0).then_inc(m["r_const"], 1)
            pool.memset(ident[:], 0.0).then_inc(m["r_const"], 1)
            pool.wait_ge(m["r_const"], 8)
            pool.affine_select(out=ident[:], in_=ident[:], compare_op=ALU.not_equal, fill=1.0, base=0,
                               pattern=[[-1, P]], channel_multiplier=1).then_inc(m["r_const"], 1)
            pool.affine_select(out=tri[:], in_=tri[:], compare_op=ALU.is_gt, fill=0.0, base=0,
                               pattern=[[1, P]], channel_multiplier=-1).then_inc(m["r_const"], 1)
            pool.wait_ge(m["r_slots"], 1)
            for t in range(TILES):
                for k in range(TOPK):
                    pool.indirect_dma_start(
                        out=dram["xs"], out_offset=bass.IndirectOffsetOnAxis(ap=slot_i[:, k, t:t + 1], axis=0),
                        in_=x1[:, t, :], in_offset=None).then_inc(m["r_scat"], 16)
            pool.wait_ge(m["r_scat"], 16 * TILES * TOPK)

        @block.tensor
        def _(pe):
            pe.wait_ge(m["r_small"], 48)
            pe.wait_ge(m["r_const"], 10)
            for c in range(HK):
                nc.tensor.transpose(b1_ps[:, c * E_:(c + 1) * E_], b1row[:, c * P:(c + 1) * P], ident[0:E_, 0:E_])
            nc.tensor.matmul(b1_ps[:, D:2 * D], onesf[:], S["vo"][:], start=True, stop=True,
                             skip_group_check=True).then_inc(m["r_b1"], 1)

            def gate_logits(u):
                pe.wait_ge(m["r_xtt"], u + 1)
                for i in range(2):
                    t = 2 * u + i
                    for k in range(DK):
                        ins = nc.tensor.matmul(lg_ps[:, t * E_:(t + 1) * E_], xtt[:, u % 2, (2 * i + k) * P:(2 * i + k + 1) * P],
                                               gate[:, k, :], start=(k == 0), stop=(k == DK - 1), skip_group_check=True)
                ins.then_inc(m["r_lg"], 1)

            for u in range(TILES // 2):
                pe.wait_ge(m["r_x1"], 2 * u + 2)
                if u >= 2:
                    pe.wait_ge(m["r_xtt"], u - 1)
                for i in range(2):
                    for k in range(DK):
                        ins = nc.tensor.transpose(tr_ps[:, u % 2, (2 * i + k) * P:(2 * i + k + 1) * P],
                                                  x1[:, 2 * u + i, k * P:(k + 1) * P], ident[:])
                ins.then_inc(m["r_xtr"], 1)
                if u >= 1:
                    gate_logits(u - 1)
            gate_logits(TILES // 2 - 1)
            pe.wait_ge(m["r_mask"], 1)
            pe.wait_ge(m["r_const"], 7)
            mb = maskb[:].rearrange("p t e -> p (t e)")
            nc.tensor.matmul(pre_ps[:], tri[:], mb, start=True, stop=True)
            nc.tensor.matmul(all_ps[:], ones[:], mb, start=True, stop=True).then_inc(m["r_pre"], 1)
            pe.wait_ge(m["r_g32"], 1)
            for u in range(2):
                for i in range(4):
                    g = 4 * u + i
                    ins = nc.tensor.transpose(tr_ps[:, u, i * P:(i + 1) * P],
                                              g32[:, 4 * g:4 * g + 4, :].rearrange("p t e -> p (t e)"), ident[:])
                ins.then_inc(m["r_gtr"], 1)

        @block.scalar
        def _(act):
            act.wait_ge(m["r_var"], 1)
            nc.scalar.activation(r[0][:], mv[:, :, 1], ACT.Sqrt, bias=eps[:, 0:1]).then_inc(m["r_std"], 1)
            for u in range(TILES // 2):
                act.wait_ge(m["r_xtr"], u + 1)
                if u >= 2:
                    act.wait_ge(m["r_lg"], u - 1)
                nc.scalar.activation(xtt[:, u % 2, :], tr_ps[:, u % 2, :], ACT.Copy).then_inc(m["r_xtt"], 1)
            act.wait_ge(m["r_sub"], 1)
            nc.scalar.activation(prob[:], tmp[:], ACT.Exp).then_inc(m["r_exp"], 1)
            for u in range(2):
                act.wait_ge(m["r_gtr"], u + 1)
                nc.scalar.activation(gT[:, 512 * u:512 * u + 512], tr_ps[:, u, :], ACT.Copy).then_inc(m["r_gt"], 1)

        @block.vector
        def _(dve):
            chain = [0]

            def link(ins):
                chain[0] += 1
                ins.then_inc(m["r_chain"], 1)
                dve.wait_ge(m["r_chain"], chain[0])

            def bc(ap, n):
                return ap.rearrange("p (t a) -> p t a", a=1).broadcast_to([P, ap.shape[1], n])

            def bt(ap, n):
                return ap.rearrange("p (t a) -> p t a", t=1).broadcast_to([P, n, ap.shape[1]])

            V = nc.vector
            V.memset(eps[:], EPS).then_inc(m["r_ln"], 1)
            dve.wait_ge(m["r_small"], 48)
            dve.wait_ge(m["r_b1"], 1)
            V.tensor_copy(b1T[:].rearrange("p c e -> p (c e)"), b1_ps[:, 0:HK * E_])
            link(V.tensor_tensor(bout[:], b1_ps[:, D:2 * D], bout[:], ALU.add))
            for t in range(TILES):
                V.tensor_tensor(x1[:, t, :], x1[:, t, :], bout[:], ALU.add).then_inc(m["r_ln"], 1)
            for t in range(TILES):
                dve.wait_ge(m["r_ln"], t + 2)
                V.bn_stats(stats[:, t, :], x1[:, t, :]).then_inc(m["r_ln"], 1)
            dve.wait_ge(m["r_ln"], 1 + 2 * TILES)
            for t in range(TILES):
                ins = V.bn_aggr(mv[:, t, :], stats[:, t, :])
            ins.then_inc(m["r_var"], 1)
            dve.wait_ge(m["r_std"], 1)
            link(V.reciprocal(r[1][:], r[0][:]))
            link(V.tensor_tensor(r[2][:], r[1][:], r[1][:], ALU.mult))
            link(V.scalar_tensor_tensor(out=r[3][:], in0=mv[:, :, 1], scalar=EPS, in1=r[2][:], op0=ALU.add, op1=ALU.mult))
            link(V.tensor_scalar(r[2][:], r[3][:], -0.5, 1.5, ALU.mult, ALU.add))
            link(V.tensor_tensor(r[0][:], r[1][:], r[2][:], ALU.mult))
            for t in range(TILES):
                V.tensor_scalar(x1[:, t, :], x1[:, t, :], mv[:, t, 0:1], r[0][:, t:t + 1],
                                ALU.subtract, ALU.mult).then_inc(m["r_x1"], 1)
            dve.wait_ge(m["r_lg"], TILES // 2)
            lg = lg_ps[:].rearrange("p (t e) -> p t e", e=E_)
            link(V.tensor_reduce(red[:, 0, :], lg, AX_X, ALU.max))
            V.tensor_tensor(tmp[:], lg, bc(red[:, 0, :], E_), ALU.subtract).then_inc(m["r_sub"], 1)
            dve.wait_ge(m["r_exp"], 1)
            link(V.tensor_reduce(red[:, 0, :], prob[:], AX_X, ALU.add))
            link(V.reciprocal(red[:, 1, :], red[:, 0, :]))
            link(V.tensor_tensor(prob[:], prob[:], bc(red[:, 1, :], E_), ALU.mult))
            for t in range(TILES):
                ins = V.max(top[:, t, :], prob[:, t, :])
            link(ins)
            for t in range(TILES):
                ins = V.max_index(topi[:, t, :], top[:, t, :], prob[:, t, :])
            link(ins)
            dve.wait_ge(m["r_const"], 10)
            link(V.tensor_copy(topf[:], topi[:, :, 0:TOPK].rearrange("p t k -> p k t")))
            for k in range(TOPK):
                ins = V.tensor_tensor(oh[:, k], bt(io16[:], TILES), bc(topf[:, k, :], E_), ALU.is_equal)
            link(ins)
            link(V.tensor_tensor(mask[:], oh[:, 0], oh[:, 1], ALU.add))
            link(V.tensor_tensor(mask[:], mask[:], oh[:, 2], ALU.add))
            V.tensor_copy(maskb[:], mask[:]).then_inc(m["r_mask"], 1)
            link(V.tensor_reduce(red[:, 0, :], top[:, :, 0:TOPK], AX_X, ALU.add))
            link(V.tensor_scalar(red[:, 0, :], red[:, 0, :], 1e-12, None, ALU.max))
            link(V.reciprocal(red[:, 1, :], red[:, 0, :]))
            V.tensor_tensor(wts[:], top[:, :, 0:TOPK], bc(red[:, 1, :], TOPK), ALU.mult)
            link(V.tensor_tensor(tmp[:], prob[:], mask[:], ALU.mult))
            V.tensor_tensor(g32[:, :, 0:E_], tmp[:], bc(red[:, 1, :], E_), ALU.mult).then_inc(m["r_g32"], 1)
            dve.wait_ge(m["r_pre"], 1)
            link(V.tensor_copy(tot[:], all_ps[:].rearrange("p (t e) -> p e t", e=E_)))
            flat = "p e t -> p (e t)"
            link(V.tensor_tensor_scan(inc[:].rearrange(flat), tot[:].rearrange(flat), zero[:], 0.0, ALU.add, ALU.add))
            link(V.tensor_reduce(cnt[:, 0, :], tot[:], AX_X, ALU.add))
            link(V.tensor_scalar(cnt[:, 1, :], cnt[:, 0, :], float(P - 1), None, ALU.add))
            link(V.tensor_copy(cnti[:, 0, :], cnt[:, 1, :]))
            link(V.tensor_scalar(cnti[:, 1, :], cnti[:, 0, :], 7, None, ALU.logical_shift_right))
            link(V.tensor_copy(cnt[:, 2, :], cnti[:, 1, :]))
            link(V.tensor_tensor_scan(cnt[:, 3, :], cnt[:, 2, :], zero[:, 0:E_], 0.0, ALU.add, ALU.add))
            link(V.tensor_tensor(cnt[:, 4, :], cnt[:, 3, :], cnt[:, 2, :], ALU.subtract))
            link(V.tensor_tensor(cnt[:, 5, :], inc[:, :, TILES - 1], cnt[:, 0, :], ALU.subtract))
            link(V.scalar_tensor_tensor(out=cnt[:, 5, :], in0=cnt[:, 4, :], scalar=float(P), in1=cnt[:, 5, :],
                                        op0=ALU.mult, op1=ALU.subtract))
            link(V.tensor_tensor(inc[:], inc[:], tot[:], ALU.subtract))
            link(V.tensor_tensor(inc[:], inc[:], bc(cnt[:, 5, :], TILES), ALU.add))
            link(V.tensor_tensor(slots[:], pre_ps[:].rearrange("p (t e) -> p t e", e=E_),
                                 inc[:].rearrange("p e t -> p t e"), ALU.add))
            for k in range(TOPK):
                link(V.tensor_tensor(tmp[:], slots[:], oh[:, k], ALU.mult))
                link(V.tensor_reduce(slotf[:, k, :], tmp[:], AX_X, ALU.add))
            V.tensor_copy(slot_i[:], slotf[:]).then_inc(m["r_slots"], 1)
            part = SLOT_TILES // 2
            for i in range(2):
                emap = xtt[0:1].rearrange("p a c -> p (a c)")[:, 0:part * E_].rearrange("p (t e) -> p t e", e=E_)
                ts = slice(i * part, (i + 1) * part)
                link(V.tensor_tensor(emap, iot[0:1, ts].rearrange("p (t a) -> p t a", a=1).broadcast_to([1, part, E_]),
                                     cnt[0:1, 3, :].rearrange("p (a e) -> p a e", a=1).broadcast_to([1, part, E_]),
                                     ALU.is_ge))
                link(V.tensor_reduce(ef[:, ts], emap, AX_X, ALU.add))
            link(V.tensor_scalar(ef[:], ef[:], float(E_ - 1), None, ALU.min))
            link(V.tensor_copy(etile[:], ef[:]))


def expert_phase(nc, A, dram, S):
    w1, w2, b1T, etile, ident = S["w1"], S["w2"], S["b1T"], S["etile"], S["ident"]
    with ExitStack() as ctx:
        def sb(name, shape, dt):
            return ctx.enter_context(nc.sbuf_tensor(name, shape, dt))

        def psum(name):
            return ctx.enter_context(nc.psum_tensor(name, [P, 2, 512], F32))

        xin = sb("xin", [P, 2, D], F32)
        xT = sb("mxT", [P, 2, D], F32)
        h = sb("h", [P, 2, HID], F32)
        hT = sb("hT", [P, 2, HID], F32)
        y = sb("y", [P, 2, D], F32)
        x_ps, h_ps, ht_ps, yo_ps = psum("x_ps"), psum("h_ps"), psum("ht_ps"), psum("yo_ps")
        names = "m_xtr m_xT m_h m_htaken m_htr m_hT m_y m_ytaken".split()
        m = {k: ctx.enter_context(nc.semaphore(k)) for k in names}
        xs_ld = [ctx.enter_context(nc.semaphore(f"xs_ld{s}")) for s in range(2)]
        ys_st = [ctx.enter_context(nc.semaphore(f"ys_st{s}")) for s in range(2)]
        block = ctx.enter_context(nc.Block())
        xs = dram["xs"].rearrange("(t p) d -> t p d", p=P)
        ys = dram["ys"].rearrange("(t p) d -> t p d", p=P)
        LOOPS = SLOT_TILES // 2 - 1

        def done(t):
            return t + 3

        def pairs(t):
            return t // 2

        @block.sync
        def _(sp):
            for s in range(2):
                sp.dma_start(xin[:, s, :], xs[s]).then_inc(xs_ld[s], 16)
            with nc.sync.Fori(0, LOOPS) as it:
                for s in range(2):
                    t = it * 2 + s
                    sp.wait_ge(m["m_xtr"], done(t))
                    sp.dma_start(xin[:, s, :], xs[bass.ds(t + 2, 1)].rearrange("a p d -> (a p) d")).then_inc(xs_ld[s], 16)
                    sp.wait_ge(m["m_ytaken"], done(t))
                    sp.dma_start(ys[bass.ds(t, 1)].rearrange("a p d -> (a p) d"), y[:, s, :]).then_inc(ys_st[s], 16)
            for s in range(2):
                t = SLOT_TILES - 2 + s
                sp.wait_ge(m["m_ytaken"], done(t))
                sp.dma_start(ys[t], y[:, s, :]).then_inc(ys_st[s], 16)
            for s in range(2):
                sp.wait_ge(ys_st[s], 16 * (SLOT_TILES // 2 + 1))

        @block.tensor
        def _(pe):
            def expert(t):
                return pe.value_load(etile[0:1, bass.ds(t, 1)], min_val=0, max_val=E_ - 1)

            def turn_x(t, s):
                pe.wait_ge(xs_ld[s], 16 * (pairs(t) + 1))
                pe.wait_ge(m["m_xT"], done(t - 2))
                for k in range(DK):
                    ins = nc.tensor.transpose(x_ps[:, s, k * P:(k + 1) * P], xin[:, s, k * P:(k + 1) * P], ident[:])
                ins.then_inc(m["m_xtr"], 1)

            def first_layer(t, s):
                e = expert(t)
                pe.wait_ge(m["m_xT"], done(t))
                pe.wait_ge(m["m_htaken"], done(t - 2))
                for k in range(DK):
                    ins = nc.tensor.matmul(h_ps[:, s, :], xT[:, s, k * P:(k + 1) * P],
                                           w1[:, bass.ds(e, 1), k, :].rearrange("p a h -> p (a h)"),
                                           start=(k == 0), stop=(k == DK - 1))
                ins.then_inc(m["m_h"], 1)

            def turn_h(t, s):
                pe.wait_ge(m["m_htaken"], done(t))
                pe.wait_ge(m["m_hT"], done(t - 2))
                for c in range(HK):
                    ins = nc.tensor.transpose(ht_ps[:, s, c * P:(c + 1) * P], h[:, s, c * P:(c + 1) * P], ident[:])
                ins.then_inc(m["m_htr"], 1)

            def second_layer(t, s):
                e = expert(t)
                pe.wait_ge(m["m_hT"], done(t))
                pe.wait_ge(m["m_ytaken"], done(t - 2))
                for c in range(HK):
                    ins = nc.tensor.matmul(yo_ps[:, s, 0:D], hT[:, s, c * P:(c + 1) * P],
                                           w2[:, bass.ds(e, 1), c, :].rearrange("p a d -> p (a d)"),
                                           start=(c == 0), stop=(c == HK - 1))
                ins.then_inc(m["m_y"], 1)

            for k in ("m_xtr", "m_h", "m_htr", "m_y"):
                pe.sem_inc(m[k], 2)
            turn_x(0, 0)
            turn_x(1, 1)
            first_layer(0, 0)
            turn_h(0, 0)
            with nc.tensor.Fori(0, LOOPS) as it:
                for s in range(2):
                    t = it * 2 + s
                    first_layer(t + 1, 1 - s)
                    turn_x(t + 2, s)
                    second_layer(t, s)
                    turn_h(t + 1, 1 - s)
            t = SLOT_TILES - 2
            first_layer(t + 1, 1)
            second_layer(t, 0)
            turn_h(t + 1, 1)
            second_layer(t + 1, 1)

        @block.scalar
        def _(act):
            def take_x(t, s):
                act.wait_ge(m["m_xtr"], done(t))
                act.wait_ge(m["m_h"], done(t - 2))
                nc.scalar.activation(xT[:, s, :], x_ps[:, s, 0:D], ACT.Copy).then_inc(m["m_xT"], 1)

            def take_h(t, s):
                act.wait_ge(m["m_h"], done(t))
                act.wait_ge(m["m_htr"], done(t - 2))
                nc.scalar.activation(h[:, s, :], h_ps[:, s, :], ACT.Copy).then_inc(m["m_htaken"], 1)

            def take_y(t, s):
                act.wait_ge(m["m_y"], done(t))
                act.wait_ge(ys_st[s], 16 * (pairs(t) + 1))
                nc.scalar.activation(y[:, s, :], yo_ps[:, s, 0:D], ACT.Copy).then_inc(m["m_ytaken"], 1)

            for k in ("m_xT", "m_htaken", "m_ytaken"):
                act.sem_inc(m[k], 2)
            for s in range(2):
                act.sem_inc(ys_st[s], 16)
            take_x(0, 0)
            take_x(1, 1)
            take_h(0, 0)
            with nc.scalar.Fori(0, LOOPS) as it:
                for s in range(2):
                    t = it * 2 + s
                    take_h(t + 1, 1 - s)
                    take_x(t + 2, s)
                    take_y(t, s)
            t = SLOT_TILES - 2
            take_h(t + 1, 1)
            take_y(t, 0)
            take_y(t + 1, 1)

        @block.vector
        def _(dve):
            def take_hT(t, s):
                e = dve.value_load(etile[0:1, bass.ds(t, 1)], min_val=0, max_val=E_ - 1)
                dve.wait_ge(m["m_htr"], done(t))
                dve.wait_ge(m["m_y"], done(t - 2))
                for c in range(HK):
                    ins = nc.vector.tensor_scalar(hT[:, s, c * P:(c + 1) * P], ht_ps[:, s, c * P:(c + 1) * P],
                                                  b1T[:, c, bass.ds(e, 1)], 0.0, ALU.add, ALU.max)
                ins.then_inc(m["m_hT"], 1)

            dve.sem_inc(m["m_hT"], 2)
            take_hT(0, 0)
            with nc.vector.Fori(0, LOOPS) as it:
                for s in range(2):
                    take_hT(it * 2 + s + 1, 1 - s)
            take_hT(SLOT_TILES - 1, 1)


def combine_phase(nc, A, dram, S, out):
    x1, slot_i, wts, gT, b2r = S["x1"], S["slot_i"], S["wts"], S["gT"], S["b2r"]
    GROUPS = TILES // GRP
    with ExitStack() as ctx:
        def sb(name, shape, dt):
            return ctx.enter_context(nc.sbuf_tensor(name, shape, dt))

        got = sb("got", [P, 2, GRP * TOPK, D], F32)
        stats = sb("stats2", [P, 2, GRP, 6], F32)
        mv = sb("mv2", [P, 2, GRP, 2], F32)
        r = sb("r2", [P, 2, 4, GRP], F32)
        outb = sb("outb", [P, 2, GRP, D], F32)
        eps = sb("eps2", [P, 1], F32)
        b_ps = ctx.enter_context(nc.psum_tensor("b_ps", [P, GRP, 512], F32))
        names = "c_b2 c_added c_chain c_var c_std c_out".split()
        m = {k: ctx.enter_context(nc.semaphore(k)) for k in names}
        gat = [ctx.enter_context(nc.semaphore(f"gat{s}")) for s in range(2)]
        st = [ctx.enter_context(nc.semaphore(f"st{s}")) for s in range(2)]
        block = ctx.enter_context(nc.Block())
        out_v = out.rearrange("b (g t p) d -> (b g) p t d", p=P, t=GRP)

        @block.gpsimd
        def _(pool):
            for g in range(GROUPS):
                if g >= 2:
                    pool.wait_ge(m["c_added"], g - 1)
                for i in range(GRP):
                    for k in range(TOPK):
                        pool.indirect_dma_start(
                            out=got[:, g % 2, i * TOPK + k, :], out_offset=None, in_=dram["ys"],
                            in_offset=bass.IndirectOffsetOnAxis(ap=slot_i[:, k, g * GRP + i:g * GRP + i + 1], axis=0)
                        ).then_inc(gat[g % 2], 16)

        @block.tensor
        def _(pe):
            for g in range(GROUPS):
                for i in range(GRP):
                    if g >= 1:
                        pe.wait_ge(m["c_added"], g)
                    ins = nc.tensor.matmul(b_ps[:, i, 0:D], gT[32 * i:32 * i + 32, g * P:(g + 1) * P],
                                           b2r[32 * i:32 * i + 32, :], start=True, stop=True)
                ins.then_inc(m["c_b2"], 1)

        @block.scalar
        def _(act):
            for g in range(GROUPS):
                act.wait_ge(m["c_var"], g + 1)
                nc.scalar.activation(r[:, g % 2, 0, :], mv[:, g % 2, :, 1], ACT.Sqrt, bias=eps[:, 0:1])\
                    .then_inc(m["c_std"], 1)

        @block.sync
        def _(sp):
            for g in range(GROUPS):
                sp.wait_ge(m["c_out"], g + 1)
                sp.dma_start(out_v[g], outb[:, g % 2]).then_inc(st[g % 2], 16)
            for s in range(2):
                sp.wait_ge(st[s], 16 * GROUPS // 2)

        @block.vector
        def _(dve):
            chain = [0]
            V = nc.vector

            def link(ins):
                chain[0] += 1
                ins.then_inc(m["c_chain"], 1)
                dve.wait_ge(m["c_chain"], chain[0])

            link(V.memset(eps[:], EPS))
            for g in range(GROUPS):
                s = g % 2
                tiles = [g * GRP + i for i in range(GRP)]
                dve.wait_ge(m["c_b2"], g + 1)
                for i, t in enumerate(tiles):
                    ins = V.tensor_tensor(x1[:, t, :], b_ps[:, i, 0:D], x1[:, t, :], ALU.add)
                link(ins)
                dve.wait_ge(gat[s], 16 * GRP * TOPK * (g // 2 + 1))
                for k in range(TOPK):
                    for i, t in enumerate(tiles):
                        ins = V.scalar_tensor_tensor(out=x1[:, t, :], in0=got[:, s, i * TOPK + k, :],
                                                     scalar=wts[:, t, k:k + 1], in1=x1[:, t, :],
                                                     op0=ALU.mult, op1=ALU.add)
                    if k == TOPK - 1:
                        ins.then_inc(m["c_added"], 1)
                        dve.wait_ge(m["c_added"], g + 1)
                    else:
                        link(ins)
                for i, t in enumerate(tiles):
                    ins = V.bn_stats(stats[:, s, i, :], x1[:, t, :])
                link(ins)
                for i in range(GRP):
                    ins = V.bn_aggr(mv[:, s, i, :], stats[:, s, i, :])
                ins.then_inc(m["c_var"], 1)
                dve.wait_ge(m["c_std"], g + 1)
                rr = [r[:, s, j, :] for j in range(4)]
                link(V.reciprocal(rr[1], rr[0]))
                link(V.tensor_tensor(rr[2], rr[1], rr[1], ALU.mult))
                link(V.scalar_tensor_tensor(out=rr[3], in0=mv[:, s, :, 1], scalar=EPS, in1=rr[2], op0=ALU.add, op1=ALU.mult))
                link(V.tensor_scalar(rr[2], rr[3], -0.5, 1.5, ALU.mult, ALU.add))
                link(V.tensor_tensor(rr[0], rr[1], rr[2], ALU.mult))
                if g >= 2:
                    dve.wait_ge(st[s], 16 * (g // 2))
                for i, t in enumerate(tiles):
                    ins = V.tensor_scalar(outb[:, s, i, :], x1[:, t, :], mv[:, s, i, 0:1], rr[0][:, i:i + 1],
                                          ALU.subtract, ALU.mult)
                ins.then_inc(m["c_out"], 1)


def post_ln_block(nc, A, dram, out):
    with ExitStack() as ctx:
        def sb(name, shape, dt):
            return ctx.enter_context(nc.sbuf_tensor(name, shape, dt))

        S = {"x1": sb("x1", [P, TILES, D], F32), "vo": sb("vo", [P, D], F32)}
        attention_phase(nc, A, dram, S)
        S.update(slot_i=sb("slot_i", [P, TOPK, TILES], I32), wts=sb("wts", [P, TILES, TOPK], F32),
                 gT=sb("gT", [P, 2 * 512], F32), etile=sb("etile", [1, SLOT_TILES], I32),
                 b2r=sb("b2r", [P, D], F32), ident=sb("ident2", [P, P], F32))
        with ExitStack() as inner:
            S["w1"] = inner.enter_context(nc.sbuf_tensor("w1", [P, E_, DK, HID], F32))
            S["w2"] = inner.enter_context(nc.sbuf_tensor("w2", [P, E_, HK, D], F32))
            S["b1T"] = inner.enter_context(nc.sbuf_tensor("b1T", [P, HK, E_], F32))
            routing_phase(nc, A, dram, S)
            expert_phase(nc, A, dram, S)
        combine_phase(nc, A, dram, S, out)


def scratch(nc):
    shapes = {"xsplit": [B, P, 2 * DK * T], "wsplit": [PAIRS, P, 2 * DK * 384], "xs": [SLOTS, D], "ys": [SLOTS, D]}
    return {k: nc.dram_tensor(f"scratch_{k}", v, F32, kind="Internal").ap() for k, v in shapes.items()}


_INS = {'L0_attn_x': 'x', 'L0_attn_W_in': 'W_in', 'L0_attn_b_in': 'b_in', 'L0_attn_W_out': 'W_out',
        'L0_attn_b_out': 'b_out', 'L0_ffn_gate': 'gate', 'L0_ffn_W1': 'W1', 'L0_ffn_b1': 'b1', 'L0_ffn_W2': 'W2',
        'L0_ffn_b2': 'b2'}


def rotary_tables():
    p = np.arange(HALF, dtype=np.float32) / np.float32(HALF - 1)
    thetas = np.float32(10000.0) ** p
    pos = np.arange(T, dtype=np.float32)[:, None] / thetas[None, :]
    scale = np.float32(1.0 / np.sqrt(HD))

    def rows(table):
        return np.ascontiguousarray(np.concatenate([table.T * scale] * 2 + [table.T] * 2, axis=0))

    return rows(np.cos(pos)), rows(np.sin(pos))


def kernel(**inputs):
    import concourse.bacc as _bacc
    from concourse.bass_utils import run_bass_kernel_spmd as _run

    nc = _bacc.Bacc("TRN2", target_bir_lowering=False, num_devices=1)
    arrays, args = {}, {}
    for name, short in _INS.items():
        a = np.ascontiguousarray(inputs[name])
        arrays[f"in_{name}_dram"] = a
        args[short] = nc.dram_tensor(f"in_{name}_dram", a.shape, mybir.dt.from_np(a.dtype), kind="ExternalInput").ap()
    for short, a in zip(("cos", "sin"), rotary_tables()):
        arrays[f"in_{short}_dram"] = a
        args[short] = nc.dram_tensor(f"in_{short}_dram", a.shape, F32, kind="ExternalInput").ap()
    out = nc.dram_tensor("out_0_dram", (B, T, D), F32, kind="ExternalOutput").ap()
    post_ln_block(nc, args, scratch(nc), out)
    r = _run(nc, [arrays], core_ids=[0])
    return r.results[0]["out_0_dram"]
```

```python
from contextlib import ExitStack

import numpy as np

import concourse.bass as bass
from concourse import mybir

ALU = mybir.AluOpType
ACT = mybir.ActivationFunctionType
AX_X = mybir.AxisListType.X
F32 = mybir.dt.float32
F32R = mybir.dt.float32r
BF16 = mybir.dt.bfloat16
I32 = mybir.dt.int32
U32 = mybir.dt.uint32

P = 128
B, T, D = 4, 1024, 256
H, HD = 16, 64
HALF = HD // 2
NTOK = B * T
TILES = NTOK // P
TB = T // P
DK = D // P
PAIRS = H // 2
STEPS = B * PAIRS
CHUNKS = 4
ITERS = STEPS // 2
MASKED = -1.0e30
EPS = 1e-5

def parse(text):
    return [(w.rstrip("+-"), 2 if w[0] in "Frhv" else (w[-1] == "+") - (w[-1] == "-")) for w in text.split()]


S_PER, QK_DMAS = 16, 20
U_PER = 20
T_BANKS = 2
PE_ORDER = parse("""Z3- S6 U00 S7 O3- V00 U01 S8 U10 S9 V01 U11 U12 S10 V10 S11 V11 U13 Y0 V12 S12 V13 U20 U21 S13 Z0 U22 V20
U23 V21 O0 Y1 S14 V22 Z1 S15 O1 U24 F0 U25 U30 V23 U31 F1 V24 U32 U33 V25 V30 F2 Y2 V31 U34 S0+ V32 U35
V33 V34 U36 U37 F3 V35 Z2 V36 S1+ O2 V37 S2+ S3+ Y3 S4+ S5+""")
ACT_ORDER = parse("""u01 u10 E8 E9 u11 N0 u12 E10 E11 u21 N1 z0 E12 u23 E13 z1 E14 u24 E15 u25 u31 h0 u30 N2 h1 v2 u35 u36 u37
E0+ h2 v3 z2 E1+ N3 E2+ E3+ z3 E4+ E5+ E6+ E7+ h3""")
DVE_ORDER = parse("""M4 M5 M6 u00 M7 o3- M8 M9 M10 M11 R0 u13 y0 u20 M12 u22 M13 R1 o0 y1 M14 M15 o1 r0 r1 u32 R2 u33 R3 r2 y2
u34 M0+ r3 M1+ o2 M2+ M3+ y3""")


def events(order, kinds):
    return [(e, ahead) for e, ahead in order if e[0] in kinds]


T_FILLS = events(PE_ORDER, "UYZO")
TAKEN = {"D": events(DVE_ORDER, "uyo"), "A": events(ACT_ORDER, "uz")}
T_NAMES = [e for e, _ in T_FILLS]


def count(order, event, n):
    names = [e for e, _ in order]
    place = names.index(event)
    turn = n - order[place][1]
    if isinstance(n, int):
        return sum(min(max(turn + ahead + (i <= place), 0), STEPS) for i, (_, ahead) in enumerate(order))
    return turn * len(order) + sum(ahead + (i <= place) for i, (_, ahead) in enumerate(order))


def wait_for(engine, semaphore, value, n):
    if not (isinstance(n, int) and n < 0):
        engine.wait_ge(semaphore, value)


def user_before(users, event, turn):
    i = [e for e, _ in users].index(event)
    while True:
        i -= 1
        e, ahead = users[i % len(users)]
        n = turn + i // len(users) + ahead
        if not isinstance(turn, int) or 0 <= n < STEPS:
            return e, n
        if turn + i // len(users) < -2:
            return None


def keys_of(q, j):
    return (128, 1) if j == 2 * q + 1 else (256, 0)


def u_index(q, j):
    return q * (q + 1) + j


def score_banks(event):
    i = int(event[1:])
    if event[0] == "F":
        return ((0, 2), (2, 2), (0, 1), (2, 1))[i]
    return ((0, 2, 1, 3)[i % 4], 1) if i < 8 else (2 * (i % 2), 2)


SCORE_USERS = [[(e, ahead) for e, ahead in events(PE_ORDER, "SF")
                if score_banks(e)[0] <= bank < sum(score_banks(e))] for bank in range(4)]


def attention_phase(nc, A, dram, shared):
    x, W_in, b_in, W_out, cosT, sinT = A["x"], A["W_in"], A["b_in"], A["W_out"], A["cos"], A["sin"]
    xsplit, wsplit, = dram["xsplit"], dram["wsplit"]
    x1, vo = shared["x1"], shared["vo"]
    with ExitStack() as ctx:
        def sb(name, shape, dt):
            return ctx.enter_context(nc.sbuf_tensor(name, shape, dt))

        def sem(name):
            return ctx.enter_context(nc.semaphore(name))

        w_sb = [sb(f"w_sb{s}", [P, 2, DK, 256], F32R) for s in range(2)]
        wv_sb = sb("wv_sb", [P, 2, DK, 256], F32R)
        xT = sb("xT", [P, 2, DK, T], F32R)
        woT = sb("woT", [P, PAIRS, D], F32)
        rot = sb("rot", [P, 2, 512], F32)
        roped = sb("roped", [P, 512], F32)
        hi = sb("hi", [P, 2, T], F32R)
        lo = sb("lo", [P, 2, T], F32R)
        q1 = [[sb(f"q1_{s}{h}", [P, T], F32R) for h in range(2)] for s in range(2)]
        k1 = [[sb(f"k1_{s}{h}", [P, T], F32R) for h in range(2)] for s in range(2)]
        q2 = [sb(f"q2_{s}", [P, T], F32R) for s in range(2)]
        v_sb = sb("v_sb", [P, 2, TB, 2, P], F32)
        prob = [sb("prob0", [P, 2, 2, 768], F32), sb("prob1", [P, 2, 2, 1024], F32)]
        pT = sb("pT", [P, 4, 512], F32)
        cos = sb("cos_sb", [P, T], F32)
        sin = sb("sin_sb", [P, T], F32)
        ych = sb("ych", [P, 2, 256], F32)
        yrow = sb("yrow", [P, 2, 256], F32)
        yT = sb("yT", [P, 2, 256], F32)
        ident = sb("ident", [P, P], F32)
        identb = sb("identb", [P, P], BF16)
        maskb = sb("maskb", [P, P], BF16)
        bias = sb("bias", [P, 3, PAIRS], F32)
        zrow = sb("zrow", [P, D], F32)
        negm = sb("negm", [P, 2, 16], F32)
        den = sb("den", [P, 2, 16], F32)
        rden = sb("rden", [P, 2, 16], F32)

        s_ps = ctx.enter_context(nc.psum_tensor("s_ps", [P, 4, 512], F32))
        t_ps = ctx.enter_context(nc.psum_tensor("t_ps", [P, T_BANKS, 512], F32))
        y_ps = ctx.enter_context(nc.psum_tensor("y_ps", [P, 2, 512], F32))

        names = ("vo_done zeroed wv_ld xsp_v consts x_in w_in tab_in bias_in wo_in setup_tr setup_hi setup_lo xsp wo_tr wo_ev "
                 "x_ld s_fill p_fill t_fill pv_done y_taken max_done exp_done rope_read v_taken "
                 "taken_d taken_a added hi_done lo_done rden_done").split()
        m = {k: sem(k) for k in names}
        wsp = [sem(f"wsp{s}") for s in range(2)]
        w_ld = [sem(f"w_ld{s}") for s in range(2)]
        qk_ld = [sem(f"qk_ld{s}") for s in range(2)]

        w_raw_qk = prob[1][:].rearrange("p a b c -> p (a b c)").rearrange("p (n h d) -> p n h d", n=PAIRS, h=2)
        w_raw_v = prob[0][:].rearrange("p a b c -> p (a b c)")[:, 0:PAIRS * D].rearrange("p (n d) -> p n d", n=PAIRS)
        wo_raw = pT[:].rearrange("p a b -> p (a b)").rearrange("p (r c) -> p r c", r=2)

        W_UNITS = [u for c in range(PAIRS // 2) for u in (("qk", 2 * c), ("qk", 2 * c + 1), ("v", c))]
        X_UNITS = [(b, k, c) for b in range(B) for k in range(DK) for c in range(2)]
        WO_UNITS = [(r, c) for r in range(2) for c in range(2)]
        NW, NX = len(W_UNITS), len(X_UNITS)

        def flat(t):
            return t[:].rearrange("p a k c -> p (a k c)").bitcast(F32)

        def turns(engine, turn):
            for it in (-2, -1, 0, 1):
                turn(it, it % 4)
            with engine.Fori(0, STEPS // 4 - 1) as four:
                for i in (2, 3, 4, 5):
                    turn(four * 4 + i, i % 4)
            for it in (STEPS - 2, STEPS - 1, STEPS):
                turn(it, it % 4)

        def scores(bank, banks):
            return s_ps[:, bank:bank + banks, :].rearrange("p a b -> p (a b)")


        def wait_unit(engine, e, n):
            q, j = int(e[1]), int(e[2])
            w = keys_of(q, j)[0]
            unit = f"U{q}{j}"
            engine.wait_ge(m["t_fill"], count(T_FILLS, unit, n))
            old = U_PER * n + u_index(q, j) - 4
            wait_for(engine, m["pv_done"], old + 1, old)
            return pT[:, u_index(q, j) % 4, 0:2 * w], t_ps[:, T_NAMES.index(unit) % T_BANKS, 0:2 * w]

        block = ctx.enter_context(nc.Block())

        @block.sync
        def _(sp):
            for qk in range(2):
                for hh in range(2):
                    o = 32 * (2 * qk + hh)
                    for f in range(2):
                        src = W_in[qk * 1024:(qk + 1) * 1024, :].rearrange("(n h f d) c -> h f d n c",
                                                                           h=2, f=2, d=HALF)[hh, f]
                        sp.dma_start(w_raw_qk[o:o + 32, :, f, :], src).then_inc(m["w_in"], 16)
            sp.dma_start(w_raw_v, W_in[2048:3072, :].rearrange("(n r) c -> r n c", r=P)).then_inc(m["w_in"], 16)
            xv = x.rearrange("b (t p) d -> p (b t) d", p=P)
            for b in range(B):
                sp.dma_start(x1[:, b * TB:(b + 1) * TB, :], xv[:, b * TB:(b + 1) * TB, :]).then_inc(m["x_in"], 16)
            sp.dma_start(wo_raw, W_out.rearrange("(r p) c -> p r c", p=P)).then_inc(m["wo_in"], 16)
            sp.dma_start(cos[:], cosT).then_inc(m["tab_in"], 16)
            sp.dma_start(sin[:], sinT).then_inc(m["tab_in"], 16)
            for half in range(2):
                for qk in range(2):
                    for hh in range(2):
                        src = b_in[qk * 1024:(qk + 1) * 1024].rearrange("(n h f d) -> f h d n", h=2, f=2, d=HALF)[half, hh]
                        o = 32 * (2 * qk + hh)
                        sp.dma_start(bias[o:o + 32, half, :], src,
                                     allow_slow_non_contiguous=True).then_inc(m["bias_in"], 16)
            sp.dma_start(bias[:, 2, :], b_in[2048:3072].rearrange("(n r) -> r n", r=P),
                         allow_slow_non_contiguous=True).then_inc(m["bias_in"], 16)
            for i, (what, p) in enumerate(W_UNITS):
                sp.wait_ge(m["setup_hi"], i + 1)
                sp.wait_ge(m["setup_lo"], i + 1)
                if what == "qk":
                    sp.dma_start(wsplit[p], flat(w_sb[p % 2])).then_inc(wsp[p % 2], 16)
                else:
                    sp.dma_start(wsplit[PAIRS + p], flat(wv_sb)).then_inc(m["xsp_v"], 16)
            for b in range(B):
                sp.wait_ge(m["setup_hi"], NW + 4 * (b + 1))
                sp.wait_ge(m["setup_lo"], NW + 4 * (b + 1))
                sp.dma_start(xsplit[b], flat(xT)).then_inc(m["xsp"], 16)
            for s in range(2):
                sp.wait_ge(wsp[s], 16 * PAIRS // 2)
            sp.wait_ge(m["xsp_v"], 16 * PAIRS // 2)
            sp.wait_ge(m["xsp"], 16 * B)

            def load_w(s, pair):
                sp.dma_start(flat(w_sb[s]), pair).then_inc(w_ld[s], 16)

            def load_wv(pairs):
                sp.dma_start(flat(wv_sb), pairs).then_inc(m["wv_ld"], 16)

            def load_x(batch):
                sp.dma_start(flat(xT), batch).then_inc(m["x_ld"], 16)

            def stack_qk(n, s):
                sp.wait_ge(m["hi_done"], 4 * n + 4)
                sp.wait_ge(m["lo_done"], 4 * n + 4)
                for h in range(2):
                    for f in range(2):
                        q_in, k_in = 32 * h, 64 + 32 * h
                        pos = 32 * f
                        flip = 64 * h
                        for dst, src, i in ((q1[s][h][pos:pos + 32], hi, q_in),
                                            (q1[s][h][64 + pos:96 + pos], hi, q_in),
                                            (q2[s][64 * h + pos:64 * h + pos + 32], lo, q_in),
                                            (k1[s][h][flip + pos:flip + pos + 32], hi, k_in),
                                            (k1[s][h][64 - flip + pos:96 - flip + pos], lo, k_in)):
                            sp.dma_start(dst.bitcast(F32), src[i:i + 32, f, :].bitcast(F32)).then_inc(qk_ld[s], 16)

            def row(table, i):
                return table[bass.ds(i, 1)].rearrange("a p c -> (a p) c")

            def two_steps(n):
                for s in range(2):
                    new = row(wsplit, (n + s + 2) % PAIRS)
                    sp.wait_ge(m["p_fill"], 4 * (n + s) + 2)
                    load_w(s, new)
                    stack_qk(n + s, s)
                new = row(wsplit, PAIRS + (n // 2 + 1) % (PAIRS // 2))
                sp.wait_ge(m["p_fill"], 4 * (n + 1) + 4)
                load_wv(new)

            load_x(xsplit[0])
            for s in range(2):
                load_w(s, wsplit[s])
            load_wv(wsplit[PAIRS])
            rows = dram["xs"].shape[0] // P
            sp.wait_ge(m["consts"], 7)
            sp.dma_start(dram["xs"].rearrange("(p r) d -> p r d", p=P),
                         zrow[:].rearrange("p (a d) -> p a d", a=1).broadcast_to([P, rows, D])).then_inc(m["zeroed"], 16)
            with nc.sync.Fori(0, B - 1) as batch:
                with nc.sync.Fori(0, PAIRS // 2) as it:
                    two_steps(batch * PAIRS + it * 2)
                load_x(row(xsplit, batch + 1))
            with nc.sync.Fori(0, PAIRS // 2) as it:
                two_steps(it * 2 + (B - 1) * PAIRS)
            for s in range(2):
                sp.wait_ge(w_ld[s], 16 * (STEPS // 2 + 1))
            sp.wait_ge(m["wv_ld"], 16 * (STEPS // 2 + 1))
            sp.wait_ge(m["x_ld"], 16 * B)
            sp.wait_ge(m["zeroed"], 16)

        @block.gpsimd
        def _(pool):
            pool.memset(ident[:], 0.0).then_inc(m["consts"], 1)
            pool.memset(identb[:], 0.0).then_inc(m["consts"], 1)
            pool.memset(maskb[:], 0.0).then_inc(m["consts"], 1)
            pool.memset(zrow[:], 0.0).then_inc(m["consts"], 1)
            pool.wait_ge(m["consts"], 4)
            for t in (ident, identb):
                pool.affine_select(out=t[:], in_=t[:], compare_op=ALU.not_equal, fill=1.0, base=0,
                                   pattern=[[-1, P]], channel_multiplier=1).then_inc(m["consts"], 1)
            pool.affine_select(out=maskb[:], in_=maskb[:], compare_op=ALU.is_ge, fill=MASKED, base=0,
                               pattern=[[-1, P]], channel_multiplier=1).then_inc(m["consts"], 1)

            def rope_part(n, g):
                u = 4 * n + g
                half, cs = g % 2, slice(512 * (g // 2), 512 * (g // 2) + 512)
                pool.wait_ge(m["rope_read"], u + 1)
                if not (isinstance(u, int) and u == 0):
                    pool.wait_ge(m["hi_done"], u)
                    pool.wait_ge(m["lo_done"], u)
                nc.gpsimd.tensor_tensor(roped[:], rot[:, 0, :], rot[:, 1, :],
                                        ALU.subtract if half else ALU.add).then_inc(m["added"], 1)
                pool.wait_ge(m["added"], u + 1)
                pool.wait_ge(m["hi_done"], u + 1)
                nc.gpsimd.tensor_tensor(lo[:, half, cs], roped[:], hi[:, half, cs].bitcast(F32),
                                        ALU.subtract).then_inc(m["lo_done"], 1)

            for g in range(4):
                rope_part(0, g)
            with nc.gpsimd.Fori(1, STEPS) as n:
                for g in range(4):
                    rope_part(n, g)

        @block.tensor
        def _(pe):
            pe.wait_ge(m["consts"], 7)
            unit = 0

            def setup_bank():
                if unit >= 2:
                    pe.wait_ge(m["setup_hi"], unit - 1)
                    pe.wait_ge(m["setup_lo"], unit - 1)
                return t_ps[:, unit % 2, :]

            pe.wait_ge(m["w_in"], 16 * 9)
            for what, p in W_UNITS:
                bank = setup_bank()
                for i in range(4):
                    k, half = i // 2, i % 2
                    src = w_raw_qk[:, p, half] if what == "qk" else w_raw_v[:, 2 * p + half]
                    ins = nc.tensor.transpose(bank[:, i * P:(i + 1) * P], src[:, k * P:(k + 1) * P], ident[:])
                ins.then_inc(m["setup_tr"], 1)
                unit += 1
            for b, k, c in X_UNITS:
                pe.wait_ge(m["x_in"], 64)
                bank = setup_bank()
                for i in range(4):
                    src = x1[:, b * TB + 4 * c + i, k * P:(k + 1) * P]
                    ins = nc.tensor.transpose(bank[:, i * P:(i + 1) * P], src, ident[:])
                ins.then_inc(m["setup_tr"], 1)
                unit += 1
            pe.wait_ge(m["wo_in"], 16)
            for i, (r, c) in enumerate(WO_UNITS):
                if i < 2:
                    pe.wait_ge(m["setup_hi"], unit)
                    pe.wait_ge(m["setup_lo"], unit)
                else:
                    pe.wait_ge(m["wo_ev"], i - 1)
                for j in range(4):
                    src = wo_raw[:, r, (4 * c + j) * P:(4 * c + j + 1) * P]
                    ins = nc.tensor.transpose(t_ps[:, i % 2, j * P:(j + 1) * P], src, ident[:])
                ins.then_inc(m["wo_tr"], 1)
            pe.wait_ge(m["wo_ev"], 4)

            def score_fill(s, i):
                h, blk = i % 2, i // 2
                width = (blk + 1) * P
                rows = slice(64 * h, 64 * h + 64)
                bank = score_banks(f"S{i}")[0]
                for c0 in range(0, width, 512):
                    w = min(512, width - c0)
                    out = s_ps[:, bank + c0 // 512, 0:w]
                    last = c0 + w == width
                    qs = slice(blk * P, blk * P + P)
                    nc.tensor.matmul(out, q1[s][h][:, qs], k1[s][h][:, c0:c0 + w], start=True, stop=False,
                                     skip_group_check=True)
                    ins = nc.tensor.matmul(out, q2[s][rows, qs], k1[s][h][rows, c0:c0 + w], start=False,
                                           stop=not last, skip_group_check=True)
                ins = nc.tensor.matmul(out[:, w - P:w], identb[:], maskb[:], start=False, stop=True,
                                       skip_group_check=True)
                ins.then_inc(m["s_fill"], 1)

            PRODUCTS = [(a, b, k) for a, b in ((0, 0), (0, 1), (1, 0)) for k in range(DK)]

            def proj_fill(s, f):
                bank = score_banks(f"F{f}")[0]
                for i in range(2):
                    for a, b, k in PRODUCTS:
                        if f < 2:
                            out = s_ps[:, bank + i, :]
                            left, right = w_sb[s][:, a, k, i * P:(i + 1) * P], xT[:, b, k, 512 * f:512 * f + 512]
                        else:
                            t = 4 * s + 2 * (f - 2) + i
                            out = s_ps[:, bank, i * 256:(i + 1) * 256]
                            left, right = xT[:, b, k, t * P:(t + 1) * P], wv_sb[:, a, k, :]
                        ins = nc.tensor.matmul(out, left, right, start=(a, b, k) == PRODUCTS[0],
                                               stop=(a, b, k) == PRODUCTS[-1], skip_group_check=True)
                ins.then_inc(m["p_fill"], 1)

            def wait_taken(unit, n):
                take = unit[0].lower() + unit[1:]
                by = "D" if take in [e for e, _ in TAKEN["D"]] else "A"
                pe.wait_ge(m["taken_d" if by == "D" else "taken_a"], count(TAKEN[by], take, n))

            def wait_score_banks(event, turn):
                first, banks = score_banks(event)
                had = []
                for users in SCORE_USERS[first:first + banks]:
                    user = user_before(users, event, turn)
                    if user and user[0] not in had:
                        had.append(user[0])
                        e, n = user
                        i = int(e[1:])
                        if e[0] == "S":
                            pe.wait_ge(m["exp_done"], S_PER * n + i + 1)
                        elif i < 2:
                            pe.wait_ge(m["rope_read"], 4 * n + 2 * i + 2)
                        else:
                            pe.wait_ge(m["v_taken"], 2 * n + i - 1)

            def turn(it, phase):
                for e, ahead in PE_ORDER:
                    n, s, pairs = it + ahead, (phase + ahead) % 2, (phase + ahead) // 2 % 2
                    if isinstance(n, int) and not 0 <= n < STEPS:
                        continue
                    kind, q = e[0], int(e[1])
                    if kind in "SF":
                        wait_score_banks(e, it)
                    if kind in "UYZO":
                        u = T_NAMES.index(e)
                        old = user_before(T_FILLS[u % T_BANKS::T_BANKS], e, it)
                        if old:
                            wait_taken(*old)
                        bank = t_ps[:, u % T_BANKS, :]
                    if kind == "S":
                        if e == "S0":
                            pe.wait_ge(qk_ld[s], 16 * QK_DMAS * (n // 2 + 1))
                        score_fill(s, int(e[1:]))
                    elif kind == "F":
                        if q == 0:
                            pe.wait_ge(w_ld[s], 16 * (n // 2 + 1))
                            pe.wait_ge(m["x_ld"], 16 * (n // PAIRS + 1))
                        if q == 2 and s == 0:
                            pe.wait_ge(m["wv_ld"], 16 * (n // 2 + 1))
                        proj_fill(s, q)
                    elif kind == "U":
                        j = int(e[2])
                        w, first = keys_of(q, j)
                        pe.wait_ge(m["exp_done"], S_PER * n + 4 * q + 4)
                        for h in range(2):
                            for ii in range(first, 2):
                                o = h * w + (ii - first) * P
                                ins = nc.tensor.transpose(bank[:, o:o + P], prob[q % 2][:, h, ii, j * P:(j + 1) * P],
                                                          ident[:])
                        ins.then_inc(m["t_fill"], 1)
                    elif kind == "V":
                        j = int(e[2])
                        w, first = keys_of(q, j)
                        if j == 0:
                            old = 4 * n + q - 2
                            wait_for(pe, m["y_taken"], old + 1, old)
                        if j % 2 == 0:
                            pe.wait_ge(m["v_taken"], 2 * (n - s + j // 4) + j // 2 % 2 + 1)
                        wait_taken(f"U{q}{j}", n)
                        for h in range(2):
                            ins = nc.tensor.matmul(y_ps[64 * h:64 * h + 64, q % 2, 256 - w:256],
                                                   v_sb[:, pairs, j, s, 64 * h:64 * h + 64],
                                                   pT[:, u_index(q, j) % 4, h * w:(h + 1) * w],
                                                   start=(j == 0), stop=(j == 2 * q + 1), skip_group_check=True)
                        ins.then_inc(m["pv_done"], 1)
                    elif kind == "Y":
                        pe.wait_ge(m["y_taken"], 4 * n + q + 1)
                        for ii in range(2):
                            ins = nc.tensor.transpose(bank[:, ii * P:(ii + 1) * P], ych[:, q % 2, ii * P:(ii + 1) * P],
                                                      ident[:])
                        ins.then_inc(m["t_fill"], 1)
                    elif kind == "Z":
                        wait_taken(f"Y{q}", n)
                        for ii in range(2):
                            ins = nc.tensor.transpose(bank[:, ii * P:(ii + 1) * P], yrow[:, q % 2, ii * P:(ii + 1) * P],
                                                      ident[:])
                        ins.then_inc(m["t_fill"], 1)
                    elif kind == "O":
                        wait_taken(f"Z{q}", n)
                        for ii in range(2):
                            ins = nc.tensor.matmul(bank[:, ii * D:(ii + 1) * D], yT[:, q % 2, ii * P:(ii + 1) * P],
                                                   woT[:, bass.ds(n % PAIRS, 1), :].rearrange("p a c -> p (a c)"),
                                                   start=True, stop=True, skip_group_check=True)
                        ins.then_inc(m["t_fill"], 1)

            turns(nc.tensor, turn)

        @block.scalar
        def _(act):
            for u in range(NW + NX):
                act.wait_ge(m["setup_tr"], u + 1)
                bank = t_ps[:, u % 2, :]
                if u < NW:
                    what, p = W_UNITS[u]
                    if what == "qk" and p >= 2:
                        act.wait_ge(wsp[p % 2], 16 * (p // 2))
                    if what == "v" and p >= 1:
                        act.wait_ge(m["xsp_v"], 16 * p)
                    nc.scalar.activation((w_sb[p % 2] if what == "qk" else wv_sb)[:, 0],
                                         bank.rearrange("p (k c) -> p k c", k=DK), ACT.Copy).then_inc(m["setup_hi"], 1)
                else:
                    b, k, c = X_UNITS[u - NW]
                    if b >= 1:
                        act.wait_ge(m["xsp"], 16 * b)
                    nc.scalar.activation(xT[:, 0, k, 512 * c:512 * c + 512], bank, ACT.Copy).then_inc(m["setup_hi"], 1)
            for i, (r, c) in enumerate(WO_UNITS):
                act.wait_ge(m["wo_tr"], i + 1)
                nc.scalar.activation(woT[:, 4 * c:4 * c + 4, r * P:(r + 1) * P],
                                     t_ps[:, i % 2, :].rearrange("p (j c) -> p j c", j=4),
                                     ACT.Copy).then_inc(m["wo_ev"], 1)

            def turn(it, phase):
                for e, ahead in ACT_ORDER:
                    n, s, pairs = it + ahead, (phase + ahead) % 2, (phase + ahead) // 2 % 2
                    if isinstance(n, int) and not 0 <= n < STEPS:
                        continue
                    kind, q = e[0], int(e[1])
                    if kind == "E":
                        i = int(e[1:])
                        h, blk = i % 2, i // 2
                        q = blk // 2
                        w = (blk + 1) * P
                        bank, banks = score_banks(f"S{i}")
                        act.wait_ge(m["max_done"], S_PER * n + i + 1)
                        if i % 4 == 0:
                            c, old = (q - 2, n) if q >= 2 else (q + 2, n - 1)
                            wait_for(act, m["t_fill"], count(T_FILLS, f"U{c}{2 * c + 1}", old), old)
                        nc.scalar.activation(prob[q % 2][:, h, blk % 2, 0:w], scores(bank, banks)[:, 0:w], ACT.Exp,
                                             bias=negm[:, s, i:i + 1], scale=1.0,
                                             accum_out=den[:, s, i:i + 1]).then_inc(m["exp_done"], 1)
                    elif kind == "h":
                        act.wait_ge(m["added"], 4 * n + q + 1)
                        if q == 0:
                            wait_for(act, qk_ld[1 - s], 16 * QK_DMAS * ((n - 1) // 2 + 1), n - 1)
                        nc.scalar.activation(hi[:, q % 2, 512 * (q // 2):512 * (q // 2) + 512], roped[:],
                                             ACT.Copy).then_inc(m["hi_done"], 1)
                    elif kind == "v":
                        act.wait_ge(m["p_fill"], 4 * n + q + 1)
                        old = n - 3 - s
                        wait_for(act, m["pv_done"], U_PER * (old + 1), old)
                        t, bank = 4 * s + 2 * (q - 2), score_banks(f"F{q}")[0]
                        nc.scalar.activation(v_sb[:, pairs, t:t + 2].rearrange("p t s c -> p (t s c)"), s_ps[:, bank, :], ACT.Copy)\
                            .then_inc(m["v_taken"], 1)
                    elif kind == "N":
                        act.wait_ge(m["pv_done"], U_PER * n + u_index(q, 2 * q + 1) + 1)
                        c, old = (q - 2, n) if q >= 2 else (q + 2, n - 1)
                        wait_for(act, m["t_fill"], count(T_FILLS, f"Y{c}", old), old)
                        nc.scalar.activation(ych[:, q % 2, :], y_ps[:, q % 2, 0:256], ACT.Copy)\
                            .then_inc(m["y_taken"], 1)
                    elif kind == "u":
                        dst, src = wait_unit(act, e, n)
                        nc.scalar.activation(dst, src, ACT.Copy).then_inc(m["taken_a"], 1)
                    elif kind == "z":
                        act.wait_ge(m["t_fill"], count(T_FILLS, f"Z{q}", n))
                        c, old = (q - 2, n) if q >= 2 else (q + 2, n - 1)
                        wait_for(act, m["t_fill"], count(T_FILLS, f"O{c}", old), old)
                        nc.scalar.activation(yT[:, q % 2, :], t_ps[:, T_NAMES.index(f"Z{q}") % T_BANKS, 0:256],
                                             ACT.Copy).then_inc(m["taken_a"], 1)

            turns(nc.scalar, turn)

        @block.vector
        def _(dve):
            for u in range(NW + NX):
                dve.wait_ge(m["setup_hi"], u + 1)
                bank = t_ps[:, u % 2, :]
                if u < NW:
                    what, p = W_UNITS[u]
                    w = w_sb[p % 2] if what == "qk" else wv_sb
                    hi_part, lo_part, src = w[:, 0], w[:, 1], bank.rearrange("p (k c) -> p k c", k=DK)
                else:
                    b, k, c = X_UNITS[u - NW]
                    cs = slice(512 * c, 512 * c + 512)
                    hi_part, lo_part, src = xT[:, 0, k, cs], xT[:, 1, k, cs], bank
                nc.vector.tensor_tensor(lo_part, src, hi_part.bitcast(F32), ALU.subtract).then_inc(m["setup_lo"], 1)

            def turn(it, phase):
                for e, ahead in DVE_ORDER:
                    n, s, pairs = it + ahead, (phase + ahead) % 2, (phase + ahead) // 2 % 2
                    if isinstance(n, int) and not 0 <= n < STEPS:
                        continue
                    kind, q = e[0], int(e[1])
                    if kind == "M":
                        i = int(e[1:])
                        w = (i // 2 + 1) * P
                        dve.wait_ge(m["s_fill"], S_PER * n + i + 1)
                        nc.vector.tensor_reduce(negm[:, s, i:i + 1], scores(*score_banks(f"S{i}"))[:, 0:w], AX_X,
                                                ALU.max, negate=True).then_inc(m["max_done"], 1)
                    elif kind == "r":
                        half, c = q % 2, q // 2
                        dve.wait_ge(m["p_fill"], 4 * n + c + 1)
                        wait_for(dve, m["added"], 4 * n + q, 4 * n + q - 1)
                        cs = slice(512 * c, 512 * c + 512)
                        for k, (src, tab) in enumerate(((1, cos), (0, sin)) if half == 0 else ((0, cos), (1, sin))):
                            ins = nc.vector.scalar_tensor_tensor(out=rot[:, k, :], in0=s_ps[:, 2 * c + src, :],
                                                                 scalar=bias[:, src, bass.ds(n % PAIRS, 1)],
                                                                 in1=tab[:, cs], op0=ALU.add, op1=ALU.mult)
                        ins.then_inc(m["rope_read"], 1)
                    elif kind == "R":
                        dve.wait_ge(m["exp_done"], S_PER * n + 4 * q + 4)
                        nc.vector.reciprocal(rden[:, s, 4 * q:4 * q + 4], den[:, s, 4 * q:4 * q + 4])\
                            .then_inc(m["rden_done"], 1)
                    elif kind == "u":
                        dst, src = wait_unit(dve, e, n)
                        nc.vector.tensor_copy(dst, src).then_inc(m["taken_d"], 1)
                    elif kind == "y":
                        dve.wait_ge(m["t_fill"], count(T_FILLS, f"Y{q}", n))
                        dve.wait_ge(m["rden_done"], 4 * n + q + 1)
                        c, old = (q - 2, n) if q >= 2 else (q + 2, n - 1)
                        wait_for(dve, m["t_fill"], count(T_FILLS, f"Z{c}", old), old)
                        bank = t_ps[:, T_NAMES.index(f"Y{q}") % T_BANKS, :]
                        nc.vector.tensor_tensor(
                            yrow[:, q % 2, :].rearrange("p (g d) -> p g d", g=4),
                            bank[:, 0:256].rearrange("p (g d) -> p g d", g=4),
                            rden[:, s, 4 * q:4 * q + 4].rearrange("p (g a) -> p g a", a=1).broadcast_to([P, 4, HD]),
                            ALU.mult).then_inc(m["taken_d"], 1)
                    elif kind == "o":
                        dve.wait_ge(m["t_fill"], count(T_FILLS, f"O{q}", n))
                        wait_for(dve, m["taken_d"], count(TAKEN["D"], e, n - 1), n - 1)
                        acc = x1[:, bass.ds((n // PAIRS) * TB + 2 * q, 2), :].rearrange("p t d -> p (t d)")
                        nc.vector.tensor_tensor(acc, t_ps[:, T_NAMES.index(f"O{q}") % T_BANKS, :], acc,
                                                ALU.add).then_inc(m["taken_d"], 1)

            dve.wait_ge(m["wo_ev"], 4)
            dve.wait_ge(m["bias_in"], 16 * 9)
            nc.vector.tensor_scalar(vo[:], woT[:, 0, :], bias[:, 2, 0:1], None, ALU.mult).then_inc(m["vo_done"], 1)
            for p in range(1, PAIRS):
                dve.wait_ge(m["vo_done"], p)
                nc.vector.scalar_tensor_tensor(out=vo[:], in0=woT[:, p, :], scalar=bias[:, 2, p:p + 1], in1=vo[:],
                                               op0=ALU.mult, op1=ALU.add).then_inc(m["vo_done"], 1)

            dve.wait_ge(m["tab_in"], 32)
            turns(nc.vector, turn)

E_, TOPK, HID = 16, 3, 512
HK = HID // P
XIN = 4
SLOT_TILES = (NTOK * TOPK + E_ * (P - 1)) // P
SLOT_TILES += -SLOT_TILES % XIN
SLOTS = SLOT_TILES * P
GRP = 4


def routing_phase(nc, A, dram, S):
    x1, w1, w2, b1T = S["x1"], S["w1"], S["w2"], S["b1T"]
    slot_i, wts, gT, etile, b2r, ident = S["slot_i"], S["wts"], S["gT"], S["etile"], S["b2r"], S["ident"]
    with ExitStack() as ctx:
        def sb(name, shape, dt):
            return ctx.enter_context(nc.sbuf_tensor(name, shape, dt))

        bout = sb("bout", [P, D], F32)
        gate = sb("gate_sb", [P, DK, E_], F32)
        b1row = sb("b1row", [E_, HID], F32)
        tri = sb("tri", [P, P], BF16)
        ones = sb("ones", [P, P], BF16)
        onesf = sb("onesf", [P, P], F32)
        stats = sb("stats", [P, TILES, 6], F32)
        mv = sb("mv", [P, TILES, 2], F32)
        r = [sb(f"ln_{i}", [P, TILES], F32) for i in range(4)]
        xtt = sb("xtt", [P, 2, 512], F32)
        prob = sb("gprob", [P, TILES, E_], F32)
        tmp = sb("gtmp", [P, TILES, E_], F32)
        red = sb("red", [P, 2, TILES], F32)
        top = sb("top", [P, TILES, 8], F32)
        topi = sb("topi", [P, TILES, 8], U32)
        topf = sb("topf", [P, TOPK, TILES], F32)
        io16 = sb("io16", [P, E_], F32)
        iot = sb("iot", [P, SLOT_TILES], F32)
        oh = sb("oh", [P, TOPK, TILES, E_], F32)
        mask = sb("gmask", [P, TILES, E_], F32)
        maskb = sb("gmaskb", [P, TILES, E_], BF16)
        tot = sb("tot", [P, E_, TILES], F32)
        inc = sb("inc", [P, E_, TILES], F32)
        zero = sb("gzero", [P, E_ * TILES], F32)
        cnt = sb("cnt", [P, 6, E_], F32)
        cnti = sb("cnti", [P, 2, E_], I32)
        slots = sb("slots", [P, TILES, E_], F32)
        slotf = sb("slotf", [P, TOPK, TILES], F32)
        g32 = sb("g32", [P, TILES, 32], F32)
        ef = sb("ef", [1, SLOT_TILES], F32)
        eps = sb("eps", [P, 1], F32)

        tr_ps = ctx.enter_context(nc.psum_tensor("tr_ps", [P, 2, 512], F32))
        lg_ps = ctx.enter_context(nc.psum_tensor("lg_ps", [P, 512], F32))
        b1_ps = ctx.enter_context(nc.psum_tensor("b1_ps", [P, 512], F32))
        pre_ps = ctx.enter_context(nc.psum_tensor("pre_ps", [P, 512], F32))
        all_ps = ctx.enter_context(nc.psum_tensor("all_ps", [P, 512], F32))
        names = ("r_w r_small r_const r_chain r_ln r_var r_std r_x1 r_xtr r_xtt r_lg r_b1 r_sub r_exp r_mask "
                 "r_pre r_slots r_scat r_g32 r_gtr r_gt r_b2z r_b2").split()
        m = {k: ctx.enter_context(nc.semaphore(k)) for k in names}
        block = ctx.enter_context(nc.Block())

        @block.sync
        def _(sp):
            sp.dma_start(bout[:], A["b_out"].rearrange("(a d) -> a d", a=1).broadcast_to([P, D])).then_inc(m["r_small"], 16)
            sp.dma_start(gate[:], A["gate"].rearrange("(k p) e -> p k e", p=P)).then_inc(m["r_small"], 16)
            sp.dma_start(b1row[:], A["b1"]).then_inc(m["r_small"], 16)
            sp.wait_ge(m["r_b2z"], 1)
            for i in range(4):
                sp.dma_start(b2r[32 * i:32 * i + E_, :], A["b2"]).then_inc(m["r_b2"], 16)
            for e in range(E_):
                sp.dma_start(w1[:, e], A["W1"][e].rearrange("(k p) h -> p k h", p=P)).then_inc(m["r_w"], 16)
                sp.dma_start(w2[:, e], A["W2"][e].rearrange("(k p) d -> p k d", p=P)).then_inc(m["r_w"], 16)
            sp.wait_ge(m["r_b2"], 64)
            sp.wait_ge(m["r_w"], 32 * E_)

        @block.gpsimd
        def _(pool):
            pool.memset(b2r[:], 0.0).then_inc(m["r_b2z"], 1)
            pool.memset(tri[:], 1.0).then_inc(m["r_const"], 1)
            pool.memset(ones[:], 1.0).then_inc(m["r_const"], 1)
            pool.memset(zero[:], 0.0).then_inc(m["r_const"], 1)
            pool.memset(g32[:], 0.0).then_inc(m["r_const"], 1)
            pool.iota(io16[:], pattern=[[1, E_]], base=0, channel_multiplier=0,
                      allow_small_or_imprecise_dtypes=True).then_inc(m["r_const"], 1)
            pool.iota(iot[:], pattern=[[1, SLOT_TILES]], base=0, channel_multiplier=0,
                      allow_small_or_imprecise_dtypes=True).then_inc(m["r_const"], 1)
            pool.memset(onesf[:], 1.0).then_inc(m["r_const"], 1)
            pool.memset(ident[:], 0.0).then_inc(m["r_const"], 1)
            pool.wait_ge(m["r_const"], 8)
            pool.affine_select(out=ident[:], in_=ident[:], compare_op=ALU.not_equal, fill=1.0, base=0,
                               pattern=[[-1, P]], channel_multiplier=1).then_inc(m["r_const"], 1)
            pool.affine_select(out=tri[:], in_=tri[:], compare_op=ALU.is_gt, fill=0.0, base=0,
                               pattern=[[1, P]], channel_multiplier=-1).then_inc(m["r_const"], 1)
            pool.wait_ge(m["r_slots"], 1)
            for t in range(TILES):
                for k in range(TOPK):
                    pool.indirect_dma_start(
                        out=dram["xs"], out_offset=bass.IndirectOffsetOnAxis(ap=slot_i[:, k, t:t + 1], axis=0),
                        in_=x1[:, t, :], in_offset=None).then_inc(m["r_scat"], 16)
            pool.wait_ge(m["r_scat"], 16 * TILES * TOPK)

        @block.tensor
        def _(pe):
            pe.wait_ge(m["r_small"], 48)
            pe.wait_ge(m["r_const"], 10)
            for c in range(HK):
                nc.tensor.transpose(b1_ps[:, c * E_:(c + 1) * E_], b1row[:, c * P:(c + 1) * P], ident[0:E_, 0:E_])
            nc.tensor.matmul(b1_ps[:, D:2 * D], onesf[:], S["vo"][:], start=True, stop=True,
                             skip_group_check=True).then_inc(m["r_b1"], 1)

            def gate_logits(u):
                pe.wait_ge(m["r_xtt"], u + 1)
                for i in range(2):
                    t = 2 * u + i
                    for k in range(DK):
                        ins = nc.tensor.matmul(lg_ps[:, t * E_:(t + 1) * E_], xtt[:, u % 2, (2 * i + k) * P:(2 * i + k + 1) * P],
                                               gate[:, k, :], start=(k == 0), stop=(k == DK - 1), skip_group_check=True)
                ins.then_inc(m["r_lg"], 1)

            for u in range(TILES // 2):
                pe.wait_ge(m["r_x1"], 2 * u + 2)
                if u >= 2:
                    pe.wait_ge(m["r_xtt"], u - 1)
                for i in range(2):
                    for k in range(DK):
                        ins = nc.tensor.transpose(tr_ps[:, u % 2, (2 * i + k) * P:(2 * i + k + 1) * P],
                                                  x1[:, 2 * u + i, k * P:(k + 1) * P], ident[:])
                ins.then_inc(m["r_xtr"], 1)
                if u >= 1:
                    gate_logits(u - 1)
            gate_logits(TILES // 2 - 1)
            pe.wait_ge(m["r_mask"], 1)
            pe.wait_ge(m["r_const"], 7)
            mb = maskb[:].rearrange("p t e -> p (t e)")
            nc.tensor.matmul(pre_ps[:], tri[:], mb, start=True, stop=True)
            nc.tensor.matmul(all_ps[:], ones[:], mb, start=True, stop=True).then_inc(m["r_pre"], 1)
            pe.wait_ge(m["r_g32"], 1)
            for u in range(2):
                for i in range(4):
                    g = 4 * u + i
                    ins = nc.tensor.transpose(tr_ps[:, u, i * P:(i + 1) * P],
                                              g32[:, 4 * g:4 * g + 4, :].rearrange("p t e -> p (t e)"), ident[:])
                ins.then_inc(m["r_gtr"], 1)

        @block.scalar
        def _(act):
            act.wait_ge(m["r_var"], 1)
            nc.scalar.activation(r[0][:], mv[:, :, 1], ACT.Sqrt, bias=eps[:, 0:1]).then_inc(m["r_std"], 1)
            for u in range(TILES // 2):
                act.wait_ge(m["r_xtr"], u + 1)
                if u >= 2:
                    act.wait_ge(m["r_lg"], u - 1)
                nc.scalar.activation(xtt[:, u % 2, :], tr_ps[:, u % 2, :], ACT.Copy).then_inc(m["r_xtt"], 1)
            act.wait_ge(m["r_sub"], 1)
            nc.scalar.activation(prob[:], tmp[:], ACT.Exp).then_inc(m["r_exp"], 1)
            for u in range(2):
                act.wait_ge(m["r_gtr"], u + 1)
                nc.scalar.activation(gT[:, 512 * u:512 * u + 512], tr_ps[:, u, :], ACT.Copy).then_inc(m["r_gt"], 1)

        @block.vector
        def _(dve):
            chain = [0]

            def link(ins):
                chain[0] += 1
                ins.then_inc(m["r_chain"], 1)
                dve.wait_ge(m["r_chain"], chain[0])

            def bc(ap, n):
                return ap.rearrange("p (t a) -> p t a", a=1).broadcast_to([P, ap.shape[1], n])

            def bt(ap, n):
                return ap.rearrange("p (t a) -> p t a", t=1).broadcast_to([P, n, ap.shape[1]])

            V = nc.vector
            V.memset(eps[:], EPS).then_inc(m["r_ln"], 1)
            dve.wait_ge(m["r_small"], 48)
            dve.wait_ge(m["r_b1"], 1)
            V.tensor_copy(b1T[:].rearrange("p c e -> p (c e)"), b1_ps[:, 0:HK * E_])
            link(V.tensor_tensor(bout[:], b1_ps[:, D:2 * D], bout[:], ALU.add))
            for t in range(TILES):
                V.tensor_tensor(x1[:, t, :], x1[:, t, :], bout[:], ALU.add).then_inc(m["r_ln"], 1)
            for t in range(TILES):
                dve.wait_ge(m["r_ln"], t + 2)
                V.bn_stats(stats[:, t, :], x1[:, t, :]).then_inc(m["r_ln"], 1)
            dve.wait_ge(m["r_ln"], 1 + 2 * TILES)
            for t in range(TILES):
                ins = V.bn_aggr(mv[:, t, :], stats[:, t, :])
            ins.then_inc(m["r_var"], 1)
            dve.wait_ge(m["r_std"], 1)
            link(V.reciprocal(r[1][:], r[0][:]))
            link(V.tensor_tensor(r[2][:], r[1][:], r[1][:], ALU.mult))
            link(V.scalar_tensor_tensor(out=r[3][:], in0=mv[:, :, 1], scalar=EPS, in1=r[2][:], op0=ALU.add, op1=ALU.mult))
            link(V.tensor_scalar(r[2][:], r[3][:], -0.5, 1.5, ALU.mult, ALU.add))
            link(V.tensor_tensor(r[0][:], r[1][:], r[2][:], ALU.mult))
            for t in range(TILES):
                V.tensor_scalar(x1[:, t, :], x1[:, t, :], mv[:, t, 0:1], r[0][:, t:t + 1],
                                ALU.subtract, ALU.mult).then_inc(m["r_x1"], 1)
            dve.wait_ge(m["r_lg"], TILES // 2)
            lg = lg_ps[:].rearrange("p (t e) -> p t e", e=E_)
            link(V.tensor_reduce(red[:, 0, :], lg, AX_X, ALU.max))
            V.tensor_tensor(tmp[:], lg, bc(red[:, 0, :], E_), ALU.subtract).then_inc(m["r_sub"], 1)
            dve.wait_ge(m["r_exp"], 1)
            link(V.tensor_reduce(red[:, 0, :], prob[:], AX_X, ALU.add))
            link(V.reciprocal(red[:, 1, :], red[:, 0, :]))
            link(V.tensor_tensor(prob[:], prob[:], bc(red[:, 1, :], E_), ALU.mult))
            for t in range(TILES):
                ins = V.max(top[:, t, :], prob[:, t, :])
            link(ins)
            for t in range(TILES):
                ins = V.max_index(topi[:, t, :], top[:, t, :], prob[:, t, :])
            link(ins)
            dve.wait_ge(m["r_const"], 10)
            link(V.tensor_copy(topf[:], topi[:, :, 0:TOPK].rearrange("p t k -> p k t")))
            for k in range(TOPK):
                ins = V.tensor_tensor(oh[:, k], bt(io16[:], TILES), bc(topf[:, k, :], E_), ALU.is_equal)
            link(ins)
            link(V.tensor_tensor(mask[:], oh[:, 0], oh[:, 1], ALU.add))
            link(V.tensor_tensor(mask[:], mask[:], oh[:, 2], ALU.add))
            V.tensor_copy(maskb[:], mask[:]).then_inc(m["r_mask"], 1)
            link(V.tensor_reduce(red[:, 0, :], top[:, :, 0:TOPK], AX_X, ALU.add))
            link(V.tensor_scalar(red[:, 0, :], red[:, 0, :], 1e-12, None, ALU.max))
            link(V.reciprocal(red[:, 1, :], red[:, 0, :]))
            V.tensor_tensor(wts[:], top[:, :, 0:TOPK], bc(red[:, 1, :], TOPK), ALU.mult)
            link(V.tensor_tensor(tmp[:], prob[:], mask[:], ALU.mult))
            V.tensor_tensor(g32[:, :, 0:E_], tmp[:], bc(red[:, 1, :], E_), ALU.mult).then_inc(m["r_g32"], 1)
            dve.wait_ge(m["r_pre"], 1)
            link(V.tensor_copy(tot[:], all_ps[:].rearrange("p (t e) -> p e t", e=E_)))
            flat = "p e t -> p (e t)"
            link(V.tensor_tensor_scan(inc[:].rearrange(flat), tot[:].rearrange(flat), zero[:], 0.0, ALU.add, ALU.add))
            link(V.tensor_reduce(cnt[:, 0, :], tot[:], AX_X, ALU.add))
            link(V.tensor_scalar(cnt[:, 1, :], cnt[:, 0, :], float(P - 1), None, ALU.add))
            link(V.tensor_copy(cnti[:, 0, :], cnt[:, 1, :]))
            link(V.tensor_scalar(cnti[:, 1, :], cnti[:, 0, :], 7, None, ALU.logical_shift_right))
            link(V.tensor_copy(cnt[:, 2, :], cnti[:, 1, :]))
            link(V.tensor_tensor_scan(cnt[:, 3, :], cnt[:, 2, :], zero[:, 0:E_], 0.0, ALU.add, ALU.add))
            link(V.tensor_tensor(cnt[:, 4, :], cnt[:, 3, :], cnt[:, 2, :], ALU.subtract))
            link(V.tensor_tensor(cnt[:, 5, :], inc[:, :, TILES - 1], cnt[:, 0, :], ALU.subtract))
            link(V.scalar_tensor_tensor(out=cnt[:, 5, :], in0=cnt[:, 4, :], scalar=float(P), in1=cnt[:, 5, :],
                                        op0=ALU.mult, op1=ALU.subtract))
            link(V.tensor_tensor(inc[:], inc[:], tot[:], ALU.subtract))
            link(V.tensor_tensor(inc[:], inc[:], bc(cnt[:, 5, :], TILES), ALU.add))
            link(V.tensor_tensor(slots[:], pre_ps[:].rearrange("p (t e) -> p t e", e=E_),
                                 inc[:].rearrange("p e t -> p t e"), ALU.add))
            for k in range(TOPK):
                link(V.tensor_tensor(tmp[:], slots[:], oh[:, k], ALU.mult))
                link(V.tensor_reduce(slotf[:, k, :], tmp[:], AX_X, ALU.add))
            V.tensor_copy(slot_i[:], slotf[:]).then_inc(m["r_slots"], 1)
            part = SLOT_TILES // 2
            for i in range(2):
                emap = xtt[0:1].rearrange("p a c -> p (a c)")[:, 0:part * E_].rearrange("p (t e) -> p t e", e=E_)
                ts = slice(i * part, (i + 1) * part)
                link(V.tensor_tensor(emap, iot[0:1, ts].rearrange("p (t a) -> p t a", a=1).broadcast_to([1, part, E_]),
                                     cnt[0:1, 3, :].rearrange("p (a e) -> p a e", a=1).broadcast_to([1, part, E_]),
                                     ALU.is_ge))
                link(V.tensor_reduce(ef[:, ts], emap, AX_X, ALU.add))
            link(V.tensor_scalar(ef[:], ef[:], float(E_ - 1), None, ALU.min))
            link(V.tensor_copy(etile[:], ef[:]))


def expert_phase(nc, A, dram, S):
    w1, w2, b1T, etile, ident = S["w1"], S["w2"], S["b1T"], S["etile"], S["ident"]
    with ExitStack() as ctx:
        def sb(name, shape, dt):
            return ctx.enter_context(nc.sbuf_tensor(name, shape, dt))

        def psum(name):
            return ctx.enter_context(nc.psum_tensor(name, [P, 2, 512], F32))

        xin = sb("xin", [P, XIN, D], F32)
        xT = sb("mxT", [P, 2, D], F32)
        h = sb("h", [P, 2, HID], F32)
        hT = sb("hT", [P, 2, HID], F32)
        y = sb("y", [P, 2, D], F32)
        x_ps, h_ps, ht_ps, yo_ps = psum("x_ps"), psum("h_ps"), psum("ht_ps"), psum("yo_ps")
        names = "m_xtr m_xT m_h m_htaken m_htr m_hT m_y m_ytaken".split()
        m = {k: ctx.enter_context(nc.semaphore(k)) for k in names}
        xs_ld = [ctx.enter_context(nc.semaphore(f"xs_ld{s}")) for s in range(XIN)]
        ys_st = [ctx.enter_context(nc.semaphore(f"ys_st{s}")) for s in range(2)]
        block = ctx.enter_context(nc.Block())
        xs = dram["xs"].rearrange("(t p) d -> t p d", p=P)
        ys = dram["ys"].rearrange("(t p) d -> t p d", p=P)
        LOOPS = SLOT_TILES // XIN - 1

        def done(t):
            return t + 3

        def pairs(t):
            return t // 2

        @block.sync
        def _(sp):
            def store(t, s):
                sp.wait_ge(m["m_ytaken"], done(t))
                sp.dma_start(ys[bass.ds(t, 1)].rearrange("a p d -> (a p) d"), y[:, s % 2, :]).then_inc(ys_st[s % 2], 16)

            for s in range(XIN):
                sp.dma_start(xin[:, s, :], xs[s]).then_inc(xs_ld[s], 16)
            with nc.sync.Fori(0, LOOPS) as it:
                for s in range(XIN):
                    t = it * XIN + s
                    sp.wait_ge(m["m_xtr"], done(t))
                    sp.dma_start(xin[:, s, :],
                                 xs[bass.ds(t + XIN, 1)].rearrange("a p d -> (a p) d")).then_inc(xs_ld[s], 16)
                    store(t, s)
            for s in range(XIN):
                store(SLOT_TILES - XIN + s, s)
            for s in range(2):
                sp.wait_ge(ys_st[s], 16 * (SLOT_TILES // 2 + 1))

        @block.tensor
        def _(pe):
            def expert(t):
                return pe.value_load(etile[0:1, bass.ds(t, 1)], min_val=0, max_val=E_ - 1)

            def turn_x(t, s):
                pe.wait_ge(xs_ld[s], 16 * (t // XIN + 1))
                pe.wait_ge(m["m_xT"], done(t - 2))
                for k in range(DK):
                    ins = nc.tensor.transpose(x_ps[:, s % 2, k * P:(k + 1) * P], xin[:, s, k * P:(k + 1) * P],
                                              ident[:])
                ins.then_inc(m["m_xtr"], 1)

            def first_layer(t, s, e):
                pe.wait_ge(m["m_xT"], done(t))
                pe.wait_ge(m["m_htaken"], done(t - 2))
                for k in range(DK):
                    ins = nc.tensor.matmul(h_ps[:, s, :], xT[:, s, k * P:(k + 1) * P],
                                           w1[:, bass.ds(e, 1), k, :].rearrange("p a h -> p (a h)"),
                                           start=(k == 0), stop=(k == DK - 1))
                ins.then_inc(m["m_h"], 1)

            def turn_h(t, s):
                pe.wait_ge(m["m_htaken"], done(t))
                pe.wait_ge(m["m_hT"], done(t - 2))
                for c in range(HK):
                    ins = nc.tensor.transpose(ht_ps[:, s, c * P:(c + 1) * P], h[:, s, c * P:(c + 1) * P], ident[:])
                ins.then_inc(m["m_htr"], 1)

            def second_layer(t, s, e):
                pe.wait_ge(m["m_hT"], done(t))
                pe.wait_ge(m["m_ytaken"], done(t - 2))
                for c in range(HK):
                    ins = nc.tensor.matmul(yo_ps[:, s, 0:D], hT[:, s, c * P:(c + 1) * P],
                                           w2[:, bass.ds(e, 1), c, :].rearrange("p a d -> p (a d)"),
                                           start=(c == 0), stop=(c == HK - 1))
                ins.then_inc(m["m_y"], 1)

            for k in ("m_xtr", "m_h", "m_htr", "m_y"):
                pe.sem_inc(m[k], 2)
            def step(t, s, left=XIN):
                now = expert(t)
                if left > 1:
                    first_layer(t + 1, (s + 1) % 2, expert(t + 1))
                if left > 2:
                    turn_x(t + 2, (s + 2) % XIN)
                second_layer(t, s % 2, now)
                if left > 1:
                    turn_h(t + 1, (s + 1) % 2)

            turn_x(0, 0)
            turn_x(1, 1)
            first_layer(0, 0, expert(0))
            turn_h(0, 0)
            with nc.tensor.Fori(0, LOOPS) as it:
                for s in range(XIN):
                    step(it * XIN + s, s)
            for s in range(XIN):
                step(SLOT_TILES - XIN + s, s, XIN - s)

        @block.scalar
        def _(act):
            def take_x(t, s):
                act.wait_ge(m["m_xtr"], done(t))
                act.wait_ge(m["m_h"], done(t - 2))
                nc.scalar.activation(xT[:, s, :], x_ps[:, s, 0:D], ACT.Copy).then_inc(m["m_xT"], 1)

            def take_h(t, s):
                act.wait_ge(m["m_h"], done(t))
                act.wait_ge(m["m_htr"], done(t - 2))
                nc.scalar.activation(h[:, s, :], h_ps[:, s, :], ACT.Copy).then_inc(m["m_htaken"], 1)

            def take_y(t, s):
                act.wait_ge(m["m_y"], done(t))
                act.wait_ge(ys_st[s], 16 * (pairs(t) + 1))
                nc.scalar.activation(y[:, s, :], yo_ps[:, s, 0:D], ACT.Copy).then_inc(m["m_ytaken"], 1)

            for k in ("m_xT", "m_htaken", "m_ytaken"):
                act.sem_inc(m[k], 2)
            for s in range(2):
                act.sem_inc(ys_st[s], 16)
            def step(t, s, left=XIN):
                if left > 1:
                    take_h(t + 1, (s + 1) % 2)
                if left > 2:
                    take_x(t + 2, s % 2)
                take_y(t, s % 2)

            take_x(0, 0)
            take_x(1, 1)
            take_h(0, 0)
            with nc.scalar.Fori(0, LOOPS) as it:
                for s in range(XIN):
                    step(it * XIN + s, s)
            for s in range(XIN):
                step(SLOT_TILES - XIN + s, s, XIN - s)

        @block.vector
        def _(dve):
            def take_hT(t, s):
                e = dve.value_load(etile[0:1, bass.ds(t, 1)], min_val=0, max_val=E_ - 1)
                dve.wait_ge(m["m_htr"], done(t))
                dve.wait_ge(m["m_y"], done(t - 2))
                for c in range(HK):
                    ins = nc.vector.tensor_scalar(hT[:, s, c * P:(c + 1) * P], ht_ps[:, s, c * P:(c + 1) * P],
                                                  b1T[:, c, bass.ds(e, 1)], 0.0, ALU.add, ALU.max)
                ins.then_inc(m["m_hT"], 1)

            dve.sem_inc(m["m_hT"], 2)
            take_hT(0, 0)
            with nc.vector.Fori(0, LOOPS) as it:
                for s in range(XIN):
                    take_hT(it * XIN + s + 1, (s + 1) % 2)
            for s in range(XIN - 1):
                take_hT(SLOT_TILES - XIN + s + 1, (s + 1) % 2)


def combine_phase(nc, A, dram, S, out):
    x1, slot_i, wts, gT, b2r = S["x1"], S["slot_i"], S["wts"], S["gT"], S["b2r"]
    GROUPS = TILES // GRP
    with ExitStack() as ctx:
        def sb(name, shape, dt):
            return ctx.enter_context(nc.sbuf_tensor(name, shape, dt))

        got = sb("got", [P, 2, GRP * TOPK, D], F32)
        stats = sb("stats2", [P, 2, GRP, 6], F32)
        mv = sb("mv2", [P, 2, GRP, 2], F32)
        r = sb("r2", [P, 2, 4, GRP], F32)
        outb = sb("outb", [P, 2, GRP, D], F32)
        eps = sb("eps2", [P, 1], F32)
        b_ps = ctx.enter_context(nc.psum_tensor("b_ps", [P, GRP, 512], F32))
        names = "c_b2 c_added c_chain c_var c_std c_out".split()
        m = {k: ctx.enter_context(nc.semaphore(k)) for k in names}
        gat = [ctx.enter_context(nc.semaphore(f"gat{s}")) for s in range(2)]
        st = [ctx.enter_context(nc.semaphore(f"st{s}")) for s in range(2)]
        block = ctx.enter_context(nc.Block())
        out_v = out.rearrange("b (g t p) d -> (b g) p t d", p=P, t=GRP)

        @block.gpsimd
        def _(pool):
            for g in range(GROUPS):
                if g >= 2:
                    pool.wait_ge(m["c_added"], g - 1)
                for i in range(GRP):
                    for k in range(TOPK):
                        pool.indirect_dma_start(
                            out=got[:, g % 2, i * TOPK + k, :], out_offset=None, in_=dram["ys"],
                            in_offset=bass.IndirectOffsetOnAxis(ap=slot_i[:, k, g * GRP + i:g * GRP + i + 1], axis=0)
                        ).then_inc(gat[g % 2], 16)

        @block.tensor
        def _(pe):
            for g in range(GROUPS):
                for i in range(GRP):
                    if g >= 1:
                        pe.wait_ge(m["c_added"], g)
                    ins = nc.tensor.matmul(b_ps[:, i, 0:D], gT[32 * i:32 * i + 32, g * P:(g + 1) * P],
                                           b2r[32 * i:32 * i + 32, :], start=True, stop=True)
                ins.then_inc(m["c_b2"], 1)

        @block.scalar
        def _(act):
            for g in range(GROUPS):
                act.wait_ge(m["c_var"], g + 1)
                nc.scalar.activation(r[:, g % 2, 0, :], mv[:, g % 2, :, 1], ACT.Sqrt, bias=eps[:, 0:1])\
                    .then_inc(m["c_std"], 1)

        @block.sync
        def _(sp):
            for g in range(GROUPS):
                sp.wait_ge(m["c_out"], g + 1)
                sp.dma_start(out_v[g], outb[:, g % 2]).then_inc(st[g % 2], 16)
            for s in range(2):
                sp.wait_ge(st[s], 16 * GROUPS // 2)

        @block.vector
        def _(dve):
            chain = [0]
            V = nc.vector

            def link(ins):
                chain[0] += 1
                ins.then_inc(m["c_chain"], 1)
                dve.wait_ge(m["c_chain"], chain[0])

            link(V.memset(eps[:], EPS))
            for g in range(GROUPS):
                s = g % 2
                tiles = [g * GRP + i for i in range(GRP)]
                dve.wait_ge(m["c_b2"], g + 1)
                for i, t in enumerate(tiles):
                    ins = V.tensor_tensor(x1[:, t, :], b_ps[:, i, 0:D], x1[:, t, :], ALU.add)
                link(ins)
                dve.wait_ge(gat[s], 16 * GRP * TOPK * (g // 2 + 1))
                for k in range(TOPK):
                    for i, t in enumerate(tiles):
                        ins = V.scalar_tensor_tensor(out=x1[:, t, :], in0=got[:, s, i * TOPK + k, :],
                                                     scalar=wts[:, t, k:k + 1], in1=x1[:, t, :],
                                                     op0=ALU.mult, op1=ALU.add)
                    if k == TOPK - 1:
                        ins.then_inc(m["c_added"], 1)
                        dve.wait_ge(m["c_added"], g + 1)
                    else:
                        link(ins)
                for i, t in enumerate(tiles):
                    ins = V.bn_stats(stats[:, s, i, :], x1[:, t, :])
                link(ins)
                for i in range(GRP):
                    ins = V.bn_aggr(mv[:, s, i, :], stats[:, s, i, :])
                ins.then_inc(m["c_var"], 1)
                dve.wait_ge(m["c_std"], g + 1)
                rr = [r[:, s, j, :] for j in range(4)]
                link(V.reciprocal(rr[1], rr[0]))
                link(V.tensor_tensor(rr[2], rr[1], rr[1], ALU.mult))
                link(V.scalar_tensor_tensor(out=rr[3], in0=mv[:, s, :, 1], scalar=EPS, in1=rr[2], op0=ALU.add, op1=ALU.mult))
                link(V.tensor_scalar(rr[2], rr[3], -0.5, 1.5, ALU.mult, ALU.add))
                link(V.tensor_tensor(rr[0], rr[1], rr[2], ALU.mult))
                if g >= 2:
                    dve.wait_ge(st[s], 16 * (g // 2))
                for i, t in enumerate(tiles):
                    ins = V.tensor_scalar(outb[:, s, i, :], x1[:, t, :], mv[:, s, i, 0:1], rr[0][:, i:i + 1],
                                          ALU.subtract, ALU.mult)
                ins.then_inc(m["c_out"], 1)


def post_ln_block(nc, A, dram, out):
    with ExitStack() as ctx:
        def sb(name, shape, dt):
            return ctx.enter_context(nc.sbuf_tensor(name, shape, dt))

        S = {"x1": sb("x1", [P, TILES, D], F32), "vo": sb("vo", [P, D], F32)}
        attention_phase(nc, A, dram, S)
        S.update(slot_i=sb("slot_i", [P, TOPK, TILES], I32), wts=sb("wts", [P, TILES, TOPK], F32),
                 gT=sb("gT", [P, 2 * 512], F32), etile=sb("etile", [1, SLOT_TILES], I32),
                 b2r=sb("b2r", [P, D], F32), ident=sb("ident2", [P, P], F32))
        with ExitStack() as inner:
            S["w1"] = inner.enter_context(nc.sbuf_tensor("w1", [P, E_, DK, HID], F32))
            S["w2"] = inner.enter_context(nc.sbuf_tensor("w2", [P, E_, HK, D], F32))
            S["b1T"] = inner.enter_context(nc.sbuf_tensor("b1T", [P, HK, E_], F32))
            routing_phase(nc, A, dram, S)
            expert_phase(nc, A, dram, S)
        combine_phase(nc, A, dram, S, out)


def scratch(nc):
    shapes = {"xsplit": [B, P, 2 * DK * T], "wsplit": [PAIRS + PAIRS // 2, P, 2 * DK * 256], "xs": [SLOTS, D], "ys": [SLOTS, D]}
    return {k: nc.dram_tensor(f"scratch_{k}", v, F32, kind="Internal").ap() for k, v in shapes.items()}


_INS = {'L0_attn_x': 'x', 'L0_attn_W_in': 'W_in', 'L0_attn_b_in': 'b_in', 'L0_attn_W_out': 'W_out',
        'L0_attn_b_out': 'b_out', 'L0_ffn_gate': 'gate', 'L0_ffn_W1': 'W1', 'L0_ffn_b1': 'b1', 'L0_ffn_W2': 'W2',
        'L0_ffn_b2': 'b2'}


def rotary_tables():
    p = np.arange(HALF, dtype=np.float32) / np.float32(HALF - 1)
    thetas = np.float32(10000.0) ** p
    pos = np.arange(T, dtype=np.float32)[:, None] / thetas[None, :]
    scale = np.float32(1.0 / np.sqrt(HD))

    def rows(table):
        return np.ascontiguousarray(np.concatenate([table.T * scale] * 2 + [table.T] * 2, axis=0))

    return rows(np.cos(pos)), rows(np.sin(pos))


def kernel(**inputs):
    import concourse.bacc as _bacc
    from concourse.bass_utils import run_bass_kernel_spmd as _run

    nc = _bacc.Bacc("TRN2", target_bir_lowering=False, num_devices=1)
    arrays, args = {}, {}
    for name, short in _INS.items():
        a = np.ascontiguousarray(inputs[name])
        arrays[f"in_{name}_dram"] = a
        args[short] = nc.dram_tensor(f"in_{name}_dram", a.shape, mybir.dt.from_np(a.dtype), kind="ExternalInput").ap()
    for short, a in zip(("cos", "sin"), rotary_tables()):
        arrays[f"in_{short}_dram"] = a
        args[short] = nc.dram_tensor(f"in_{short}_dram", a.shape, F32, kind="ExternalInput").ap()
    out = nc.dram_tensor("out_0_dram", (B, T, D), F32, kind="ExternalOutput").ap()
    post_ln_block(nc, args, scratch(nc), out)
    r = _run(nc, [arrays], core_ids=[0])
    return r.results[0]["out_0_dram"]
```

```python
from contextlib import ExitStack

import numpy as np

import concourse.bass as bass
from concourse import mybir

ALU = mybir.AluOpType
ACT = mybir.ActivationFunctionType
AX_X = mybir.AxisListType.X
F32 = mybir.dt.float32
F32R = mybir.dt.float32r
BF16 = mybir.dt.bfloat16
I32 = mybir.dt.int32
U32 = mybir.dt.uint32

P = 128
B, T, D = 4, 1024, 256
H, HD = 16, 64
HALF = HD // 2
NTOK = B * T
TILES = NTOK // P
TB = T // P
DK = D // P
PAIRS = H // 2
STEPS = B * PAIRS
CHUNKS = 4
ITERS = STEPS // 2
MASKED = -1.0e30
EPS = 1e-5

def parse(text):
    return [(w.rstrip("+-"), 2 if w[0] in "Frhv" else (w[-1] == "+") - (w[-1] == "-")) for w in text.split()]


S_PER, QK_DMAS = 16, 20
U_PER = 20
T_BANKS = 2
PE_ORDER = parse("""Z3- S6 U00 S7 O3- V00 U01 S8 U10 S9 V01 U11 U12 S10 V10 S11 V11 U13 Y0 V12 S12 V13 U20 U21 S13 Z0 U22 V20
U23 V21 O0 Y1 S14 V22 Z1 S15 O1 U24 F0 U25 U30 V23 U31 F1 V24 U32 U33 V25 V30 F2 Y2 V31 U34 S0+ V32 U35
V33 V34 U36 U37 F3 V35 Z2 V36 S1+ O2 V37 S2+ S3+ Y3 S4+ S5+""")
ACT_ORDER = parse("""u01 u10 E8 E9 u11 N0 u12 E10 E11 u21 N1 z0 E12 u23 E13 z1 E14 u24 E15 u25 u31 h0 u30 N2 h1 v2 u35 u36 u37
E0+ h2 v3 z2 E1+ N3 E2+ E3+ z3 E4+ E5+ E6+ E7+ h3""")
DVE_ORDER = parse("""M4 M5 M6 u00 M7 o3- M8 M9 M10 M11 R0 u13 y0 u20 M12 u22 M13 R1 o0 y1 M14 M15 o1 r0 r1 u32 R2 u33 R3 r2 y2
u34 M0+ r3 M1+ o2 M2+ M3+ y3""")


def events(order, kinds):
    return [(e, ahead) for e, ahead in order if e[0] in kinds]


T_FILLS = events(PE_ORDER, "UYZO")
TAKEN = {"D": events(DVE_ORDER, "uyo"), "A": events(ACT_ORDER, "uz")}
T_NAMES = [e for e, _ in T_FILLS]


def count(order, event, n):
    names = [e for e, _ in order]
    place = names.index(event)
    turn = n - order[place][1]
    if isinstance(n, int):
        return sum(min(max(turn + ahead + (i <= place), 0), STEPS) for i, (_, ahead) in enumerate(order))
    return turn * len(order) + sum(ahead + (i <= place) for i, (_, ahead) in enumerate(order))


def wait_for(engine, semaphore, value, n):
    if not (isinstance(n, int) and n < 0):
        engine.wait_ge(semaphore, value)


def user_before(users, event, turn):
    i = [e for e, _ in users].index(event)
    while True:
        i -= 1
        e, ahead = users[i % len(users)]
        n = turn + i // len(users) + ahead
        if not isinstance(turn, int) or 0 <= n < STEPS:
            return e, n
        if turn + i // len(users) < -2:
            return None


def keys_of(q, j):
    return (128, 1) if j == 2 * q + 1 else (256, 0)


def u_index(q, j):
    return q * (q + 1) + j


def score_banks(event):
    i = int(event[1:])
    if event[0] == "F":
        return ((0, 2), (2, 2), (0, 1), (2, 1))[i]
    return ((0, 2, 1, 3)[i % 4], 1) if i < 8 else (2 * (i % 2), 2)


SCORE_USERS = [[(e, ahead) for e, ahead in events(PE_ORDER, "SF")
                if score_banks(e)[0] <= bank < sum(score_banks(e))] for bank in range(4)]


def attention_phase(nc, A, dram, shared):
    x, W_in, b_in, W_out, cosT, sinT = A["x"], A["W_in"], A["b_in"], A["W_out"], A["cos"], A["sin"]
    xsplit, wsplit, = dram["xsplit"], dram["wsplit"]
    x1, vo = shared["x1"], shared["vo"]
    with ExitStack() as ctx:
        def sb(name, shape, dt):
            return ctx.enter_context(nc.sbuf_tensor(name, shape, dt))

        def sem(name):
            return ctx.enter_context(nc.semaphore(name))

        w_sb = [sb(f"w_sb{s}", [P, 2, DK, 256], F32R) for s in range(2)]
        wv_sb = sb("wv_sb", [P, 2, DK, 256], F32R)
        xT = sb("xT", [P, 2, DK, T], F32R)
        woT = sb("woT", [P, PAIRS, D], F32)
        rot = sb("rot", [P, 2, 512], F32)
        roped = sb("roped", [P, 512], F32)
        hi = sb("hi", [P, 2, T], F32R)
        lo = sb("lo", [P, 2, T], F32R)
        q1 = [[sb(f"q1_{s}{h}", [P, T], F32R) for h in range(2)] for s in range(2)]
        k1 = [[sb(f"k1_{s}{h}", [P, T], F32R) for h in range(2)] for s in range(2)]
        q2 = [sb(f"q2_{s}", [P, T], F32R) for s in range(2)]
        v_sb = sb("v_sb", [P, 2, TB, 2, P], F32)
        prob = [sb("prob0", [P, 2, 2, 768], F32), sb("prob1", [P, 2, 2, 1024], F32)]
        pT = sb("pT", [P, 4, 512], F32)
        cos = sb("cos_sb", [P, T], F32)
        sin = sb("sin_sb", [P, T], F32)
        ych = sb("ych", [P, 2, 256], F32)
        yrow = sb("yrow", [P, 2, 256], F32)
        yT = sb("yT", [P, 2, 256], F32)
        ident = sb("ident", [P, P], F32)
        identb = sb("identb", [P, P], BF16)
        maskb = sb("maskb", [P, P], BF16)
        bias = sb("bias", [P, 3, PAIRS], F32)
        negm = sb("negm", [P, 2, 16], F32)
        den = sb("den", [P, 2, 16], F32)
        rden = sb("rden", [P, 2, 16], F32)

        s_ps = ctx.enter_context(nc.psum_tensor("s_ps", [P, 4, 512], F32))
        t_ps = ctx.enter_context(nc.psum_tensor("t_ps", [P, T_BANKS, 512], F32))
        y_ps = ctx.enter_context(nc.psum_tensor("y_ps", [P, 2, 512], F32))

        names = ("vo_done wv_ld wsp consts w_in tab_in bias_in wo_in setup_tr setup_hi setup_lo wo_tr wo_ev "
                 "x_ld s_fill p_fill t_fill pv_done y_taken max_done exp_done rope_read v_taken "
                 "taken_d taken_a added hi_done lo_done rden_done").split()
        m = {k: sem(k) for k in names}
        xsp = [sem(f"xsp{b}") for b in range(B)]
        x_in = [sem(f"x_in{b}") for b in range(B)]
        w_ld = [sem(f"w_ld{s}") for s in range(2)]
        qk_ld = [sem(f"qk_ld{s}") for s in range(2)]

        w_raw_qk = prob[1][:].rearrange("p a b c -> p (a b c)").rearrange("p (n h d) -> p n h d", n=PAIRS, h=2)
        w_raw_v = prob[0][:].rearrange("p a b c -> p (a b c)")[:, 0:PAIRS * D].rearrange("p (n d) -> p n d", n=PAIRS)
        wo_raw = pT[:].rearrange("p a b -> p (a b)").rearrange("p (r c) -> p r c", r=2)

        X_BATCHES = (0, 1, 3, 2)
        W_UNITS = [u for c in range(PAIRS // 2) for u in (("qk", 2 * c), ("qk", 2 * c + 1), ("v", c))]
        X_UNITS = [(b, k, c) for b in X_BATCHES for k in range(DK) for c in range(2)]
        WO_UNITS = [(r, c) for r in range(2) for c in range(2)]
        NW, NX = len(W_UNITS), len(X_UNITS)
        EARLY = NW + NX // B

        def flat(t):
            return t[:].rearrange("p a k c -> p (a k c)").bitcast(F32)

        stacks = [t for group in (q1[0], k1[0], q1[1], k1[1], [q2[0]]) for t in group]
        w_place, later = [], iter(stacks)
        for what, p in W_UNITS:
            t = wv_sb if (what, p) == ("v", 0) else w_sb[p] if what == "qk" and p < 2 else None
            w_place.append(t[:] if t is not None else
                           next(later)[:].rearrange("p (a k c) -> p a k c", a=2, k=DK))
        prob_flat = [t[:].rearrange("p a b c -> p (a b c)").bitcast(F32R) for t in prob]
        v_flat = v_sb[:, 1].rearrange("p t s c -> p (t s c)").bitcast(F32R)
        x_place = [[[xT[:, a, k, :] for k in range(DK)] for a in range(2)],
                   [[prob_flat[1][:, (2 * a + k) * T:(2 * a + k + 1) * T] for k in range(DK)] for a in range(2)],
                   [[t[:] for t in q1[1]], [t[:] for t in k1[1]]],
                   [[t[:, k * T:(k + 1) * T] for k in range(DK)] for t in (v_flat, prob_flat[0])]]

        def setup_places(u):
            if u < NW:
                return w_place[u][:, 0], w_place[u][:, 1]
            b, k, c = X_UNITS[u - NW]
            return [x_place[b][a][k][:, 512 * c:512 * c + 512] for a in range(2)]

        early_banks = [s_ps[:, i, :] for i in range(4)] + [t_ps[:, i, :] for i in range(2)]
        late_banks = [t_ps[:, i, :] for i in range(2)] + [y_ps[:, i, :] for i in range(2)]

        def setup_bank(u):
            if u < EARLY:
                return early_banks[u % 6]
            return late_banks[(u - EARLY) % 4]

        def turns(engine, turn, order, first, shadow):
            turn(-2, 2, first, shadow)
            for it in (-1, 0, 1):
                turn(it, it % 4, order)
            with engine.Fori(0, STEPS // 4 - 1) as four:
                for i in (2, 3, 4, 5):
                    turn(four * 4 + i, i % 4, order)
            for it in (STEPS - 2, STEPS - 1, STEPS):
                turn(it, it % 4, order)

        def scores(bank, banks):
            return s_ps[:, bank:bank + banks, :].rearrange("p a b -> p (a b)")


        def wait_unit(engine, e, n):
            q, j = int(e[1]), int(e[2])
            w = keys_of(q, j)[0]
            unit = f"U{q}{j}"
            engine.wait_ge(m["t_fill"], count(T_FILLS, unit, n))
            old = U_PER * n + u_index(q, j) - 4
            wait_for(engine, m["pv_done"], old + 1, old)
            return pT[:, u_index(q, j) % 4, 0:2 * w], t_ps[:, T_NAMES.index(unit) % T_BANKS, 0:2 * w]

        block = ctx.enter_context(nc.Block())

        @block.sync
        def _(sp):
            for qk in range(2):
                for hh in range(2):
                    o = 32 * (2 * qk + hh)
                    for f in range(2):
                        src = W_in[qk * 1024:(qk + 1) * 1024, :].rearrange("(n h f d) c -> h f d n c",
                                                                           h=2, f=2, d=HALF)[hh, f]
                        sp.dma_start(w_raw_qk[o:o + 32, :, f, :], src).then_inc(m["w_in"], 16)
            sp.dma_start(w_raw_v, W_in[2048:3072, :].rearrange("(n r) c -> r n c", r=P)).then_inc(m["w_in"], 16)
            xv = x.rearrange("b (t p) d -> p (b t) d", p=P)
            def x_in_dma(b):
                sp.dma_start(x1[:, b * TB:(b + 1) * TB, :], xv[:, b * TB:(b + 1) * TB, :]).then_inc(x_in[b], 16)

            x_in_dma(0)
            x_in_dma(1)
            sp.dma_start(cos[:], cosT).then_inc(m["tab_in"], 16)
            sp.dma_start(sin[:], sinT).then_inc(m["tab_in"], 16)
            for half in range(2):
                for qk in range(2):
                    for hh in range(2):
                        src = b_in[qk * 1024:(qk + 1) * 1024].rearrange("(n h f d) -> f h d n", h=2, f=2, d=HALF)[half, hh]
                        o = 32 * (2 * qk + hh)
                        sp.dma_start(bias[o:o + 32, half, :], src,
                                     allow_slow_non_contiguous=True).then_inc(m["bias_in"], 16)
            sp.dma_start(bias[:, 2, :], b_in[2048:3072].rearrange("(n r) -> r n", r=P),
                         allow_slow_non_contiguous=True).then_inc(m["bias_in"], 16)
            for b in X_BATCHES[2:]:
                x_in_dma(b)
            for t, src in ((shared["bout"], A["b_out"].rearrange("(a d) -> a d", a=1).broadcast_to([P, D])),
                           (shared["gate"], A["gate"].rearrange("(k p) e -> p k e", p=P))):
                sp.dma_start(t[:], src).then_inc(shared["small_in"], 16)
            sp.dma_start(wo_raw, W_out.rearrange("(r p) c -> p r c", p=P)).then_inc(m["wo_in"], 16)
            for i, (what, p) in enumerate(W_UNITS):
                sp.wait_ge(m["setup_hi"], i + 1)
                sp.wait_ge(m["setup_lo"], i + 1)
                sp.dma_start(wsplit[p if what == "qk" else PAIRS + p].rearrange("p (a k c) -> p a k c", a=2, k=DK),
                             w_place[i].bitcast(F32)).then_inc(m["wsp"], 16)
            sp.wait_ge(m["setup_hi"], EARLY)
            sp.wait_ge(m["setup_lo"], EARLY)
            for loaded in (w_ld[0], w_ld[1], m["wv_ld"], m["x_ld"]):
                sp.sem_inc(loaded, 16)
            for i, b in enumerate(X_BATCHES):
                if b > 0:
                    sp.wait_ge(m["setup_hi"], NW + 4 * (i + 1))
                    sp.wait_ge(m["setup_lo"], NW + 4 * (i + 1))
                    dst = xsplit[b].rearrange("p (a k c) -> p a k c", a=2, k=DK)
                    for a in range(2):
                        if b == 2:
                            for k in range(DK):
                                sp.dma_start(dst[:, a, k], x_place[b][a][k].bitcast(F32)).then_inc(xsp[b], 16)
                        else:
                            whole = {1: prob_flat[1][:, 2 * a * T:2 * (a + 1) * T],
                                     3: (v_flat, prob_flat[0][:, 0:2 * T])[a]}[b]
                            sp.dma_start(dst[:, a], whole.rearrange("p (k c) -> p k c", k=DK).bitcast(F32))\
                                .then_inc(xsp[b], 16)
            sp.wait_ge(m["wsp"], 16 * NW)

            def load_w(s, pair):
                sp.dma_start(flat(w_sb[s]), pair).then_inc(w_ld[s], 16)

            def load_wv(pairs):
                sp.dma_start(flat(wv_sb), pairs).then_inc(m["wv_ld"], 16)

            def load_x(batch):
                sp.dma_start(flat(xT), batch).then_inc(m["x_ld"], 16)

            def stack_qk(n, s):
                sp.wait_ge(m["hi_done"], 4 * n + 4)
                sp.wait_ge(m["lo_done"], 4 * n + 4)
                for h in range(2):
                    for f in range(2):
                        q_in, k_in = 32 * h, 64 + 32 * h
                        pos = 32 * f
                        flip = 64 * h
                        for dst, src, i in ((q1[s][h][pos:pos + 32], hi, q_in),
                                            (q1[s][h][64 + pos:96 + pos], hi, q_in),
                                            (q2[s][64 * h + pos:64 * h + pos + 32], lo, q_in),
                                            (k1[s][h][flip + pos:flip + pos + 32], hi, k_in),
                                            (k1[s][h][64 - flip + pos:96 - flip + pos], lo, k_in)):
                            sp.dma_start(dst.bitcast(F32), src[i:i + 32, f, :].bitcast(F32)).then_inc(qk_ld[s], 16)

            def row(table, i):
                return table[bass.ds(i, 1)].rearrange("a p c -> (a p) c")

            def two_steps(n, new_x=None):
                for s in range(2):
                    new = row(wsplit, (n + s + 2) % PAIRS)
                    sp.wait_ge(m["p_fill"], 4 * (n + s) + 2)
                    load_w(s, new)
                    if s == 1:
                        new = row(wsplit, PAIRS + (n // 2 + 1) % (PAIRS // 2))
                        sp.wait_ge(m["p_fill"], 4 * (n + 1) + 4)
                        load_wv(new)
                        if new_x is not None:
                            load_x(new_x)
                    stack_qk(n + s, s)

            with nc.sync.Fori(0, B - 1) as batch:
                with nc.sync.Fori(0, PAIRS // 2 - 1) as it:
                    two_steps(batch * PAIRS + it * 2)
                two_steps(batch * PAIRS + PAIRS - 2, row(xsplit, batch + 1))
            with nc.sync.Fori(0, PAIRS // 2) as it:
                two_steps(it * 2 + (B - 1) * PAIRS)
            for s in range(2):
                sp.wait_ge(w_ld[s], 16 * (STEPS // 2 + 1))
            sp.wait_ge(m["wv_ld"], 16 * (STEPS // 2 + 1))
            sp.wait_ge(m["x_ld"], 16 * B)
            sp.wait_ge(shared["small_in"], 32)

        @block.gpsimd
        def _(pool):
            pool.memset(ident[:], 0.0).then_inc(m["consts"], 1)
            pool.memset(identb[:], 0.0).then_inc(m["consts"], 1)
            pool.memset(maskb[:], 0.0).then_inc(m["consts"], 1)
            pool.wait_ge(m["consts"], 3)
            for t in (ident, identb):
                pool.affine_select(out=t[:], in_=t[:], compare_op=ALU.not_equal, fill=1.0, base=0,
                                   pattern=[[-1, P]], channel_multiplier=1).then_inc(m["consts"], 1)
            pool.affine_select(out=maskb[:], in_=maskb[:], compare_op=ALU.is_ge, fill=MASKED, base=0,
                               pattern=[[-1, P]], channel_multiplier=1).then_inc(m["consts"], 1)

            def rope_part(n, g):
                u = 4 * n + g
                half, cs = g % 2, slice(512 * (g // 2), 512 * (g // 2) + 512)
                pool.wait_ge(m["rope_read"], u + 1)
                if not (isinstance(u, int) and u == 0):
                    pool.wait_ge(m["hi_done"], u)
                    pool.wait_ge(m["lo_done"], u)
                nc.gpsimd.tensor_tensor(roped[:], rot[:, 0, :], rot[:, 1, :],
                                        ALU.subtract if half else ALU.add).then_inc(m["added"], 1)
                pool.wait_ge(m["added"], u + 1)
                pool.wait_ge(m["hi_done"], u + 1)
                nc.gpsimd.tensor_tensor(lo[:, half, cs], roped[:], hi[:, half, cs].bitcast(F32),
                                        ALU.subtract).then_inc(m["lo_done"], 1)

            for g in range(4):
                rope_part(0, g)
            with nc.gpsimd.Fori(1, STEPS) as n:
                for g in range(4):
                    rope_part(n, g)

        @block.tensor
        def _(pe):
            pe.wait_ge(m["consts"], 6)
            def transposes(u, blocks):
                if EARLY > u >= 6 or u >= EARLY + 4:
                    old = u - (6 if u < EARLY else 4)
                    pe.wait_ge(m["setup_hi"], old + 1)
                    pe.wait_ge(m["setup_lo"], old + 1)
                for i, block_ in enumerate(blocks):
                    ins = nc.tensor.transpose(setup_bank(u)[:, i * P:(i + 1) * P], block_, ident[:])
                ins.then_inc(m["setup_tr"], 1)

            def x_transposes(first, end):
                for u in range(first, end):
                    b, k, c = X_UNITS[u]
                    pe.wait_ge(x_in[b], 16)
                    transposes(NW + u, [x1[:, b * TB + 4 * c + i, k * P:(k + 1) * P] for i in range(4)])

            def late_transposes():
                x_transposes(EARLY - NW, NX)
                pe.wait_ge(m["wo_in"], 16)
                for i, (r, c) in enumerate(WO_UNITS):
                    transposes(NW + NX + i, [wo_raw[:, r, (4 * c + j) * P:(4 * c + j + 1) * P] for j in range(4)])
                pe.wait_ge(m["setup_lo"], NW + NX)
                pe.wait_ge(m["wo_ev"], len(WO_UNITS))

            pe.wait_ge(m["w_in"], 16 * 9)
            for u, (what, p) in enumerate(W_UNITS):
                transposes(u, [(w_raw_qk[:, p, half] if what == "qk" else w_raw_v[:, 2 * p + half])[:, k * P:(k + 1) * P]
                               for k in range(DK) for half in range(2)])
            x_transposes(0, EARLY - NW)
            pe.wait_ge(m["setup_hi"], EARLY)
            pe.wait_ge(m["setup_lo"], EARLY)

            def score_fill(s, i):
                h, blk = i % 2, i // 2
                width = (blk + 1) * P
                rows = slice(64 * h, 64 * h + 64)
                bank = score_banks(f"S{i}")[0]
                for c0 in range(0, width, 512):
                    w = min(512, width - c0)
                    out = s_ps[:, bank + c0 // 512, 0:w]
                    last = c0 + w == width
                    qs = slice(blk * P, blk * P + P)
                    nc.tensor.matmul(out, q1[s][h][:, qs], k1[s][h][:, c0:c0 + w], start=True, stop=False,
                                     skip_group_check=True)
                    ins = nc.tensor.matmul(out, q2[s][rows, qs], k1[s][h][rows, c0:c0 + w], start=False,
                                           stop=not last, skip_group_check=True)
                ins = nc.tensor.matmul(out[:, w - P:w], identb[:], maskb[:], start=False, stop=True,
                                       skip_group_check=True)
                ins.then_inc(m["s_fill"], 1)

            PRODUCTS = [(a, b, k) for a, b in ((0, 0), (0, 1), (1, 0)) for k in range(DK)]

            def proj_fill(s, f):
                bank = score_banks(f"F{f}")[0]
                for i in range(2):
                    for a, b, k in PRODUCTS:
                        if f < 2:
                            out = s_ps[:, bank + i, :]
                            left, right = w_sb[s][:, a, k, i * P:(i + 1) * P], xT[:, b, k, 512 * f:512 * f + 512]
                        else:
                            t = 4 * s + 2 * (f - 2) + i
                            out = s_ps[:, bank, i * 256:(i + 1) * 256]
                            left, right = xT[:, b, k, t * P:(t + 1) * P], wv_sb[:, a, k, :]
                        ins = nc.tensor.matmul(out, left, right, start=(a, b, k) == PRODUCTS[0],
                                               stop=(a, b, k) == PRODUCTS[-1], skip_group_check=True)
                ins.then_inc(m["p_fill"], 1)

            def wait_taken(unit, n):
                take = unit[0].lower() + unit[1:]
                by = "D" if take in [e for e, _ in TAKEN["D"]] else "A"
                pe.wait_ge(m["taken_d" if by == "D" else "taken_a"], count(TAKEN[by], take, n))

            def wait_score_banks(event, turn):
                first, banks = score_banks(event)
                had = []
                for users in SCORE_USERS[first:first + banks]:
                    user = user_before(users, event, turn)
                    if user and user[0] not in had:
                        had.append(user[0])
                        e, n = user
                        i = int(e[1:])
                        if e[0] == "S":
                            pe.wait_ge(m["exp_done"], S_PER * n + i + 1)
                        elif i < 2:
                            pe.wait_ge(m["rope_read"], 4 * n + 2 * i + 2)
                        else:
                            pe.wait_ge(m["v_taken"], 2 * n + i - 1)

            def turn(it, phase, order, shadow={}):
                for e, ahead in order:
                    n, s, pairs = it + ahead, (phase + ahead) % 2, (phase + ahead) // 2 % 2
                    if isinstance(n, int) and not 0 <= n < STEPS:
                        continue
                    kind, q = e[0], int(e[1])
                    if kind in "SF":
                        wait_score_banks(e, it)
                    if kind in "UYZO":
                        u = T_NAMES.index(e)
                        old = user_before(T_FILLS[u % T_BANKS::T_BANKS], e, it)
                        if old:
                            wait_taken(*old)
                        bank = t_ps[:, u % T_BANKS, :]
                    if kind == "S":
                        if e == "S0":
                            pe.wait_ge(qk_ld[s], 16 * QK_DMAS * (n // 2 + 1))
                        score_fill(s, int(e[1:]))
                    elif kind == "F":
                        first = isinstance(n, int) and n < 2
                        if q == 0 and not first:
                            pe.wait_ge(w_ld[s], 16 * (n // 2 + 1))
                            pe.wait_ge(m["x_ld"], 16 * (n // PAIRS + 1))
                        if q == 2 and s == 0 and not first:
                            pe.wait_ge(m["wv_ld"], 16 * (n // 2 + 1))
                        proj_fill(s, q)
                    elif kind == "U":
                        j = int(e[2])
                        w, first = keys_of(q, j)
                        pe.wait_ge(m["exp_done"], S_PER * n + 4 * q + 4)
                        for h in range(2):
                            for ii in range(first, 2):
                                o = h * w + (ii - first) * P
                                ins = nc.tensor.transpose(bank[:, o:o + P], prob[q % 2][:, h, ii, j * P:(j + 1) * P],
                                                          ident[:])
                        ins.then_inc(m["t_fill"], 1)
                    elif kind == "V":
                        j = int(e[2])
                        w, first = keys_of(q, j)
                        if j == 0:
                            old = 4 * n + q - 2
                            wait_for(pe, m["y_taken"], old + 1, old)
                        if j % 2 == 0:
                            pe.wait_ge(m["v_taken"], 2 * (n - s + j // 4) + j // 2 % 2 + 1)
                        wait_taken(f"U{q}{j}", n)
                        for h in range(2):
                            ins = nc.tensor.matmul(y_ps[64 * h:64 * h + 64, q % 2, 256 - w:256],
                                                   v_sb[:, pairs, j, s, 64 * h:64 * h + 64],
                                                   pT[:, u_index(q, j) % 4, h * w:(h + 1) * w],
                                                   start=(j == 0), stop=(j == 2 * q + 1), skip_group_check=True)
                        ins.then_inc(m["pv_done"], 1)
                    elif kind == "Y":
                        pe.wait_ge(m["y_taken"], 4 * n + q + 1)
                        for ii in range(2):
                            ins = nc.tensor.transpose(bank[:, ii * P:(ii + 1) * P], ych[:, q % 2, ii * P:(ii + 1) * P],
                                                      ident[:])
                        ins.then_inc(m["t_fill"], 1)
                    elif kind == "Z":
                        wait_taken(f"Y{q}", n)
                        for ii in range(2):
                            ins = nc.tensor.transpose(bank[:, ii * P:(ii + 1) * P], yrow[:, q % 2, ii * P:(ii + 1) * P],
                                                      ident[:])
                        ins.then_inc(m["t_fill"], 1)
                    elif kind == "O":
                        wait_taken(f"Z{q}", n)
                        for ii in range(2):
                            ins = nc.tensor.matmul(bank[:, ii * D:(ii + 1) * D], yT[:, q % 2, ii * P:(ii + 1) * P],
                                                   woT[:, bass.ds(n % PAIRS, 1), :].rearrange("p a c -> p (a c)"),
                                                   start=True, stop=True, skip_group_check=True)
                        ins.then_inc(m["t_fill"], 1)
                    if e in shadow:
                        shadow[e]()

            turns(nc.tensor, turn, PE_ORDER, PE_ORDER, {"F1": late_transposes})

        @block.scalar
        def _(act):
            def high_halves(first, end):
                for u in range(first, end):
                    act.wait_ge(m["setup_tr"], u + 1)
                    if u >= NW and X_UNITS[u - NW] == (2, 0, 0):
                        act.wait_ge(m["wsp"], 16 * NW)
                    src = setup_bank(u)
                    if u < NW:
                        src = src.rearrange("p (k c) -> p k c", k=DK)
                    nc.scalar.activation(setup_places(u)[0], src, ACT.Copy).then_inc(m["setup_hi"], 1)

            def finish_high_halves():
                high_halves(EARLY + 10, NW + NX)
                for i, (r, c) in enumerate(WO_UNITS):
                    act.wait_ge(m["setup_tr"], NW + NX + i + 1)
                    nc.scalar.activation(woT[:, 4 * c:4 * c + 4, r * P:(r + 1) * P],
                                         setup_bank(NW + NX + i).rearrange("p (j c) -> p j c", j=4),
                                         ACT.Copy).then_inc(m["wo_ev"], 1)
                act.wait_ge(xsp[2], 64)
                act.wait_ge(xsp[1], 32)
                act.wait_ge(xsp[3], 32)

            high_halves(0, EARLY)

            def turn(it, phase, order, shadow={}):
                for e, ahead in order:
                    n, s, pairs = it + ahead, (phase + ahead) % 2, (phase + ahead) // 2 % 2
                    if isinstance(n, int) and not 0 <= n < STEPS:
                        continue
                    kind, q = e[0], int(e[1])
                    if kind == "E":
                        i = int(e[1:])
                        h, blk = i % 2, i // 2
                        q = blk // 2
                        w = (blk + 1) * P
                        bank, banks = score_banks(f"S{i}")
                        act.wait_ge(m["max_done"], S_PER * n + i + 1)
                        if i % 4 == 0:
                            c, old = (q - 2, n) if q >= 2 else (q + 2, n - 1)
                            wait_for(act, m["t_fill"], count(T_FILLS, f"U{c}{2 * c + 1}", old), old)
                        nc.scalar.activation(prob[q % 2][:, h, blk % 2, 0:w], scores(bank, banks)[:, 0:w], ACT.Exp,
                                             bias=negm[:, s, i:i + 1], scale=1.0,
                                             accum_out=den[:, s, i:i + 1]).then_inc(m["exp_done"], 1)
                    elif kind == "h":
                        act.wait_ge(m["added"], 4 * n + q + 1)
                        if q == 0:
                            wait_for(act, qk_ld[1 - s], 16 * QK_DMAS * ((n - 1) // 2 + 1), n - 1)
                        nc.scalar.activation(hi[:, q % 2, 512 * (q // 2):512 * (q // 2) + 512], roped[:],
                                             ACT.Copy).then_inc(m["hi_done"], 1)
                    elif kind == "v":
                        act.wait_ge(m["p_fill"], 4 * n + q + 1)
                        old = n - 3 - s
                        wait_for(act, m["pv_done"], U_PER * (old + 1), old)
                        t, bank = 4 * s + 2 * (q - 2), score_banks(f"F{q}")[0]
                        nc.scalar.activation(v_sb[:, pairs, t:t + 2].rearrange("p t s c -> p (t s c)"), s_ps[:, bank, :], ACT.Copy)\
                            .then_inc(m["v_taken"], 1)
                    elif kind == "N":
                        act.wait_ge(m["pv_done"], U_PER * n + u_index(q, 2 * q + 1) + 1)
                        c, old = (q - 2, n) if q >= 2 else (q + 2, n - 1)
                        wait_for(act, m["t_fill"], count(T_FILLS, f"Y{c}", old), old)
                        nc.scalar.activation(ych[:, q % 2, :], y_ps[:, q % 2, 0:256], ACT.Copy)\
                            .then_inc(m["y_taken"], 1)
                    elif kind == "u":
                        dst, src = wait_unit(act, e, n)
                        nc.scalar.activation(dst, src, ACT.Copy).then_inc(m["taken_a"], 1)
                    elif kind == "z":
                        act.wait_ge(m["t_fill"], count(T_FILLS, f"Z{q}", n))
                        c, old = (q - 2, n) if q >= 2 else (q + 2, n - 1)
                        wait_for(act, m["t_fill"], count(T_FILLS, f"O{c}", old), old)
                        nc.scalar.activation(yT[:, q % 2, :], t_ps[:, T_NAMES.index(f"Z{q}") % T_BANKS, 0:256],
                                             ACT.Copy).then_inc(m["taken_a"], 1)
                    if e in shadow:
                        shadow[e]()

            turns(nc.scalar, turn, ACT_ORDER, parse("h0 h1 h2 h3 v2 v3"), {
                "h0": lambda: high_halves(EARLY, EARLY + 3), "h1": lambda: high_halves(EARLY + 3, EARLY + 7),
                "h2": lambda: high_halves(EARLY + 7, EARLY + 10), "h3": finish_high_halves})

        @block.vector
        def _(dve):
            def low_halves(first, end):
                for u in range(first, end):
                    hi_part, lo_part = setup_places(u)
                    src = setup_bank(u)
                    if u < NW:
                        src = src.rearrange("p (k c) -> p k c", k=DK)
                    dve.wait_ge(m["setup_hi"], u + 1)
                    nc.vector.tensor_tensor(lo_part, src, hi_part.bitcast(F32), ALU.subtract)\
                        .then_inc(m["setup_lo"], 1)

            def turn(it, phase, order, shadow={}):
                for e, ahead in order:
                    n, s, pairs = it + ahead, (phase + ahead) % 2, (phase + ahead) // 2 % 2
                    if isinstance(n, int) and not 0 <= n < STEPS:
                        continue
                    kind, q = e[0], int(e[1])
                    if kind == "M":
                        i = int(e[1:])
                        w = (i // 2 + 1) * P
                        dve.wait_ge(m["s_fill"], S_PER * n + i + 1)
                        nc.vector.tensor_reduce(negm[:, s, i:i + 1], scores(*score_banks(f"S{i}"))[:, 0:w], AX_X,
                                                ALU.max, negate=True).then_inc(m["max_done"], 1)
                    elif kind == "r":
                        half, c = q % 2, q // 2
                        dve.wait_ge(m["p_fill"], 4 * n + c + 1)
                        wait_for(dve, m["added"], 4 * n + q, 4 * n + q - 1)
                        cs = slice(512 * c, 512 * c + 512)
                        for k, (src, tab) in enumerate(((1, cos), (0, sin)) if half == 0 else ((0, cos), (1, sin))):
                            ins = nc.vector.scalar_tensor_tensor(out=rot[:, k, :], in0=s_ps[:, 2 * c + src, :],
                                                                 scalar=bias[:, src, bass.ds(n % PAIRS, 1)],
                                                                 in1=tab[:, cs], op0=ALU.add, op1=ALU.mult)
                        ins.then_inc(m["rope_read"], 1)
                    elif kind == "R":
                        dve.wait_ge(m["exp_done"], S_PER * n + 4 * q + 4)
                        nc.vector.reciprocal(rden[:, s, 4 * q:4 * q + 4], den[:, s, 4 * q:4 * q + 4])\
                            .then_inc(m["rden_done"], 1)
                    elif kind == "u":
                        dst, src = wait_unit(dve, e, n)
                        nc.vector.tensor_copy(dst, src).then_inc(m["taken_d"], 1)
                    elif kind == "y":
                        dve.wait_ge(m["t_fill"], count(T_FILLS, f"Y{q}", n))
                        dve.wait_ge(m["rden_done"], 4 * n + q + 1)
                        c, old = (q - 2, n) if q >= 2 else (q + 2, n - 1)
                        wait_for(dve, m["t_fill"], count(T_FILLS, f"Z{c}", old), old)
                        bank = t_ps[:, T_NAMES.index(f"Y{q}") % T_BANKS, :]
                        nc.vector.tensor_tensor(
                            yrow[:, q % 2, :].rearrange("p (g d) -> p g d", g=4),
                            bank[:, 0:256].rearrange("p (g d) -> p g d", g=4),
                            rden[:, s, 4 * q:4 * q + 4].rearrange("p (g a) -> p g a", a=1).broadcast_to([P, 4, HD]),
                            ALU.mult).then_inc(m["taken_d"], 1)
                    elif kind == "o":
                        dve.wait_ge(m["t_fill"], count(T_FILLS, f"O{q}", n))
                        wait_for(dve, m["taken_d"], count(TAKEN["D"], e, n - 1), n - 1)
                        acc = x1[:, bass.ds((n // PAIRS) * TB + 2 * q, 2), :].rearrange("p t d -> p (t d)")
                        nc.vector.tensor_tensor(acc, t_ps[:, T_NAMES.index(f"O{q}") % T_BANKS, :], acc,
                                                ALU.add).then_inc(m["taken_d"], 1)
                    if e in shadow:
                        shadow[e]()

            def v_bias():
                dve.wait_ge(m["wo_ev"], 4)
                nc.vector.tensor_scalar(vo[:], woT[:, 0, :], bias[:, 2, 0:1], None, ALU.mult).then_inc(m["vo_done"], 1)
                for p in range(1, PAIRS):
                    dve.wait_ge(m["vo_done"], p)
                    nc.vector.scalar_tensor_tensor(out=vo[:], in0=woT[:, p, :], scalar=bias[:, 2, p:p + 1], in1=vo[:],
                                                   op0=ALU.mult, op1=ALU.add).then_inc(m["vo_done"], 1)

            low_halves(0, EARLY)
            dve.wait_ge(m["tab_in"], 32)
            dve.wait_ge(m["bias_in"], 16 * 9)
            turns(nc.vector, turn, DVE_ORDER, DVE_ORDER, {
                "r0": lambda: low_halves(EARLY, EARLY + 3), "r1": lambda: low_halves(EARLY + 3, EARLY + 7),
                "r2": lambda: low_halves(EARLY + 7, EARLY + 10),
                "r3": lambda: (low_halves(EARLY + 10, NW + NX), v_bias())})

E_, TOPK, HID = 16, 3, 512
HK = HID // P
XIN = 4
SLOT_TILES = (NTOK * TOPK + E_ * (P - 1)) // P
SLOT_TILES += -SLOT_TILES % XIN

GRP = 4
PLACES = 4


def routing_phase(nc, A, dram, S):
    bout, gate = S["bout"], S["gate"]
    x1, w1, w2, b1T = S["x1"], S["w1"], S["w2"], S["b1T"]
    src_i, dst_i, wts, gT, etile, b2r, ident = (S[k] for k in "src_i dst_i wts gT etile b2r ident".split())
    with ExitStack() as ctx:
        def sb(name, shape, dt):
            return ctx.enter_context(nc.sbuf_tensor(name, shape, dt))

        b1row = sb("b1row", [E_, HID], F32)
        tri = sb("tri", [P, P], BF16)
        ones = sb("ones", [P, P], BF16)
        onesf = sb("onesf", [P, P], F32)
        stats = sb("stats", [P, TILES, 6], F32)
        mv = sb("mv", [P, TILES, 2], F32)
        r = [sb(f"ln_{i}", [P, TILES], F32) for i in range(5)]
        EARLY_BIASES = 10
        HOT = 8
        LG = 8
        BY_POOL = 5
        xtt = sb("xtt", [P, 2, 512], F32)
        prob = sb("gprob", [P, TILES, E_], F32)
        tmp = sb("gtmp", [P, TILES, E_], F32)
        red = sb("red", [P, 2, TILES], F32)
        top = sb("top", [P, TILES, 8], F32)
        topi = sb("topi", [P, TILES, 8], U32)
        topf = sb("topf", [P, TOPK, TILES], F32)
        io16 = sb("io16", [P, E_], F32)
        iot = sb("iot", [P, SLOT_TILES], F32)
        oh = sb("oh", [P, TOPK, TILES, E_], F32)
        hot = oh[:].rearrange("p k t e -> p (k t e)")
        hot = hot.bitcast(BF16)
        row_hot = hot[:, 0:HOT * P].rearrange("p (i c) -> p i c", i=HOT)
        row_hot_k = hot[:, HOT * P:2 * HOT * P].rearrange("p (i c) -> p i c", i=HOT)
        tile_hot = hot[:, 2 * HOT * P:HOT * (2 * P + SLOT_TILES)].rearrange("p (i c) -> p i c", i=HOT)
        mask = sb("gmask", [P, TILES, E_], F32)
        maskb = sb("gmaskb", [P, TILES, E_], BF16)
        tot = sb("tot", [P, E_, TILES], F32)
        back = tot[:].rearrange("p e t -> p (e t)")[:, 0:2 * SLOT_TILES].rearrange("p (i c) -> p i c", i=2)
        inc = sb("inc", [P, E_, TILES], F32)
        zero = sb("gzero", [P, E_ * TILES], F32)
        cnt = sb("cnt", [P, 6, E_], F32)
        cnti = sb("cnti", [P, 2, E_], I32)
        slots = sb("slots", [P, TILES, E_], F32)
        slotf = sb("slotf", [P, TOPK, TILES], F32)
        sloti = sb("sloti", [P, 3, TOPK, TILES], I32)
        row_of = sb("row_of", [P, TOPK, TILES], F32)
        tile_of = sb("tile_of", [P, TOPK, TILES], F32)
        part = sb("part", [P, 1], F32)
        unused = sb("unused", [P, SLOT_TILES], F32)
        ioq = sb("ioq", [P, P], BF16)
        biases = xtt[:, :, 0:D]
        g32 = xtt[:].rearrange("p a (t e) -> p (a t) e", e=32)
        ef = sb("ef", [1, SLOT_TILES], F32)
        eps = sb("eps", [P, 1], F32)

        tr_ps = ctx.enter_context(nc.psum_tensor("tr_ps", [P, 2, 512], F32))
        lg_ps = ctx.enter_context(nc.psum_tensor("lg_ps", [P, 512], F32))
        b1_ps = ctx.enter_context(nc.psum_tensor("b1_ps", [P, 512], F32))
        pre_ps = ctx.enter_context(nc.psum_tensor("pre_ps", [P, 512], F32))
        all_ps = ctx.enter_context(nc.psum_tensor("all_ps", [P, 512], F32))
        lt_ps = [all_ps, pre_ps]
        lt_sb = [tmp[:].rearrange("p t e -> p (t e)"), prob[:].rearrange("p t e -> p (t e)")]
        inv_ps = ctx.enter_context(nc.psum_tensor("inv_ps", [P, 512], F32))
        bb_ps = ctx.enter_context(nc.psum_tensor("bb_ps", [P, 512], F32))
        names = ("r_slots r_ef r_oh r_oh_a r_oh_k r_bb_sb r_inv r_stored r_bb r_bbadd r_w r_small r_const r_chain r_ln r_var r_std r_x1 r_xtr r_xtt r_lg r_lt r_lgt r_vo r_b1 r_bout r_bias_p r_bias_v r_rs r_sub r_exp r_mask "
                 "r_pre r_g32 r_gtr r_gt r_b2z r_b2").split()
        m = {k: ctx.enter_context(nc.semaphore(k)) for k in names}
        block = ctx.enter_context(nc.Block())

        @block.sync
        def _(sp):
            sp.dma_start(b1row[:], A["b1"]).then_inc(m["r_small"], 16)
            sp.wait_ge(m["r_b2z"], 1)
            for i in range(4):
                sp.dma_start(b2r[32 * i:32 * i + E_, :], A["b2"]).then_inc(m["r_b2"], 16)
            for e in range(E_):
                sp.dma_start(w1[:, e], A["W1"][e].rearrange("(k p) h -> p k h", p=P)).then_inc(m["r_w"], 16)
                sp.dma_start(w2[:, e], A["W2"][e].rearrange("(k p) d -> p k d", p=P)).then_inc(m["r_w"], 16)
            xn = dram["xn"].rearrange("(t p) d -> p t d", p=P)
            for g in range(0, TILES, LG):
                sp.wait_ge(m["r_x1"], g + LG)
                sp.dma_start(xn[:, g:g + LG, :], x1[:, g:g + LG, :]).then_inc(m["r_stored"], 16)
            sp.wait_ge(m["r_stored"], 16 * TILES // LG)
            sp.wait_ge(m["r_b2"], 64)
            sp.wait_ge(m["r_w"], 32 * E_)

        @block.gpsimd
        def _(pool):
            pool.memset(b2r[:], 0.0).then_inc(m["r_b2z"], 1)
            pool.memset(tri[:], 1.0).then_inc(m["r_const"], 1)
            pool.memset(ones[:], 1.0).then_inc(m["r_const"], 1)
            pool.memset(zero[:], 0.0).then_inc(m["r_const"], 1)
            pool.iota(io16[:], pattern=[[1, E_]], base=0, channel_multiplier=0,
                      allow_small_or_imprecise_dtypes=True).then_inc(m["r_const"], 1)
            pool.iota(iot[:], pattern=[[1, SLOT_TILES]], base=0, channel_multiplier=0,
                      allow_small_or_imprecise_dtypes=True).then_inc(m["r_const"], 1)
            pool.memset(onesf[:], 1.0).then_inc(m["r_const"], 1)
            pool.memset(ident[:], 0.0).then_inc(m["r_const"], 1)
            for t, pattern, base, mult in ((ioq, [[1, P]], 0, 0), (unused, [[P, SLOT_TILES]], PLACES * NTOK + P, 1),
                                           (part, [[0, 1]], 1, 1)):
                pool.iota(t[:], pattern=pattern, base=base, channel_multiplier=mult,
                          allow_small_or_imprecise_dtypes=True).then_inc(m["r_const"], 1)
            pool.wait_ge(m["r_const"], 10)
            pool.affine_select(out=ident[:], in_=ident[:], compare_op=ALU.not_equal, fill=1.0, base=0,
                               pattern=[[-1, P]], channel_multiplier=1).then_inc(m["r_const"], 1)
            pool.affine_select(out=tri[:], in_=tri[:], compare_op=ALU.is_gt, fill=0.0, base=0,
                               pattern=[[1, P]], channel_multiplier=-1).then_inc(m["r_const"], 1)
            pool.wait_ge(m["r_bout"], 1)
            for g in range(0, TILES, LG):
                for t in range(g, g + BY_POOL):
                    nc.gpsimd.tensor_tensor(x1[:, t, :], x1[:, t, :], bout[:], ALU.add).then_inc(m["r_bias_p"], 1)
            pool.wait_ge(m["r_stored"], 16 * TILES // LG)
            for t in range(TILES):
                pool.wait_ge(m["r_bb_sb"], t + 1)
                nc.gpsimd.tensor_tensor(x1[:, t, :], biases[:, t % 2, :], x1[:, t, :], ALU.add)\
                    .then_inc(m["r_bbadd"], 1)

        @block.tensor
        def _(pe):
            pe.wait_ge(m["r_const"], 12)
            nc.tensor.matmul(all_ps[:, 0:D], onesf[:], S["vo"][:], start=True, stop=True).then_inc(m["r_vo"], 1)
            pe.wait_ge(m["r_small"], 16)
            for c in range(HK):
                ins = nc.tensor.transpose(b1_ps[:, c * E_:(c + 1) * E_], b1row[:, c * P:(c + 1) * P],
                                          ident[0:E_, 0:E_])
            ins.then_inc(m["r_b1"], 1)

            def gate_logits(u):
                pe.wait_ge(m["r_xtt"], u + 1)
                if u >= 4 and u % 2 == 0:
                    pe.wait_ge(m["r_lt"], u // 2 - 1)
                x_cols = xtt[:, u % 2, :].rearrange("p (i k c) -> p i k c", i=2, k=DK)
                for k in range(DK):
                    ins = nc.tensor.matmul(lt_ps[u // 2 % 2][0:E_, (u % 2) * 256:(u % 2) * 256 + 256], gate[:, k, :],
                                           x_cols[:, :, k, :], start=(k == 0), stop=(k == DK - 1),
                                           skip_group_check=True)
                ins.then_inc(m["r_lg"], 1)

            def turn_logits(v):
                pe.wait_ge(m["r_lt"], v + 1)
                for i in range(4):
                    ins = nc.tensor.transpose(lg_ps[:, (4 * v + i) * E_:(4 * v + i + 1) * E_],
                                              lt_sb[v % 2][0:E_, i * P:(i + 1) * P], ident[0:E_, 0:E_])
                ins.then_inc(m["r_lgt"], 1)

            pe.wait_ge(m["r_bout"], 1)
            UNITS = TILES // 2
            for u in range(UNITS):
                pe.wait_ge(m["r_x1"], 2 * u + 2)
                if u >= 2:
                    pe.wait_ge(m["r_xtt"], u - 1)
                for i in range(2):
                    for k in range(DK):
                        ins = nc.tensor.transpose(tr_ps[:, u % 2, (2 * i + k) * P:(2 * i + k + 1) * P],
                                                  x1[:, 2 * u + i, k * P:(k + 1) * P], ident[:])
                ins.then_inc(m["r_xtr"], 1)
                if u >= 1:
                    gate_logits(u - 1)
                if u >= 4 and u % 2 == 0:
                    turn_logits(u // 2 - 2)
            gate_logits(UNITS - 1)
            turn_logits(UNITS // 2 - 2)
            turn_logits(UNITS // 2 - 1)
            pe.wait_ge(m["r_mask"], 1)
            pe.wait_ge(m["r_const"], 7)
            mb = maskb[:].rearrange("p t e -> p (t e)")
            nc.tensor.matmul(pre_ps[:], tri[:], mb, start=True, stop=True)
            nc.tensor.matmul(all_ps[:], ones[:], mb, start=True, stop=True).then_inc(m["r_pre"], 1)
            pe.wait_ge(m["r_g32"], 1)
            for u in range(2):
                for i in range(4):
                    g = 4 * u + i
                    ins = nc.tensor.transpose(tr_ps[:, u, i * P:(i + 1) * P],
                                              xtt[:, u, i * P:(i + 1) * P], ident[:])
                ins.then_inc(m["r_gtr"], 1)
            def weighted_biases(t):
                if t >= 2:
                    pe.wait_ge(m["r_bb_sb"], t - 1)
                r0 = 32 * (t % 4)
                nc.tensor.matmul((lg_ps, bb_ps)[t % 2][:, 0:D], gT[r0:r0 + 32, (t // 4) * P:(t // 4 + 1) * P],
                                 b2r[r0:r0 + 32, :], start=True, stop=True).then_inc(m["r_bb"], 1)

            pe.wait_ge(m["r_gt"], 2)
            pe.wait_ge(m["r_b2"], 64)
            for t in range(EARLY_BIASES):
                weighted_biases(t)
            last = TOPK * TILES - 1
            for i in range(last + 1):
                pe.wait_ge(m["r_oh"], i + 1)
                nc.tensor.matmul(inv_ps[:, 0:SLOT_TILES], row_hot[:, i % HOT, :], tile_hot[:, i % HOT, :],
                                 start=(i == 0), stop=(i == last), skip_group_check=True)
                pe.wait_ge(m["r_oh_k"], i + 1)
                nc.tensor.matmul(tr_ps[:, 0, 0:SLOT_TILES], row_hot_k[:, i % HOT, :],
                                 tile_hot[:, i % HOT, :], start=(i == 0), stop=(i == last),
                                 skip_group_check=True).then_inc(m["r_inv"], 1)
                if i % 4 == 0 and EARLY_BIASES + i // 4 < TILES:
                    weighted_biases(EARLY_BIASES + i // 4)

        @block.scalar
        def _(act):
            def take_logits(v):
                act.wait_ge(m["r_lg"], 2 * v + 2)
                if v >= 2:
                    act.wait_ge(m["r_lgt"], v - 1)
                nc.scalar.activation(lt_sb[v % 2][0:E_, :], lt_ps[v % 2][0:E_, :], ACT.Copy).then_inc(m["r_lt"], 1)

            def take_transposes(u):
                act.wait_ge(m["r_xtr"], u + 1)
                if u >= 2:
                    act.wait_ge(m["r_lg"], u - 1)
                nc.scalar.activation(xtt[:, u % 2, :], tr_ps[:, u % 2, :], ACT.Copy).then_inc(m["r_xtt"], 1)
                if u >= 2 and u % 2 == 0:
                    take_logits(u // 2 - 1)

            for g in range(TILES // LG):
                ts = slice(g * LG, (g + 1) * LG)
                act.wait_ge(m["r_var"], g + 1)
                nc.scalar.activation(r[0][:, ts], mv[:, ts, 1], ACT.Sqrt, bias=eps[:, 0:1]).then_inc(m["r_std"], 1)
                act.wait_ge(m["r_rs"], g + 1)
                for t in range(g * LG, (g + 1) * LG):
                    nc.scalar.activation(x1[:, t, :], x1[:, t, :], ACT.Identity, bias=r[4][:, t:t + 1],
                                         scale=r[3][:, t:t + 1]).then_inc(m["r_x1"], 1)
                    if g >= 1 and t % 2 == 1:
                        take_transposes((t - LG) // 2)
            for u in range((TILES - LG) // 2, TILES // 2):
                take_transposes(u)
            take_logits(TILES // 4 - 1)
            act.wait_ge(m["r_sub"], 1)
            nc.scalar.activation(prob[:], tmp[:], ACT.Exp).then_inc(m["r_exp"], 1)
            for u in range(2):
                act.wait_ge(m["r_gtr"], u + 1)
                nc.scalar.activation(gT[:, 512 * u:512 * u + 512], tr_ps[:, u, :], ACT.Copy).then_inc(m["r_gt"], 1)
            def take_biases(t):
                act.wait_ge(m["r_bb"], t + 1)
                if t >= 2:
                    act.wait_ge(m["r_bbadd"], t - 1)
                nc.scalar.activation(biases[:, t % 2, :], (lg_ps, bb_ps)[t % 2][:, 0:D], ACT.Copy)\
                    .then_inc(m["r_bb_sb"], 1)

            for t in range(EARLY_BIASES):
                take_biases(t)
            for i in range(TOPK * TILES):
                t, k = i // TOPK, i % TOPK
                act.wait_ge(m["r_oh_a"], i + 1)
                if i >= HOT:
                    act.wait_ge(m["r_inv"], i - HOT + 1)
                nc.scalar.activation(row_hot_k[:, i % HOT, :], row_hot[:, i % HOT, :], ACT.Copy,
                                     scale=float(PLACES * t + k + 1)).then_inc(m["r_oh_k"], 1)
                if i % 4 == 3 and EARLY_BIASES + i // 4 < TILES:
                    take_biases(EARLY_BIASES + i // 4)

        @block.vector
        def _(dve):
            chain = [0]

            def link(ins):
                chain[0] += 1
                ins.then_inc(m["r_chain"], 1)
                dve.wait_ge(m["r_chain"], chain[0])

            def bc(ap, n):
                return ap.rearrange("p (t a) -> p t a", a=1).broadcast_to([P, ap.shape[1], n])

            def bt(ap, n):
                return ap.rearrange("p (t a) -> p t a", t=1).broadcast_to([P, n, ap.shape[1]])

            V = nc.vector
            V.memset(eps[:], EPS).then_inc(m["r_ln"], 1)
            dve.wait_ge(m["r_vo"], 1)
            V.tensor_tensor(bout[:], all_ps[:, 0:D], bout[:], ALU.add).then_inc(m["r_bout"], 1)
            dve.wait_ge(m["r_bout"], 1)
            for g in range(TILES // LG):
                ts = slice(g * LG, (g + 1) * LG)
                for t in range(g * LG + BY_POOL, (g + 1) * LG):
                    V.tensor_tensor(x1[:, t, :], x1[:, t, :], bout[:], ALU.add).then_inc(m["r_bias_v"], 1)
                dve.wait_ge(m["r_bias_p"], BY_POOL * (g + 1))
                for i, t in enumerate(range(g * LG, (g + 1) * LG)):
                    if i == BY_POOL:
                        dve.wait_ge(m["r_bias_v"], (LG - BY_POOL) * (g + 1))
                    ins = V.bn_stats(stats[:, t, :], x1[:, t, :])
                link(ins)
                for t in range(g * LG, (g + 1) * LG):
                    ins = V.bn_aggr(mv[:, t, :], stats[:, t, :])
                ins.then_inc(m["r_var"], 1)
                dve.wait_ge(m["r_std"], g + 1)
                root, first, a, rs, shift = (r[i][:, ts] for i in range(5))
                link(V.reciprocal(first, root))
                link(V.tensor_tensor(a, first, first, ALU.mult))
                link(V.scalar_tensor_tensor(out=root, in0=mv[:, ts, 1], scalar=EPS, in1=a, op0=ALU.add, op1=ALU.mult))
                link(V.tensor_scalar(a, root, -0.5, 1.5, ALU.mult, ALU.add))
                link(V.tensor_tensor(rs, first, a, ALU.mult))
                V.scalar_tensor_tensor(out=shift, in0=mv[:, ts, 0], scalar=-1.0, in1=rs, op0=ALU.mult,
                                       op1=ALU.mult).then_inc(m["r_rs"], 1)
            dve.wait_ge(m["r_b1"], 1)
            V.tensor_copy(b1T[:].rearrange("p c e -> p (c e)"), b1_ps[:, 0:HK * E_])
            dve.wait_ge(m["r_lgt"], TILES // 4)
            lg = lg_ps[:].rearrange("p (t e) -> p t e", e=E_)
            V.memset(g32, 0.0)
            link(V.tensor_reduce(red[:, 0, :], lg, AX_X, ALU.max))
            V.tensor_tensor(tmp[:], lg, bc(red[:, 0, :], E_), ALU.subtract).then_inc(m["r_sub"], 1)
            dve.wait_ge(m["r_exp"], 1)
            link(V.tensor_reduce(red[:, 0, :], prob[:], AX_X, ALU.add))
            link(V.reciprocal(red[:, 1, :], red[:, 0, :]))
            link(V.tensor_tensor(prob[:], prob[:], bc(red[:, 1, :], E_), ALU.mult))
            for t in range(TILES):
                ins = V.max(top[:, t, :], prob[:, t, :])
            link(ins)
            for t in range(TILES):
                ins = V.max_index(topi[:, t, :], top[:, t, :], prob[:, t, :])
            link(ins)
            dve.wait_ge(m["r_const"], 12)
            link(V.tensor_copy(topf[:], topi[:, :, 0:TOPK].rearrange("p t k -> p k t")))
            for k in range(TOPK):
                ins = V.tensor_tensor(oh[:, k], bt(io16[:], TILES), bc(topf[:, k, :], E_), ALU.is_equal)
            link(ins)
            link(V.tensor_tensor(mask[:], oh[:, 0], oh[:, 1], ALU.add))
            link(V.tensor_tensor(mask[:], mask[:], oh[:, 2], ALU.add))
            V.tensor_copy(maskb[:], mask[:]).then_inc(m["r_mask"], 1)
            link(V.tensor_reduce(red[:, 0, :], top[:, :, 0:TOPK], AX_X, ALU.add))
            link(V.tensor_scalar(red[:, 0, :], red[:, 0, :], 1e-12, None, ALU.max))
            link(V.reciprocal(red[:, 1, :], red[:, 0, :]))
            V.tensor_tensor(wts[:], top[:, :, 0:TOPK], bc(red[:, 1, :], TOPK), ALU.mult)
            link(V.tensor_tensor(tmp[:], prob[:], mask[:], ALU.mult))
            V.tensor_tensor(g32[:, :, 0:E_], tmp[:], bc(red[:, 1, :], E_), ALU.mult).then_inc(m["r_g32"], 1)
            dve.wait_ge(m["r_pre"], 1)
            link(V.tensor_copy(tot[:], all_ps[:].rearrange("p (t e) -> p e t", e=E_)))
            flat = "p e t -> p (e t)"
            link(V.tensor_tensor_scan(inc[:].rearrange(flat), tot[:].rearrange(flat), zero[:], 0.0, ALU.add, ALU.add))
            link(V.tensor_reduce(cnt[:, 0, :], tot[:], AX_X, ALU.add))
            link(V.tensor_scalar(cnt[:, 1, :], cnt[:, 0, :], float(P - 1), None, ALU.add))
            link(V.tensor_copy(cnti[:, 0, :], cnt[:, 1, :]))
            link(V.tensor_scalar(cnti[:, 1, :], cnti[:, 0, :], 7, None, ALU.logical_shift_right))
            link(V.tensor_copy(cnt[:, 2, :], cnti[:, 1, :]))
            link(V.tensor_tensor_scan(cnt[:, 3, :], cnt[:, 2, :], zero[:, 0:E_], 0.0, ALU.add, ALU.add))
            link(V.tensor_tensor(cnt[:, 4, :], cnt[:, 3, :], cnt[:, 2, :], ALU.subtract))
            link(V.tensor_tensor(cnt[:, 5, :], inc[:, :, TILES - 1], cnt[:, 0, :], ALU.subtract))
            link(V.scalar_tensor_tensor(out=cnt[:, 5, :], in0=cnt[:, 4, :], scalar=float(P), in1=cnt[:, 5, :],
                                        op0=ALU.mult, op1=ALU.subtract))
            link(V.tensor_tensor(inc[:], inc[:], tot[:], ALU.subtract))
            link(V.tensor_tensor(inc[:], inc[:], bc(cnt[:, 5, :], TILES), ALU.add))
            link(V.tensor_tensor(slots[:], pre_ps[:].rearrange("p (t e) -> p t e", e=E_),
                                 inc[:].rearrange("p e t -> p t e"), ALU.add))
            for k in range(TOPK):
                link(V.tensor_tensor(tmp[:], slots[:], oh[:, k], ALU.mult))
                link(V.tensor_reduce(slotf[:, k, :], tmp[:], AX_X, ALU.add))
            link(V.tensor_copy(sloti[:, 0], slotf[:]))
            V.tensor_scalar(sloti[:, 1], sloti[:, 0], P - 1, None, ALU.bitwise_and)
            link(V.tensor_scalar(sloti[:, 2], sloti[:, 0], 7, None, ALU.logical_shift_right))
            V.tensor_copy(row_of[:], sloti[:, 1])
            V.tensor_copy(tile_of[:], sloti[:, 2]).then_inc(m["r_slots"], 1)
            dve.wait_ge(m["r_slots"], 1)
            for i in range(TOPK * TILES):
                t, k = i // TOPK, i % TOPK
                if i >= HOT:
                    dve.wait_ge(m["r_inv"], i - HOT + 1)
                V.tensor_scalar(row_hot[:, i % HOT, :], ioq[:], row_of[:, k, t:t + 1], None, ALU.is_equal)\
                    .then_inc(m["r_oh_a"], 1)
                V.tensor_scalar(tile_hot[:, i % HOT, :], ioq[:, 0:SLOT_TILES], tile_of[:, k, t:t + 1],
                                part[:, 0:1], ALU.is_equal, ALU.mult).then_inc(m["r_oh"], 1)
                if i % (TOPK * TILES // E_) == 0:
                    e = i // (TOPK * TILES // E_)
                    if e == 0:
                        ins = V.tensor_scalar(ef[:], iot[0:1, :], cnt[0:1, 3, 0:1], None, ALU.is_ge)
                    else:
                        dve.wait_ge(m["r_ef"], e)
                        ins = V.scalar_tensor_tensor(out=ef[:], in0=iot[0:1, :], scalar=cnt[0:1, 3, e:e + 1], in1=ef[:],
                                                     op0=ALU.is_ge, op1=ALU.add)
                    ins.then_inc(m["r_ef"], 1)
            dve.wait_ge(m["r_ef"], E_)
            link(V.tensor_scalar(ef[:], ef[:], float(E_ - 1), None, ALU.min))
            link(V.tensor_copy(etile[:], ef[:]))
            dve.wait_ge(m["r_inv"], TOPK * TILES)
            sums, place, more = inv_ps[:, 0:SLOT_TILES], back[:, 0, :], back[:, 1, :]
            row = inc[:].rearrange("p e t -> p (e t)")[:, 0:SLOT_TILES]
            V.tensor_scalar(row, sums, -1.0, 0.0, ALU.add, ALU.max)
            link(V.tensor_scalar(more, sums, 1.0, None, ALU.max))
            link(V.reciprocal(more, more))
            link(V.tensor_tensor(more, tr_ps[:, 0, 0:SLOT_TILES], more, ALU.mult))
            link(V.tensor_scalar(src_i[:], more, 0.25, None, ALU.add))
            link(V.tensor_copy(more, src_i[:]))
            link(V.tensor_scalar(place, more, -1.0, None, ALU.add))
            V.tensor_scalar(src_i[:], place, 0.0, None, ALU.max)
            link(V.scalar_tensor_tensor(out=back[:, 1, :], in0=place, scalar=-0.5, in1=unused[:], op0=ALU.is_lt,
                                        op1=ALU.mult))
            link(V.scalar_tensor_tensor(out=place, in0=place, scalar=float(P), in1=row, op0=ALU.mult, op1=ALU.add))
            V.tensor_tensor(dst_i[:], place, back[:, 1, :], ALU.add)
            link(V.tensor_scalar(src_i[:], src_i[:], PLACES.bit_length() - 1, None, ALU.logical_shift_right))
            link(V.tensor_copy(back[:, 1, :], src_i[:]))
            V.scalar_tensor_tensor(out=src_i[:], in0=back[:, 1, :], scalar=float(P), in1=row, op0=ALU.mult, op1=ALU.add)


def expert_phase(nc, A, dram, S):
    src_i, dst_i = S["src_i"], S["dst_i"]
    w1, w2, b1T, etile, ident = S["w1"], S["w2"], S["b1T"], S["etile"], S["ident"]
    with ExitStack() as ctx:
        def sb(name, shape, dt):
            return ctx.enter_context(nc.sbuf_tensor(name, shape, dt))

        def psum(name):
            return ctx.enter_context(nc.psum_tensor(name, [P, 2, 512], F32))

        xin = sb("xin", [P, XIN, D], F32)
        xT = sb("mxT", [P, 2, D], F32)
        w1_now = sb("w1_now", [P, 2, DK, HID], F32)
        hT = sb("hT", [P, 2, HID], F32)
        y = sb("y", [P, 2, D], F32)
        x_ps, h_ps, yo_ps = psum("x_ps"), psum("h_ps"), psum("yo_ps")
        names = "m_xtr m_xT m_w1 m_h m_hT m_y m_ytaken".split()
        m = {k: ctx.enter_context(nc.semaphore(k)) for k in names}
        xs_ld = [ctx.enter_context(nc.semaphore(f"xs_ld{s}")) for s in range(XIN)]
        ys_st = [ctx.enter_context(nc.semaphore(f"ys_st{s}")) for s in range(2)]
        block = ctx.enter_context(nc.Block())
        LOOPS = SLOT_TILES // XIN - 1

        def done(t):
            return t + 3

        def pairs(t):
            return t // 2

        @block.gpsimd
        def _(pool):
            def gather(t):
                pool.indirect_dma_start(
                    out=xin[:, t % XIN, :], out_offset=None, in_=dram["xn"],
                    in_offset=bass.IndirectOffsetOnAxis(ap=src_i[:, t:t + 1], axis=0)).then_inc(xs_ld[t % XIN], 16)

            for t in range(XIN):
                gather(t)
            for t in range(SLOT_TILES):
                if t + XIN < SLOT_TILES:
                    pool.wait_ge(m["m_xtr"], done(t))
                    gather(t + XIN)
                pool.wait_ge(m["m_ytaken"], done(t))
                pool.indirect_dma_start(
                    out=dram["ys"], out_offset=bass.IndirectOffsetOnAxis(ap=dst_i[:, t:t + 1], axis=0),
                    in_=y[:, t % 2, :], in_offset=None).then_inc(ys_st[t % 2], 16)
            for s in range(2):
                pool.wait_ge(ys_st[s], 16 * SLOT_TILES // 2)

        @block.tensor
        def _(pe):
            def expert(t):
                return pe.value_load(etile[0:1, bass.ds(t, 1)], min_val=0, max_val=E_ - 1)

            def turn_x(t, s):
                pe.wait_ge(xs_ld[s], 16 * (t // XIN + 1))
                pe.wait_ge(m["m_xT"], done(t - 2))
                for k in range(DK):
                    ins = nc.tensor.transpose(x_ps[:, s % 2, k * P:(k + 1) * P], xin[:, s, k * P:(k + 1) * P],
                                              ident[:])
                ins.then_inc(m["m_xtr"], 1)

            def first_layer(t, s):
                pe.wait_ge(m["m_xT"], done(t))
                pe.wait_ge(m["m_w1"], done(t))
                pe.wait_ge(m["m_hT"], done(t - 2))
                for c in range(HK):
                    for k in range(DK):
                        ins = nc.tensor.matmul(h_ps[:, s, c * P:(c + 1) * P], w1_now[:, s, k, c * P:(c + 1) * P],
                                               xT[:, s, k * P:(k + 1) * P], start=(k == 0), stop=(k == DK - 1),
                                               skip_group_check=True)
                ins.then_inc(m["m_h"], 1)

            def second_layer(t, s, e):
                pe.wait_ge(m["m_hT"], done(t))
                pe.wait_ge(m["m_ytaken"], done(t - 2))
                for c in range(HK):
                    ins = nc.tensor.matmul(yo_ps[:, s, 0:D], hT[:, s, c * P:(c + 1) * P],
                                           w2[:, bass.ds(e, 1), c, :].rearrange("p a d -> p (a d)"),
                                           start=(c == 0), stop=(c == HK - 1))
                ins.then_inc(m["m_y"], 1)

            for k in ("m_xtr", "m_h", "m_y"):
                pe.sem_inc(m[k], 2)

            def step(t, s, left=XIN):
                e = expert(t)
                if left > 1:
                    first_layer(t + 1, (s + 1) % 2)
                if left > 2:
                    turn_x(t + 2, (s + 2) % XIN)
                second_layer(t, s % 2, e)

            turn_x(0, 0)
            turn_x(1, 1)
            first_layer(0, 0)
            with nc.tensor.Fori(0, LOOPS) as it:
                for s in range(XIN):
                    step(it * XIN + s, s)
            for s in range(XIN):
                step(SLOT_TILES - XIN + s, s, XIN - s)

        @block.scalar
        def _(act):
            def take_x(t, s):
                act.wait_ge(m["m_xtr"], done(t))
                act.wait_ge(m["m_h"], done(t - 2))
                nc.scalar.activation(xT[:, s, :], x_ps[:, s, 0:D], ACT.Copy).then_inc(m["m_xT"], 1)

            def take_y(t, s):
                act.wait_ge(m["m_y"], done(t))
                if not (isinstance(t, int) and t < 2):
                    act.wait_ge(ys_st[s], 16 * pairs(t))
                nc.scalar.activation(y[:, s, :], yo_ps[:, s, 0:D], ACT.Copy).then_inc(m["m_ytaken"], 1)

            for k in ("m_xT", "m_ytaken"):
                act.sem_inc(m[k], 2)
            def step(t, s, left=XIN):
                if left > 2:
                    take_x(t + 2, s % 2)
                take_y(t, s % 2)

            take_x(0, 0)
            take_x(1, 1)
            for t in range(XIN):
                step(t, t)
            with nc.scalar.Fori(1, LOOPS) as it:
                for s in range(XIN):
                    step(it * XIN + s, s)
            for s in range(XIN):
                step(SLOT_TILES - XIN + s, s, XIN - s)

        @block.vector
        def _(dve):
            def fetch_w1(t, s):
                e = dve.value_load(etile[0:1, bass.ds(t, 1)], min_val=0, max_val=E_ - 1)
                dve.wait_ge(m["m_h"], done(t - 2))
                nc.vector.tensor_copy(w1_now[:, s].rearrange("p k h -> p (k h)"),
                                      w1[:, bass.ds(e, 1)].rearrange("p a k h -> p (a k h)")).then_inc(m["m_w1"], 1)

            def take_hT(t, s):
                e = dve.value_load(etile[0:1, bass.ds(t, 1)], min_val=0, max_val=E_ - 1)
                dve.wait_ge(m["m_h"], done(t))
                dve.wait_ge(m["m_y"], done(t - 2))
                for c in range(HK):
                    ins = nc.vector.tensor_scalar(hT[:, s, c * P:(c + 1) * P], h_ps[:, s, c * P:(c + 1) * P],
                                                  b1T[:, c, bass.ds(e, 1)], 0.0, ALU.add, ALU.max)
                ins.then_inc(m["m_hT"], 1)

            def step(t, s, left=XIN):
                if left > 2:
                    fetch_w1(t + 2, s % 2)
                if left > 1:
                    take_hT(t + 1, (s + 1) % 2)

            dve.sem_inc(m["m_hT"], 2)
            dve.sem_inc(m["m_w1"], 2)
            fetch_w1(0, 0)
            fetch_w1(1, 1)
            take_hT(0, 0)
            with nc.vector.Fori(0, LOOPS) as it:
                for s in range(XIN):
                    step(it * XIN + s, s)
            for s in range(XIN):
                step(SLOT_TILES - XIN + s, s, XIN - s)


def combine_phase(nc, A, dram, S, out):
    x1, wts = S["x1"], S["wts"]
    GROUPS = TILES // GRP
    AHEAD = 4
    SUMS_V = 2
    SUMS_P = GRP - SUMS_V
    with ExitStack() as ctx:
        def sb(name, shape, dt):
            return ctx.enter_context(nc.sbuf_tensor(name, shape, dt))

        got = sb("got", [P, AHEAD, GRP, TOPK * D], F32)
        stats = sb("stats2", [P, TILES, 6], F32)
        mv = sb("mv2", [P, TILES, 2], F32)
        r = sb("r2", [P, 5, TILES], F32)
        outb = sb("outb", [P, 2, GRP, D], F32)
        eps = sb("eps2", [P, 1], F32)
        names = "c_scaled c_pool c_dve c_chain c_eps c_var c_std c_rs c_out".split()
        m = {k: ctx.enter_context(nc.semaphore(k)) for k in names}
        ld = [ctx.enter_context(nc.semaphore(f"got_ld{s}")) for s in range(AHEAD)]
        st = [ctx.enter_context(nc.semaphore(f"st{s}")) for s in range(2)]
        block = ctx.enter_context(nc.Block())
        out_v = out.rearrange("b (g t p) d -> (b g) p t d", p=P, t=GRP)
        ys = dram["ys"][0:NTOK * PLACES, :].rearrange("(t k p) d -> t p k d", k=PLACES, p=P)

        @block.sync
        def _(sp):
            def load(g):
                for i in range(GRP):
                    sp.dma_start(got[:, g % AHEAD, i].rearrange("p (k d) -> p k d", k=TOPK),
                                 ys[g * GRP + i][:, 0:TOPK, :]).then_inc(ld[g % AHEAD], 16)

            for g in range(AHEAD):
                load(g)
            for g in range(GROUPS):
                if g + AHEAD < GROUPS:
                    sp.wait_ge(m["c_pool"], TOPK * SUMS_P * (g + 1))
                    sp.wait_ge(m["c_dve"], TOPK * SUMS_V * (g + 1))
                    load(g + AHEAD)
                sp.wait_ge(m["c_out"], GRP * (g + 1))
                sp.dma_start(out_v[g], outb[:, g % 2]).then_inc(st[g % 2], 16)
            for s in range(2):
                sp.wait_ge(st[s], 16 * GROUPS // 2)

        @block.gpsimd
        def _(pool):
            for g in range(GROUPS):
                pool.wait_ge(ld[g % AHEAD], 16 * GRP * (g // AHEAD + 1))
                pool.wait_ge(m["c_scaled"], TOPK * SUMS_P * (g + 1))
                for k in range(TOPK):
                    for n, i in enumerate(range(SUMS_V, GRP)):
                        t = g * GRP + i
                        if k:
                            pool.wait_ge(m["c_pool"], (g * TOPK + k - 1) * SUMS_P + n + 1)
                        nc.gpsimd.tensor_tensor(x1[:, t, :], got[:, g % AHEAD, i, k * D:(k + 1) * D], x1[:, t, :],
                                                ALU.add).then_inc(m["c_pool"], 1)

        @block.scalar
        def _(act):
            def scale_rows(g):
                act.wait_ge(ld[g % AHEAD], 16 * GRP * (g // AHEAD + 1))
                for k in range(TOPK):
                    for i in range(SUMS_V, GRP):
                        rows = got[:, g % AHEAD, i, k * D:(k + 1) * D]
                        t = g * GRP + i
                        nc.scalar.activation(rows, rows, ACT.Copy, scale=wts[:, t, k:k + 1])\
                            .then_inc(m["c_scaled"], 1)

            act.wait_ge(m["c_eps"], 1)
            scale_rows(0)
            for g in range(GROUPS):
                if g + 1 < GROUPS:
                    scale_rows(g + 1)
                ts = slice(g * GRP, (g + 1) * GRP)
                act.wait_ge(m["c_var"], g + 1)
                nc.scalar.activation(r[:, 0, ts], mv[:, ts, 1], ACT.Sqrt, bias=eps[:, 0:1]).then_inc(m["c_std"], 1)
                act.wait_ge(m["c_rs"], g + 1)
                if g >= 2:
                    act.wait_ge(st[g % 2], 16 * (g // 2))
                for i in range(GRP):
                    t = g * GRP + i
                    nc.scalar.activation(outb[:, g % 2, i, :], x1[:, t, :], ACT.Identity, bias=r[:, 4, t:t + 1],
                                         scale=r[:, 3, t:t + 1]).then_inc(m["c_out"], 1)

        @block.vector
        def _(dve):
            chain = [0]
            V = nc.vector

            def link(ins):
                chain[0] += 1
                ins.then_inc(m["c_chain"], 1)
                dve.wait_ge(m["c_chain"], chain[0])

            V.memset(eps[:], EPS).then_inc(m["c_eps"], 1)
            for g in range(GROUPS):
                dve.wait_ge(ld[g % AHEAD], 16 * GRP * (g // AHEAD + 1))
                for k in range(TOPK):
                    for i in range(SUMS_V):
                        t = g * GRP + i
                        if k:
                            dve.wait_ge(m["c_dve"], (g * TOPK + k - 1) * SUMS_V + i + 1)
                        V.scalar_tensor_tensor(out=x1[:, t, :], in0=got[:, g % AHEAD, i, k * D:(k + 1) * D],
                                               scalar=wts[:, t, k:k + 1], in1=x1[:, t, :],
                                               op0=ALU.mult, op1=ALU.add).then_inc(m["c_dve"], 1)
                for i in range(GRP):
                    t = g * GRP + i
                    if i == 0:
                        dve.wait_ge(m["c_dve"], TOPK * SUMS_V * (g + 1))
                    if i == SUMS_V:
                        dve.wait_ge(m["c_pool"], TOPK * SUMS_P * (g + 1))
                    ins = V.bn_stats(stats[:, t, :], x1[:, t, :])
                link(ins)
                for t in range(g * GRP, (g + 1) * GRP):
                    ins = V.bn_aggr(mv[:, t, :], stats[:, t, :])
                ins.then_inc(m["c_var"], 1)
                dve.wait_ge(m["c_std"], g + 1)
                ts = slice(g * GRP, (g + 1) * GRP)
                root, first, a, rs, shift = (r[:, i, ts] for i in range(5))
                link(V.reciprocal(first, root))
                link(V.tensor_tensor(a, first, first, ALU.mult))
                link(V.scalar_tensor_tensor(out=root, in0=mv[:, ts, 1], scalar=EPS, in1=a, op0=ALU.add, op1=ALU.mult))
                link(V.tensor_scalar(a, root, -0.5, 1.5, ALU.mult, ALU.add))
                link(V.tensor_tensor(rs, first, a, ALU.mult))
                V.scalar_tensor_tensor(out=shift, in0=mv[:, ts, 0], scalar=-1.0, in1=rs, op0=ALU.mult,
                                       op1=ALU.mult).then_inc(m["c_rs"], 1)


def post_ln_block(nc, A, dram, out):
    with ExitStack() as ctx:
        def sb(name, shape, dt):
            return ctx.enter_context(nc.sbuf_tensor(name, shape, dt))

        S = {"x1": sb("x1", [P, TILES, D], F32), "vo": sb("vo", [P, D], F32),
             "bout": sb("bout", [P, D], F32), "gate": sb("gate_sb", [P, DK, E_], F32),
             "small_in": ctx.enter_context(nc.semaphore("small_in"))}
        attention_phase(nc, A, dram, S)
        S.update(src_i=sb("src_i", [P, SLOT_TILES], I32), dst_i=sb("dst_i", [P, SLOT_TILES], I32),
                 wts=sb("wts", [P, TILES, TOPK], F32),
                 gT=sb("gT", [P, 2 * 512], F32), etile=sb("etile", [1, SLOT_TILES], I32),
                 b2r=sb("b2r", [P, D], F32), ident=sb("ident2", [P, P], F32))
        with ExitStack() as inner:
            S["w1"] = inner.enter_context(nc.sbuf_tensor("w1", [P, E_, DK, HID], F32))
            S["w2"] = inner.enter_context(nc.sbuf_tensor("w2", [P, E_, HK, D], F32))
            S["b1T"] = inner.enter_context(nc.sbuf_tensor("b1T", [P, HK, E_], F32))
            routing_phase(nc, A, dram, S)
            expert_phase(nc, A, dram, S)
        combine_phase(nc, A, dram, S, out)


def scratch(nc):
    shapes = {"xsplit": [B, P, 2 * DK * T], "wsplit": [PAIRS + PAIRS // 2, P, 2 * DK * 256], "xn": [NTOK, D],
              "ys": [PLACES * NTOK + SLOT_TILES * P, D]}
    return {k: nc.dram_tensor(f"scratch_{k}", v, F32, kind="Internal").ap() for k, v in shapes.items()}


_INS = {'L0_attn_x': 'x', 'L0_attn_W_in': 'W_in', 'L0_attn_b_in': 'b_in', 'L0_attn_W_out': 'W_out',
        'L0_attn_b_out': 'b_out', 'L0_ffn_gate': 'gate', 'L0_ffn_W1': 'W1', 'L0_ffn_b1': 'b1', 'L0_ffn_W2': 'W2',
        'L0_ffn_b2': 'b2'}


def rotary_tables():
    p = np.arange(HALF, dtype=np.float32) / np.float32(HALF - 1)
    thetas = np.float32(10000.0) ** p
    pos = np.arange(T, dtype=np.float32)[:, None] / thetas[None, :]
    scale = np.float32(1.0 / np.sqrt(HD))

    def rows(table):
        return np.ascontiguousarray(np.concatenate([table.T * scale] * 2 + [table.T] * 2, axis=0))

    return rows(np.cos(pos)), rows(np.sin(pos))


def kernel(**inputs):
    import concourse.bacc as _bacc
    from concourse.bass_utils import run_bass_kernel_spmd as _run

    nc = _bacc.Bacc("TRN2", target_bir_lowering=False, num_devices=1)
    arrays, args = {}, {}
    for name, short in _INS.items():
        a = np.ascontiguousarray(inputs[name])
        arrays[f"in_{name}_dram"] = a
        args[short] = nc.dram_tensor(f"in_{name}_dram", a.shape, mybir.dt.from_np(a.dtype), kind="ExternalInput").ap()
    for short, a in zip(("cos", "sin"), rotary_tables()):
        arrays[f"in_{short}_dram"] = a
        args[short] = nc.dram_tensor(f"in_{short}_dram", a.shape, F32, kind="ExternalInput").ap()
    out = nc.dram_tensor("out_0_dram", (B, T, D), F32, kind="ExternalOutput").ap()
    post_ln_block(nc, args, scratch(nc), out)
    r = _run(nc, [arrays], core_ids=[0])
    return r.results[0]["out_0_dram"]
```
